# Optimizing a Trainium2 kernel written in Bass

```python
import numpy as np
import jax
import jax.numpy as jnp

def _softmax(x, axis=-1):
    return jax.nn.softmax(x, axis=axis)

def _gelu(x):
    return jax.nn.gelu(x, approximate=True)

def _silu(x):
    return jax.nn.silu(x)

def _sigmoid(x):
    return jax.nn.sigmoid(x)

def _layernorm(x, axis=-1, eps=1e-05):
    m = jnp.mean(x, axis=axis, keepdims=True)
    v = jnp.var(x, axis=axis, keepdims=True)
    return (x - m) / jnp.sqrt(v + eps)

def _scatter_add(tgt, idx, src, axis=0):
    return tgt.at[idx].add(src)

def _segment_sum(src, seg, n):
    return jax.ops.segment_sum(src, seg, n)
kernel_name = 'mk_prb_d4_jaxref_r8_775e81'

def setup_inputs(seed: int=0):
    np.random.seed(seed)
    _w = jnp.asarray

    def _L0_attn_setup():
        import jax, jax.numpy as jnp
        import numpy as np
        from jax import lax
        D_MODEL, D_INNER, D_STATE, DT_RANK, D_CONV = (128, 256, 16, 64, 4)
        B, L = (2, 128)

        def _depthwise_conv_same(x, k, b):
            kw = k.shape[0]
            y = lax.conv_general_dilated(x, k, window_strides=(1,), padding=[((kw - 1) // 2, kw // 2)], dimension_numbers=('NWC', 'WIO', 'NWC'), feature_group_count=x.shape[-1])
            return y + b

        def _selective_scan(u, delta, A, Bm, Cm, Dv):
            deltaA = jnp.exp(jnp.einsum('bld,dn->bldn', delta, A))
            deltaB_u = (delta * u)[..., None] * Bm[:, :, None, :]
            dA = jnp.transpose(deltaA, (1, 0, 2, 3))
            dBu = jnp.transpose(deltaB_u, (1, 0, 2, 3))
            Ct = jnp.transpose(Cm, (1, 0, 2))
            h0 = jnp.zeros((u.shape[0], u.shape[2], A.shape[1]), u.dtype)

            def step(h, t):
                dA_t, dBu_t, C_t = t
                h = dA_t * h + dBu_t
                return (h, jnp.einsum('bdn,bn->bd', h, C_t))
            _, ys = lax.scan(step, h0, (dA, dBu, Ct))
            y = jnp.transpose(ys, (1, 0, 2))
            return y + u * Dv
        key = jax.random.key(seed)
        ks = jax.random.split(key, 8)
        f32 = jnp.float32
        return {'inputs': jax.random.normal(ks[0], (B, L, D_MODEL), f32), 'W_in': jax.random.normal(ks[1], (D_MODEL, 2 * D_INNER), f32) / np.sqrt(D_MODEL), 'K_conv': jax.random.normal(ks[2], (D_CONV, 1, D_INNER), f32) / np.sqrt(D_CONV), 'b_conv': jnp.zeros((D_INNER,), f32), 'W_x': jax.random.normal(ks[3], (D_MODEL, DT_RANK + 2 * D_STATE), f32) / np.sqrt(D_MODEL), 'W_dt': jax.random.normal(ks[4], (DT_RANK, D_INNER), f32) / np.sqrt(DT_RANK), 'b_dt': jnp.zeros((D_INNER,), f32), 'A_log': 0.02 * jax.random.normal(ks[5], (D_INNER, D_STATE), f32), 'D': jnp.ones((D_INNER,), f32), 'W_out': jax.random.normal(ks[6], (D_INNER, D_MODEL), f32) / np.sqrt(D_INNER), 'b_out': jnp.zeros((D_MODEL,), f32)}
    _L0_attn_in = _L0_attn_setup()

    def _L0_ffn_setup():
        import math
        import jax, jax.numpy as jnp
        import numpy as np
        B, S, H = (4, 512, 128)
        FFN = 512
        E = 16
        N_ZERO, N_COPY, N_CONST = (1, 1, 2)
        MLP_START = N_ZERO + N_COPY + N_CONST
        E_MLP = E - MLP_START
        TOP_K = 2
        CAP_FACTOR = 1.0
        EPS = 1e-05

        def _rmsnorm(x, w, eps):
            return x * jax.lax.rsqrt(jnp.mean(x * x, axis=-1, keepdims=True) + eps) * w
        key = jax.random.key(seed)
        ks = jax.random.split(key, 6)
        std = jnp.float32(0.02)
        return {'x': jax.random.normal(ks[0], (B, S, H), jnp.float32), 'norm_weight': jnp.ones((H,), jnp.float32), 'router_weight': jax.random.normal(ks[1], (E, H), jnp.float32) * std, 'router_bias': jnp.zeros((E,), jnp.float32), 'fc1_weight': jax.random.normal(ks[2], (E_MLP, FFN, H), jnp.float32) * std, 'fc1_bias': jnp.zeros((E_MLP, FFN), jnp.float32), 'fc2_weight': jax.random.normal(ks[3], (E_MLP, H, FFN), jnp.float32) * std, 'fc2_bias': jnp.zeros((E_MLP, H), jnp.float32), 'constant_vectors': jax.random.normal(ks[4], (N_CONST, H), jnp.float32) * std}
    _L0_ffn_in = _L0_ffn_setup()

    def _L1_attn_setup():
        import jax, jax.numpy as jnp
        import numpy as np
        import math
        B, T, D = (2, 512, 128)
        H = 16
        HEAD_DIM = D // H
        CHUNK = 64

        def chunked_attention(q, k, v, chunk_size, scale):
            Bq, Hq, Tq, hd = q.shape
            S = k.shape[2]
            nc = Tq // chunk_size
            q_chunks = q.reshape(Bq, Hq, nc, chunk_size, hd).transpose(2, 0, 1, 3, 4)
            starts = jnp.arange(nc, dtype=jnp.int32) * chunk_size
            k_pos = jnp.arange(S)

            def body(carry, xs):
                qc, start = xs
                scores = jnp.einsum('bhqd,bhkd->bhqk', qc, k) * scale
                q_pos = start + jnp.arange(chunk_size)
                causal_mask = k_pos[None, :] > q_pos[:, None]
                scores = jnp.where(causal_mask[None, None], -jnp.inf, scores)
                m = jnp.max(scores, axis=-1, keepdims=True)
                m = jnp.where(jnp.isinf(m), jnp.zeros_like(m), m)
                p = jax.nn.softmax(scores - m, axis=-1)
                oc = jnp.einsum('bhqk,bhkd->bhqd', p, v)
                return (carry, oc)
            _, outs = jax.lax.scan(body, None, (q_chunks, starts))
            return outs.transpose(1, 2, 0, 3, 4).reshape(Bq, Hq, Tq, hd)
        key = jax.random.key(seed)
        ks = jax.random.split(key, 9)
        s = 1.0 / math.sqrt(D)
        return {'x': jax.random.normal(ks[0], (B, T, D), dtype=jnp.float32), 'Wq': jax.random.normal(ks[1], (D, D), dtype=jnp.float32) * s, 'bq': jax.random.normal(ks[2], (D,), dtype=jnp.float32) * 0.01, 'Wk': jax.random.normal(ks[3], (D, D), dtype=jnp.float32) * s, 'bk': jax.random.normal(ks[4], (D,), dtype=jnp.float32) * 0.01, 'Wv': jax.random.normal(ks[5], (D, D), dtype=jnp.float32) * s, 'bv': jax.random.normal(ks[6], (D,), dtype=jnp.float32) * 0.01, 'Wo': jax.random.normal(ks[7], (D, D), dtype=jnp.float32) * s, 'bo': jax.random.normal(ks[8], (D,), dtype=jnp.float32) * 0.01}
    _L1_attn_in = _L1_attn_setup()

    def _L1_ffn_setup():
        import jax, jax.numpy as jnp
        import numpy as np
        TOP_K = 2
        ROUTE_SCALE = 1.0
        EPS = 1e-20
        key = jax.random.key(seed)
        ks = jax.random.split(key, 8)
        dim, hid, E, X = (128, 352, 8, 1)
        std = 0.02
        x = jax.random.normal(ks[0], (2, 256, dim), dtype=jnp.float32)
        w1 = jax.random.normal(ks[1], (E, hid, dim), dtype=jnp.float32) * std
        w2 = jax.random.normal(ks[2], (E, dim, hid), dtype=jnp.float32) * std
        w3 = jax.random.normal(ks[3], (E, hid, dim), dtype=jnp.float32) * std
        new_w1 = jax.random.normal(ks[4], (X, hid, dim), dtype=jnp.float32) * std
        new_w2 = jnp.zeros((X, dim, hid), dtype=jnp.float32)
        new_w3 = jax.random.normal(ks[5], (X, hid, dim), dtype=jnp.float32) * std
        gate_weight = jax.random.normal(ks[6], (E, dim), dtype=jnp.float32) * std
        new_gate_weight = jax.random.normal(ks[7], (X, dim), dtype=jnp.float32) * std
        gate_bias = jnp.zeros((X,), dtype=jnp.float32)
        return dict(x=x, w1=w1, w2=w2, w3=w3, new_w1=new_w1, new_w2=new_w2, new_w3=new_w3, gate_weight=gate_weight, new_gate_weight=new_gate_weight, gate_bias=gate_bias)
    _L1_ffn_in = _L1_ffn_setup()

    def _L2_attn_setup():
        import jax, jax.numpy as jnp
        import numpy as np
        B, N, C = (2, 256, 128)
        H = 16
        HD = C // H
        R = 16
        LORA_SCALE = 32.0 / R
        ATTN_SCALE = HD ** (-0.5)
        key = jax.random.key(seed)
        ks = jax.random.split(key, 10)
        s = lambda fan_in: 1.0 / np.sqrt(fan_in)
        return {'x': jax.random.normal(ks[0], (B, N, C), dtype=jnp.float32), 'w_qkv': jax.random.normal(ks[1], (C, 3 * C), dtype=jnp.float32) * s(C), 'b_qkv': jax.random.normal(ks[2], (3 * C,), dtype=jnp.float32) * 0.02, 'a_q': jax.random.normal(ks[3], (HD, R), dtype=jnp.float32) * s(HD), 'b_q': jax.random.normal(ks[4], (R, HD), dtype=jnp.float32) * 0.02, 'a_v': jax.random.normal(ks[5], (HD, R), dtype=jnp.float32) * s(HD), 'b_v': jax.random.normal(ks[6], (R, HD), dtype=jnp.float32) * 0.02, 'w_proj': jax.random.normal(ks[7], (C, C), dtype=jnp.float32) * s(C), 'b_proj': jax.random.normal(ks[8], (C,), dtype=jnp.float32) * 0.02}
    _L2_attn_in = _L2_attn_setup()

    def _L2_ffn_setup():
        import jax, jax.numpy as jnp
        import numpy as np
        MICRO_BATCHES = 2
        TOP_K = 2
        LN_EPS = 1e-05
        B, S, D = (4, 512, 128)
        E = 8
        DFF = 4 * D

        def _layernorm(x, g, b):
            mu = jnp.mean(x, axis=-1, keepdims=True)
            var = jnp.mean(jnp.square(x - mu), axis=-1, keepdims=True)
            return (x - mu) * jax.lax.rsqrt(var + LN_EPS) * g + b
        key = jax.random.key(seed)
        ks = jax.random.split(key, 12)
        sd = 1.0 / np.sqrt(D)
        sf = 1.0 / np.sqrt(DFF)
        return {'x': jax.random.normal(ks[0], (B, S, D), dtype=jnp.float32), 'ln_g': jnp.ones((D,), jnp.float32), 'ln_b': jnp.zeros((D,), jnp.float32), 'attn_w': jax.random.normal(ks[1], (D, D), jnp.float32) * sd, 'attn_b': jnp.zeros((D,), jnp.float32), 'gate_w': jax.random.normal(ks[2], (D, E), jnp.float32) * sd, 'w1': jax.random.normal(ks[3], (E, D, DFF), jnp.float32) * sd, 'b1': jnp.zeros((E, DFF), jnp.float32), 'w2': jax.random.normal(ks[4], (E, DFF, D), jnp.float32) * sf, 'b2': jnp.zeros((E, D), jnp.float32), 'next_w': jax.random.normal(ks[5], (D, D), jnp.float32) * sd, 'next_b': jnp.zeros((D,), jnp.float32)}
    _L2_ffn_in = _L2_ffn_setup()

    def _L3_attn_setup():
        import jax, jax.numpy as jnp
        import numpy as np
        D = 128
        E = 2 * D
        S = 128
        LN_EPS = 1e-05
        key = jax.random.key(seed)
        ks = jax.random.split(key, 4)
        bs, seq_len = (4, 256)
        x = jax.random.normal(ks[0], (bs, seq_len, D), dtype=jnp.float32)
        W_in = jax.random.normal(ks[1], (D, 2 * E + S), dtype=jnp.float32) / np.sqrt(D)
        b_in = jnp.zeros((2 * E + S,), dtype=jnp.float32)
        W_out = jax.random.normal(ks[2], (E, D), dtype=jnp.float32) / np.sqrt(E)
        b_out = jnp.zeros((D,), dtype=jnp.float32)
        ln_g = jnp.ones((D,), dtype=jnp.float32)
        ln_b = jnp.zeros((D,), dtype=jnp.float32)
        gamma_q = jnp.ones((S,), dtype=jnp.float32)
        beta_q = jnp.zeros((S,), dtype=jnp.float32)
        gamma_k = jnp.ones((S,), dtype=jnp.float32)
        beta_k = jnp.zeros((S,), dtype=jnp.float32)
        return {'x': x, 'ln_g': ln_g, 'ln_b': ln_b, 'W_in': W_in, 'b_in': b_in, 'W_out': W_out, 'b_out': b_out, 'gamma_q': gamma_q, 'beta_q': beta_q, 'gamma_k': gamma_k, 'beta_k': beta_k}
    _L3_attn_in = _L3_attn_setup()

    def _L3_ffn_setup():
        import jax, jax.numpy as jnp
        import numpy as np
        B, S, M, E, DFF = (4, 256, 128, 8, 512)
        CAPACITY_FACTOR = 1.25

        def _top1_gate(tokens, wg, capacity):
            gates = jax.nn.softmax(tokens @ wg)
            expert_idx = jnp.argmax(gates, axis=-1)
            mask1 = jax.nn.one_hot(expert_idx, gates.shape[-1], dtype=gates.dtype)
            pos = jnp.sum(jnp.cumsum(mask1, axis=0) * mask1, axis=-1).astype(jnp.int32) - 1
            keep = (pos < capacity).astype(gates.dtype)
            mask1c = mask1 * keep[:, None]
            gates1 = jnp.sum(gates * mask1c, axis=-1)
            loc_oh = jax.nn.one_hot(pos, capacity, dtype=gates.dtype)
            combine = gates1[:, None, None] * mask1c[:, :, None] * loc_oh[:, None, :]
            dispatch = (combine > 0).astype(tokens.dtype)
            return (combine, dispatch)
        key = jax.random.key(seed)
        k = jax.random.split(key, 5)
        x = jax.random.normal(k[0], (B, S, M), dtype=jnp.float32)
        wg = jax.random.normal(k[1], (M, E), dtype=jnp.float32) * 0.02
        w1 = jax.random.normal(k[2], (E, M, DFF), dtype=jnp.float32) * 0.02
        b1 = jnp.zeros((E, DFF), dtype=jnp.float32)
        w2 = jax.random.normal(k[3], (E, DFF, M), dtype=jnp.float32) * 0.02
        b2 = jnp.zeros((E, M), dtype=jnp.float32)
        return {'x': x, 'wg': wg, 'w1': w1, 'b1': b1, 'w2': w2, 'b2': b2}
    _L3_ffn_in = _L3_ffn_setup()
    _d = {'L0_attn_inputs': _L0_attn_in['inputs'], 'L0_attn_W_in': _L0_attn_in['W_in'], 'L0_attn_K_conv': _L0_attn_in['K_conv'], 'L0_attn_b_conv': _L0_attn_in['b_conv'], 'L0_attn_W_x': _L0_attn_in['W_x'], 'L0_attn_W_dt': _L0_attn_in['W_dt'], 'L0_attn_b_dt': _L0_attn_in['b_dt'], 'L0_attn_A_log': _L0_attn_in['A_log'], 'L0_attn_D': _L0_attn_in['D'], 'L0_attn_W_out': _L0_attn_in['W_out'], 'L0_attn_b_out': _L0_attn_in['b_out'], 'L0_ffn_norm_weight': _L0_ffn_in['norm_weight'], 'L0_ffn_router_weight': _L0_ffn_in['router_weight'], 'L0_ffn_router_bias': _L0_ffn_in['router_bias'], 'L0_ffn_fc1_weight': _L0_ffn_in['fc1_weight'], 'L0_ffn_fc1_bias': _L0_ffn_in['fc1_bias'], 'L0_ffn_fc2_weight': _L0_ffn_in['fc2_weight'], 'L0_ffn_fc2_bias': _L0_ffn_in['fc2_bias'], 'L0_ffn_constant_vectors': _L0_ffn_in['constant_vectors'], 'L1_attn_Wq': _L1_attn_in['Wq'], 'L1_attn_bq': _L1_attn_in['bq'], 'L1_attn_Wk': _L1_attn_in['Wk'], 'L1_attn_bk': _L1_attn_in['bk'], 'L1_attn_Wv': _L1_attn_in['Wv'], 'L1_attn_bv': _L1_attn_in['bv'], 'L1_attn_Wo': _L1_attn_in['Wo'], 'L1_attn_bo': _L1_attn_in['bo'], 'L1_ffn_w1': _L1_ffn_in['w1'], 'L1_ffn_w2': _L1_ffn_in['w2'], 'L1_ffn_w3': _L1_ffn_in['w3'], 'L1_ffn_new_w1': _L1_ffn_in['new_w1'], 'L1_ffn_new_w2': _L1_ffn_in['new_w2'], 'L1_ffn_new_w3': _L1_ffn_in['new_w3'], 'L1_ffn_gate_weight': _L1_ffn_in['gate_weight'], 'L1_ffn_new_gate_weight': _L1_ffn_in['new_gate_weight'], 'L1_ffn_gate_bias': _L1_ffn_in['gate_bias'], 'L2_attn_w_qkv': _L2_attn_in['w_qkv'], 'L2_attn_b_qkv': _L2_attn_in['b_qkv'], 'L2_attn_a_q': _L2_attn_in['a_q'], 'L2_attn_b_q': _L2_attn_in['b_q'], 'L2_attn_a_v': _L2_attn_in['a_v'], 'L2_attn_b_v': _L2_attn_in['b_v'], 'L2_attn_w_proj': _L2_attn_in['w_proj'], 'L2_attn_b_proj': _L2_attn_in['b_proj'], 'L2_ffn_ln_g': _L2_ffn_in['ln_g'], 'L2_ffn_ln_b': _L2_ffn_in['ln_b'], 'L2_ffn_attn_w': _L2_ffn_in['attn_w'], 'L2_ffn_attn_b': _L2_ffn_in['attn_b'], 'L2_ffn_gate_w': _L2_ffn_in['gate_w'], 'L2_ffn_w1': _L2_ffn_in['w1'], 'L2_ffn_b1': _L2_ffn_in['b1'], 'L2_ffn_w2': _L2_ffn_in['w2'], 'L2_ffn_b2': _L2_ffn_in['b2'], 'L2_ffn_next_w': _L2_ffn_in['next_w'], 'L2_ffn_next_b': _L2_ffn_in['next_b'], 'L3_attn_ln_g': _L3_attn_in['ln_g'], 'L3_attn_ln_b': _L3_attn_in['ln_b'], 'L3_attn_W_in': _L3_attn_in['W_in'], 'L3_attn_b_in': _L3_attn_in['b_in'], 'L3_attn_W_out': _L3_attn_in['W_out'], 'L3_attn_b_out': _L3_attn_in['b_out'], 'L3_attn_gamma_q': _L3_attn_in['gamma_q'], 'L3_attn_beta_q': _L3_attn_in['beta_q'], 'L3_attn_gamma_k': _L3_attn_in['gamma_k'], 'L3_attn_beta_k': _L3_attn_in['beta_k'], 'L3_ffn_wg': _L3_ffn_in['wg'], 'L3_ffn_w1': _L3_ffn_in['w1'], 'L3_ffn_b1': _L3_ffn_in['b1'], 'L3_ffn_w2': _L3_ffn_in['w2'], 'L3_ffn_b2': _L3_ffn_in['b2']}
    _x0 = _d['L0_attn_inputs']
    _d['L0_attn_inputs'] = jax.random.normal(jax.random.fold_in(jax.random.key(seed), 1), (16, 256, 128), dtype=_x0.dtype)
    del _x0
    return _d

def reference(L0_attn_inputs, L0_attn_W_in, L0_attn_K_conv, L0_attn_b_conv, L0_attn_W_x, L0_attn_W_dt, L0_attn_b_dt, L0_attn_A_log, L0_attn_D, L0_attn_W_out, L0_attn_b_out, L0_ffn_norm_weight, L0_ffn_router_weight, L0_ffn_router_bias, L0_ffn_fc1_weight, L0_ffn_fc1_bias, L0_ffn_fc2_weight, L0_ffn_fc2_bias, L0_ffn_constant_vectors, L1_attn_Wq, L1_attn_bq, L1_attn_Wk, L1_attn_bk, L1_attn_Wv, L1_attn_bv, L1_attn_Wo, L1_attn_bo, L1_ffn_w1, L1_ffn_w2, L1_ffn_w3, L1_ffn_new_w1, L1_ffn_new_w2, L1_ffn_new_w3, L1_ffn_gate_weight, L1_ffn_new_gate_weight, L1_ffn_gate_bias, L2_attn_w_qkv, L2_attn_b_qkv, L2_attn_a_q, L2_attn_b_q, L2_attn_a_v, L2_attn_b_v, L2_attn_w_proj, L2_attn_b_proj, L2_ffn_ln_g, L2_ffn_ln_b, L2_ffn_attn_w, L2_ffn_attn_b, L2_ffn_gate_w, L2_ffn_w1, L2_ffn_b1, L2_ffn_w2, L2_ffn_b2, L2_ffn_next_w, L2_ffn_next_b, L3_attn_ln_g, L3_attn_ln_b, L3_attn_W_in, L3_attn_b_in, L3_attn_W_out, L3_attn_b_out, L3_attn_gamma_q, L3_attn_beta_q, L3_attn_gamma_k, L3_attn_beta_k, L3_ffn_wg, L3_ffn_w1, L3_ffn_b1, L3_ffn_w2, L3_ffn_b2):

    def _L0_attn_ref(inputs, W_in, K_conv, b_conv, W_x, W_dt, b_dt, A_log, D, W_out, b_out):
        import jax, jax.numpy as jnp
        import numpy as np
        from jax import lax
        D_MODEL, D_INNER, D_STATE, DT_RANK, D_CONV = (128, 256, 16, 64, 4)
        B, L = (2, 128)

        def _depthwise_conv_same(x, k, b):
            kw = k.shape[0]
            y = lax.conv_general_dilated(x, k, window_strides=(1,), padding=[((kw - 1) // 2, kw // 2)], dimension_numbers=('NWC', 'WIO', 'NWC'), feature_group_count=x.shape[-1])
            return y + b

        def _selective_scan(u, delta, A, Bm, Cm, Dv):
            deltaA = jnp.exp(jnp.einsum('bld,dn->bldn', delta, A))
            deltaB_u = (delta * u)[..., None] * Bm[:, :, None, :]
            dA = jnp.transpose(deltaA, (1, 0, 2, 3))
            dBu = jnp.transpose(deltaB_u, (1, 0, 2, 3))
            Ct = jnp.transpose(Cm, (1, 0, 2))
            h0 = jnp.zeros((u.shape[0], u.shape[2], A.shape[1]), u.dtype)

            def step(h, t):
                dA_t, dBu_t, C_t = t
                h = dA_t * h + dBu_t
                return (h, jnp.einsum('bdn,bn->bd', h, C_t))
            _, ys = lax.scan(step, h0, (dA, dBu, Ct))
            y = jnp.transpose(ys, (1, 0, 2))
            return y + u * Dv
        x_and_res = inputs @ W_in
        x, res = jnp.split(x_and_res, 2, axis=-1)
        x = jax.nn.silu(_depthwise_conv_same(x, K_conv, b_conv))
        A = -jnp.exp(A_log)
        x_dbl = inputs @ W_x
        delta, Bm, Cm = jnp.split(x_dbl, [DT_RANK, DT_RANK + D_STATE], axis=-1)
        delta = jax.nn.softplus(delta @ W_dt + b_dt)
        y = _selective_scan(x, delta, A, Bm, Cm, D)
        y = y * jax.nn.silu(res)
        return y @ W_out + b_out

    def _L0_ffn_ref(x, norm_weight, router_weight, router_bias, fc1_weight, fc1_bias, fc2_weight, fc2_bias, constant_vectors):
        import math
        import jax, jax.numpy as jnp
        import numpy as np
        B, S, H = (4, 512, 128)
        FFN = 512
        E = 16
        N_ZERO, N_COPY, N_CONST = (1, 1, 2)
        MLP_START = N_ZERO + N_COPY + N_CONST
        E_MLP = E - MLP_START
        TOP_K = 2
        CAP_FACTOR = 1.0
        EPS = 1e-05

        def _rmsnorm(x, w, eps):
            return x * jax.lax.rsqrt(jnp.mean(x * x, axis=-1, keepdims=True) + eps) * w
        Bsz, Sl, Hd = x.shape
        N = Bsz * Sl
        CAP = int(math.ceil(CAP_FACTOR * N * TOP_K / E))
        x_flat = x.reshape(N, Hd)
        xn = _rmsnorm(x_flat, norm_weight, EPS)
        logits = xn @ router_weight.T + router_bias
        probs = jax.nn.softmax(logits, axis=-1)
        gate_vals, expert_idx = jax.lax.top_k(probs, TOP_K)
        e_flat = expert_idx.reshape(-1)
        g_flat = gate_vals.reshape(-1)
        oh = jax.nn.one_hot(e_flat, E, dtype=jnp.int32)
        pos = jnp.sum(jnp.cumsum(oh, axis=0) * oh, axis=-1) - 1
        keep = pos < CAP
        slot = jnp.clip(pos, 0, CAP - 1)
        tok = jnp.repeat(jnp.arange(N), TOP_K)
        contrib = xn[tok] * keep[:, None].astype(x.dtype)
        dispatch = jnp.zeros((E, CAP, Hd), x.dtype).at[e_flat, slot].add(contrib)
        out_zero = jnp.zeros((N_ZERO, CAP, Hd), x.dtype)
        out_copy = dispatch[N_ZERO:N_ZERO + N_COPY]
        out_const = jnp.broadcast_to(constant_vectors[:, None, :], (N_CONST, CAP, Hd))
        dm = dispatch[MLP_START:]
        h = jnp.einsum('ech,efh->ecf', dm, fc1_weight) + fc1_bias[:, None, :]
        h = jax.nn.gelu(h, approximate=False)
        out_mlp = jnp.einsum('ecf,ehf->ech', h, fc2_weight) + fc2_bias[:, None, :]
        expert_out = jnp.concatenate([out_zero, out_copy, out_const, out_mlp], axis=0)
        gathered = expert_out[e_flat, slot]
        w = g_flat * keep.astype(g_flat.dtype)
        combined = (gathered * w[:, None]).reshape(N, TOP_K, Hd).sum(axis=1)
        gate_sums = w.reshape(N, TOP_K).sum(axis=1, keepdims=True)
        out = combined / jnp.where(gate_sums > 0, gate_sums, 1.0)
        return out.reshape(Bsz, Sl, Hd)

    def _L1_attn_ref(x, Wq, bq, Wk, bk, Wv, bv, Wo, bo):
        import jax, jax.numpy as jnp
        import numpy as np
        import math
        B, T, D = (2, 512, 128)
        H = 16
        HEAD_DIM = D // H
        CHUNK = 64

        def chunked_attention(q, k, v, chunk_size, scale):
            Bq, Hq, Tq, hd = q.shape
            S = k.shape[2]
            nc = Tq // chunk_size
            q_chunks = q.reshape(Bq, Hq, nc, chunk_size, hd).transpose(2, 0, 1, 3, 4)
            starts = jnp.arange(nc, dtype=jnp.int32) * chunk_size
            k_pos = jnp.arange(S)

            def body(carry, xs):
                qc, start = xs
                scores = jnp.einsum('bhqd,bhkd->bhqk', qc, k) * scale
                q_pos = start + jnp.arange(chunk_size)
                causal_mask = k_pos[None, :] > q_pos[:, None]
                scores = jnp.where(causal_mask[None, None], -jnp.inf, scores)
                m = jnp.max(scores, axis=-1, keepdims=True)
                m = jnp.where(jnp.isinf(m), jnp.zeros_like(m), m)
                p = jax.nn.softmax(scores - m, axis=-1)
                oc = jnp.einsum('bhqk,bhkd->bhqd', p, v)
                return (carry, oc)
            _, outs = jax.lax.scan(body, None, (q_chunks, starts))
            return outs.transpose(1, 2, 0, 3, 4).reshape(Bq, Hq, Tq, hd)
        Bx, Tx, Dx = x.shape
        scale = 1.0 / math.sqrt(HEAD_DIM)

        def proj(W, b):
            y = x @ W.T + b
            return y.reshape(Bx, Tx, H, HEAD_DIM).transpose(0, 2, 1, 3)
        q = proj(Wq, bq)
        k = proj(Wk, bk)
        v = proj(Wv, bv)
        out = chunked_attention(q, k, v, CHUNK, scale)
        out = out.transpose(0, 2, 1, 3).reshape(Bx, Tx, Dx)
        return out @ Wo.T + bo

    def _L1_ffn_ref(x, w1, w2, w3, new_w1, new_w2, new_w3, gate_weight, new_gate_weight, gate_bias):
        import jax, jax.numpy as jnp
        import numpy as np
        TOP_K = 2
        ROUTE_SCALE = 1.0
        EPS = 1e-20
        bs, slen, dim = x.shape
        x_flat = x.reshape(-1, dim)
        ew1 = jnp.concatenate([w1, new_w1], axis=0)
        ew2 = jnp.concatenate([w2, new_w2], axis=0)
        ew3 = jnp.concatenate([w3, new_w3], axis=0)
        gate = jnp.concatenate([gate_weight, new_gate_weight], axis=0)
        e_orig = w1.shape[0]
        e_tot = gate.shape[0]
        bias = jnp.concatenate([jnp.zeros((e_orig,), x.dtype), gate_bias])
        scores = jax.nn.sigmoid((x_flat @ gate.T + bias).astype(jnp.float32))
        top_scores, selected = jax.lax.top_k(scores, TOP_K)
        top_scores = top_scores / (jnp.sum(top_scores, axis=-1, keepdims=True) + EPS)
        top_scores = top_scores * ROUTE_SCALE
        onehot = jax.nn.one_hot(selected, e_tot, dtype=jnp.float32)
        cw = jnp.einsum('tk,tke->te', top_scores, onehot)
        out = jnp.zeros_like(x_flat)
        for e in range(e_tot):
            h = jax.nn.silu(x_flat @ ew1[e].T) * (x_flat @ ew3[e].T)
            out = out + cw[:, e:e + 1] * (h @ ew2[e].T)
        return out.reshape(bs, slen, dim)

    def _L2_attn_ref(x, w_qkv, b_qkv, a_q, b_q, a_v, b_v, w_proj, b_proj):
        import jax, jax.numpy as jnp
        import numpy as np
        B, N, C = (2, 256, 128)
        H = 16
        HD = C // H
        R = 16
        LORA_SCALE = 32.0 / R
        ATTN_SCALE = HD ** (-0.5)
        Bb, Nn, Cc = x.shape
        qkv = (x @ w_qkv + b_qkv).reshape(Bb, Nn, 3, H, HD).transpose(2, 0, 3, 1, 4)
        q, k, v = (qkv[0], qkv[1], qkv[2])
        q = q + jnp.einsum('bhnr,rd->bhnd', jnp.einsum('bhnd,dr->bhnr', q, a_q), b_q) * LORA_SCALE
        v = v + jnp.einsum('bhnr,rd->bhnd', jnp.einsum('bhnd,dr->bhnr', v, a_v), b_v) * LORA_SCALE
        attn = jax.nn.softmax(jnp.einsum('bhnd,bhmd->bhnm', q, k) * ATTN_SCALE, axis=-1)
        out = jnp.einsum('bhnm,bhmd->bhnd', attn, v)
        out = out.transpose(0, 2, 1, 3).reshape(Bb, Nn, Cc)
        return out @ w_proj + b_proj

    def _L2_ffn_ref(x, ln_g, ln_b, attn_w, attn_b, gate_w, w1, b1, w2, b2, next_w, next_b):
        import jax, jax.numpy as jnp
        import numpy as np
        MICRO_BATCHES = 2
        TOP_K = 2
        LN_EPS = 1e-05
        B, S, D = (4, 512, 128)
        E = 8
        DFF = 4 * D

        def _layernorm(x, g, b):
            mu = jnp.mean(x, axis=-1, keepdims=True)
            var = jnp.mean(jnp.square(x - mu), axis=-1, keepdims=True)
            return (x - mu) * jax.lax.rsqrt(var + LN_EPS) * g + b
        Bx, Sx, Dx = x.shape
        N = Bx * Sx
        x_flat = x.reshape(N, Dx)
        x_attn = _layernorm(x_flat, ln_g, ln_b) @ attn_w + attn_b + x_flat
        logits = x_attn @ gate_w
        _ = jax.lax.top_k(logits, TOP_K)
        tpe = N // (MICRO_BATCHES * E)
        g = x_attn.reshape(MICRO_BATCHES, E, tpe, Dx)
        h = jax.nn.gelu(jnp.einsum('metd,edf->metf', g, w1) + b1[None, :, None, :], approximate=False)
        y = jnp.einsum('metf,efd->metd', h, w2) + b2[None, :, None, :]
        out = jax.nn.gelu(y @ next_w + next_b, approximate=False)
        return out.reshape(Bx, Sx, Dx)

    def _L3_attn_ref(x, ln_g, ln_b, W_in, b_in, W_out, b_out, gamma_q, beta_q, gamma_k, beta_k):
        import jax, jax.numpy as jnp
        import numpy as np
        D = 128
        E = 2 * D
        S = 128
        LN_EPS = 1e-05
        seq_len = x.shape[1]
        mu = jnp.mean(x, axis=-1, keepdims=True)
        var = jnp.mean(jnp.square(x - mu), axis=-1, keepdims=True)
        xn = (x - mu) * jax.lax.rsqrt(var + LN_EPS) * ln_g + ln_b
        uvz = jax.nn.silu(jnp.einsum('bld,df->blf', xn, W_in) + b_in)
        u, v, z = (uvz[..., :E], uvz[..., E:2 * E], uvz[..., 2 * E:])
        q = z * gamma_q + beta_q
        k = z * gamma_k + beta_k
        attn = jnp.einsum('bqs,bks->bqk', q, k) / seq_len
        attn = jnp.square(jax.nn.relu(attn))
        out = u * jnp.einsum('bqk,bke->bqe', attn, v)
        return x + jnp.einsum('ble,ed->bld', out, W_out) + b_out

    def _L3_ffn_ref(x, wg, w1, b1, w2, b2):
        import jax, jax.numpy as jnp
        import numpy as np
        B, S, M, E, DFF = (4, 256, 128, 8, 512)
        CAPACITY_FACTOR = 1.25

        def _top1_gate(tokens, wg, capacity):
            gates = jax.nn.softmax(tokens @ wg)
            expert_idx = jnp.argmax(gates, axis=-1)
            mask1 = jax.nn.one_hot(expert_idx, gates.shape[-1], dtype=gates.dtype)
            pos = jnp.sum(jnp.cumsum(mask1, axis=0) * mask1, axis=-1).astype(jnp.int32) - 1
            keep = (pos < capacity).astype(gates.dtype)
            mask1c = mask1 * keep[:, None]
            gates1 = jnp.sum(gates * mask1c, axis=-1)
            loc_oh = jax.nn.one_hot(pos, capacity, dtype=gates.dtype)
            combine = gates1[:, None, None] * mask1c[:, :, None] * loc_oh[:, None, :]
            dispatch = (combine > 0).astype(tokens.dtype)
            return (combine, dispatch)
        d_model = x.shape[-1]
        tokens = x.reshape(-1, d_model)
        T = tokens.shape[0]
        num_experts = wg.shape[1]
        capacity = int(CAPACITY_FACTOR * T / num_experts)
        combine, dispatch = _top1_gate(tokens, wg, capacity)
        dispatched = jnp.einsum('sec,sm->ecm', dispatch, tokens)
        h = jax.nn.relu(jnp.einsum('ecm,emf->ecf', dispatched, w1) + b1[:, None, :])
        expert_out = jnp.einsum('ecf,efm->ecm', h, w2) + b2[:, None, :]
        combined = jnp.einsum('sec,ecm->sm', combine, expert_out)
        return combined.reshape(x.shape)
    x = L0_attn_inputs
    xn = _layernorm(x, axis=-1)
    x = x + _L0_attn_ref(xn, L0_attn_W_in, L0_attn_K_conv, L0_attn_b_conv, L0_attn_W_x, L0_attn_W_dt, L0_attn_b_dt, L0_attn_A_log, L0_attn_D, L0_attn_W_out, L0_attn_b_out) + _L0_ffn_ref(xn, L0_ffn_norm_weight, L0_ffn_router_weight, L0_ffn_router_bias, L0_ffn_fc1_weight, L0_ffn_fc1_bias, L0_ffn_fc2_weight, L0_ffn_fc2_bias, L0_ffn_constant_vectors)
    xn = _layernorm(x, axis=-1)
    x = x + _L1_attn_ref(xn, L1_attn_Wq, L1_attn_bq, L1_attn_Wk, L1_attn_bk, L1_attn_Wv, L1_attn_bv, L1_attn_Wo, L1_attn_bo) + _L1_ffn_ref(xn, L1_ffn_w1, L1_ffn_w2, L1_ffn_w3, L1_ffn_new_w1, L1_ffn_new_w2, L1_ffn_new_w3, L1_ffn_gate_weight, L1_ffn_new_gate_weight, L1_ffn_gate_bias)
    xn = _layernorm(x, axis=-1)
    x = x + _L2_attn_ref(xn, L2_attn_w_qkv, L2_attn_b_qkv, L2_attn_a_q, L2_attn_b_q, L2_attn_a_v, L2_attn_b_v, L2_attn_w_proj, L2_attn_b_proj) + _L2_ffn_ref(xn, L2_ffn_ln_g, L2_ffn_ln_b, L2_ffn_attn_w, L2_ffn_attn_b, L2_ffn_gate_w, L2_ffn_w1, L2_ffn_b1, L2_ffn_w2, L2_ffn_b2, L2_ffn_next_w, L2_ffn_next_b)
    xn = _layernorm(x, axis=-1)
    x = x + _L3_attn_ref(xn, L3_attn_ln_g, L3_attn_ln_b, L3_attn_W_in, L3_attn_b_in, L3_attn_W_out, L3_attn_b_out, L3_attn_gamma_q, L3_attn_beta_q, L3_attn_gamma_k, L3_attn_beta_k) + _L3_ffn_ref(xn, L3_ffn_wg, L3_ffn_w1, L3_ffn_b1, L3_ffn_w2, L3_ffn_b2)
    return x

_drawn_inputs = setup_inputs


def setup_inputs(seed=0):
    import zlib

    import numpy as np

    out = dict(_drawn_inputs(seed))
    spreads = {'L0_attn_b_conv': (0.0, 0.1),
     'L0_attn_b_dt': (0.0, 0.1),
     'L0_attn_D': (1.0, 0.2),
     'L0_attn_b_out': (0.0, 0.1),
     'L0_ffn_norm_weight': (1.0, 0.2),
     'L0_ffn_router_bias': (0.0, 0.1),
     'L0_ffn_fc1_bias': (0.0, 0.8),
     'L0_ffn_fc2_bias': (0.0, 0.1),
     'L1_ffn_new_w2': (0.0, 0.8),
     'L2_ffn_ln_g': (1.0, 0.6),
     'L2_ffn_ln_b': (0.0, 0.407),
     'L2_ffn_attn_b': (0.0, 0.308),
     'L2_ffn_b1': (0.0, 0.35),
     'L2_ffn_b2': (0.0, 0.411),
     'L2_ffn_next_b': (0.0, 0.272),
     'L3_attn_ln_g': (1.0, 0.6),
     'L3_attn_ln_b': (0.0, 0.733),
     'L3_attn_b_in': (0.0, 0.8),
     'L3_attn_b_out': (0.0, 0.8),
     'L3_attn_gamma_q': (1.0, 0.6),
     'L3_attn_beta_q': (0.0, 0.8),
     'L3_attn_gamma_k': (1.0, 0.6),
     'L3_attn_beta_k': (0.0, 0.8),
     'L3_ffn_b1': (0.0, 2.0),
     'L3_ffn_b2': (0.0, 2.0)}
    factors = {'L0_attn_A_log': 6.579,
     'L0_ffn_fc1_weight': 3.013,
     'L0_ffn_fc2_weight': 2.703,
     'L0_ffn_constant_vectors': 8.0,
     'L1_attn_bq': 64.0,
     'L1_attn_bk': 64.0,
     'L1_attn_bv': 7.839,
     'L1_attn_bo': 21.963,
     'L1_ffn_w1': 8.0,
     'L1_ffn_w2': 8.0,
     'L1_ffn_w3': 8.0,
     'L1_ffn_new_w1': 8.0,
     'L1_ffn_new_w3': 8.0,
     'L1_ffn_gate_weight': 8.0,
     'L1_ffn_new_gate_weight': 8.0,
     'L2_attn_b_qkv': 5.265,
     'L2_attn_a_q': 5.05,
     'L2_attn_b_q': 4.175,
     'L2_attn_a_v': 3.825,
     'L2_attn_b_v': 4.355,
     'L2_attn_b_proj': 5.474,
     'L3_ffn_wg': 36.72,
     'L3_ffn_w1': 46.21,
     'L3_ffn_w2': 36.134}
    for name, (base, spread) in spreads.items():
        noise = np.random.default_rng([zlib.crc32(name.encode()), seed]).standard_normal(out[name].shape)
        drawn = base * np.exp(spread * noise) if base else spread * noise
        out[name] = jnp.asarray(drawn.astype(out[name].dtype))
    for name, factor in factors.items():
        out[name] = (out[name] * factor).astype(out[name].dtype)
    return out
```

```python
from collections import namedtuple
from contextlib import ExitStack, contextmanager

import concourse.bass as bass
from concourse import mybir

F32 = mybir.dt.float32
BF16 = mybir.dt.bfloat16
I32 = mybir.dt.int32
ALU = mybir.AluOpType
ACT = mybir.ActivationFunctionType
AX_X = mybir.AxisListType.X

P = 128
D = 128
BATCH, T = 16, 256
N = BATCH * T
NT = N // P
QT = T // P
HEADS = 16
HD = D // HEADS
LN_EPS = 1e-5
OUT_OF_RANGE = 65536.0
TAKEN = -1e30
EXP_CENTRE = 2e-6

DI, DS, DTR, TAPS = 256, 16, 64, 4
DC = DI // P
E0, CAP0, F0, FIRST_MLP0 = 16, 512, 512, 4
E1, H1 = 9, 352
H1_CUTS = [(0, 128), (128, 128), (256, 96)]
TILES1 = (2 * N + E1 * (P - 1)) // P
E2, F2 = 8, 512
EG = 256
E3, CAP3, F3 = 8, 640, 512
FC = F0 // P


class Names:
    pass


class Chain:

    def __init__(self, eng, sem, base=0):
        self.eng, self.sem, self.base, self.n = eng, sem, base, 0

    def add(self, ins):
        self.n += 1
        ins.then_inc(self.sem, 1)

    def wait(self):
        self.eng.wait_ge(self.sem, self.base + self.n)

    def step(self, ins):
        self.add(ins)
        self.wait()


@contextmanager
def section(nc, title, *names):
    sems = [nc.alloc_semaphore(f"{title}_{n}") for n in names]
    with ExitStack() as ctx:
        def sb(name, shape, dt=F32):
            return ctx.enter_context(nc.sbuf_tensor(f"{title}_{name}", shape, dt))

        yield namedtuple("Section", names + ("sems", "sb"))(*sems, sems, sb)
    nc.clear_and_free_semaphores(sems)
    nc.all_engine_barrier()


def rows(ap):
    return ap.rearrange("p a b -> p (a b)")


def setup(nc, g, t):
    with section(nc, "setup", "x_in", "filled", "consts") as s, nc.Block() as block:

        @block.sync
        def _(sp):
            sp.dma_start(g.x[:], t["x"].rearrange("(t p) d -> p t d", p=P)).then_inc(s.x_in, 16)
            sp.wait_ge(s.x_in, 16)

        @block.gpsimd
        def _(pool):
            for b, v in ((g.ident, 0.0), (g.ident_b, 0.0), (g.ones_b, 1.0), (g.before, 0.0), (g.after_neg, 0.0),
                         (g.ones_row, 1.0), (g.zeros, 0.0), (g.head_sel, 0.0), (g.future_q, 0.0)):
                nc.gpsimd.memset(b[:], v).then_inc(s.filled, 1)
            pool.wait_ge(s.filled, 9)
            for b in (g.ident, g.ident_b):
                nc.gpsimd.affine_select(out=b[:], in_=b[:], compare_op=ALU.not_equal, fill=1.0, base=0,
                                        pattern=[[-1, P]], channel_multiplier=1).then_inc(s.consts, 1)
            nc.gpsimd.affine_select(out=g.before[:], in_=g.before[:], compare_op=ALU.is_ge, fill=1.0, base=0,
                                    pattern=[[-1, P]], channel_multiplier=1).then_inc(s.consts, 1)
            nc.gpsimd.affine_select(out=g.after_neg[:], in_=g.after_neg[:], compare_op=ALU.is_ge, fill=-1e30, base=0,
                                    pattern=[[1, P]], channel_multiplier=-1).then_inc(s.consts, 1)
            nc.gpsimd.affine_select(out=g.future_q[:], in_=g.future_q[:], compare_op=ALU.is_ge, fill=-1e30, base=0,
                                    pattern=[[-1, P]], channel_multiplier=1).then_inc(s.consts, 1)
            for half in range(2):
                v = g.head_sel[:]
                nc.gpsimd.affine_select(out=v, in_=v, compare_op=ALU.not_equal, fill=-1.0, base=-HEADS * half,
                                        pattern=[[-1, HEADS], [0, P]], channel_multiplier=1).then_inc(s.consts, 1)
                pool.wait_ge(s.consts, 6 + half)


def normalise(nc, g, title, src, dst, dst_t, kind, scale_col=None, bias_col=None, w_row=None):
    G = 4
    with section(nc, title, "cols_in", "stats_done", "aggr_done", "var_ready", "std_ready", "rstd_step", "xn_ready",
                 "turned", "t_ready") as s:
        stats = s.sb("stats", [P, NT, 6])
        mv = s.sb("mv", [P, NT, 2])
        std = s.sb("std", [P, NT])
        rstd = s.sb("rstd", [P, NT])
        inv = s.sb("inv", [P, NT])
        cols = s.sb("norm_cols", [P, 2])
        wr = s.sb("norm_row", [P, D])
        n_cols = 0
        with nc.Block() as block:

            @block.sync
            def _(sp):
                nonlocal n_cols
                for c, col in enumerate((scale_col, bias_col)):
                    if col is not None:
                        sp.dma_start(cols[:, c:c + 1], col).then_inc(s.cols_in, 16)
                        n_cols += 16
                if w_row is not None:
                    sp.dma_start(wr[:], w_row.to_broadcast([P, D])).then_inc(s.cols_in, 16)
                    n_cols += 16

            @block.vector
            def _(dve):
                for i in range(NT):
                    nc.vector.bn_stats(stats[:, i, :], src[:, i, :]).then_inc(s.stats_done, 1)
                for i in range(NT):
                    dve.wait_ge(s.stats_done, i + 1)
                    nc.vector.bn_aggr(mv[:, i, :], stats[:, i, :]).then_inc(s.aggr_done, 1)
                dve.wait_ge(s.aggr_done, NT)
                step = Chain(dve, s.rstd_step)
                var = mv[:, :, 1]
                if kind == "rms":
                    step.step(nc.vector.tensor_tensor(std[:], mv[:, :, 0], mv[:, :, 0], ALU.mult))
                    step.step(nc.vector.tensor_tensor(std[:], std[:], mv[:, :, 1], ALU.add))
                    var = std[:]
                nc.vector.tensor_scalar(rstd[:], var, LN_EPS, None, ALU.add).then_inc(s.var_ready, 1)
                dve.wait_ge(s.std_ready, 1)
                step.step(nc.vector.reciprocal(inv[:], std[:]))
                step.step(nc.vector.tensor_tensor(rstd[:], rstd[:], inv[:], ALU.mult))
                step.step(nc.vector.tensor_tensor(rstd[:], rstd[:], inv[:], ALU.mult))
                step.step(nc.vector.tensor_scalar(rstd[:], rstd[:], -0.5, 1.5, ALU.mult, ALU.add))
                step.step(nc.vector.tensor_tensor(rstd[:], rstd[:], inv[:], ALU.mult))
                if n_cols:
                    dve.wait_ge(s.cols_in, n_cols)
                for i in range(NT):
                    if kind == "ln":
                        ins = nc.vector.tensor_scalar(dst[:, i, :], src[:, i, :], mv[:, i, 0:1], rstd[:, i:i + 1],
                                                      ALU.subtract, ALU.mult)
                    else:
                        ins = nc.vector.scalar_tensor_tensor(out=dst[:, i, :], in0=src[:, i, :],
                                                             scalar=rstd[:, i:i + 1], in1=wr[:],
                                                             op0=ALU.mult, op1=ALU.mult)
                    ins.then_inc(s.xn_ready, 1)

            @block.tensor
            def _(pe):
                for i in range(NT):
                    pe.wait_ge(s.xn_ready, i + 1)
                    ins = nc.tensor.transpose(g.ps[:, i // G, (i % G) * P:(i % G + 1) * P], dst[:, i, :], g.ident[:])
                    if i % G == G - 1:
                        ins.then_inc(s.turned, 1)

            @block.scalar
            def _(act):
                act.wait_ge(s.var_ready, 1)
                nc.scalar.activation(std[:], rstd[:], ACT.Sqrt).then_inc(s.std_ready, 1)
                if n_cols:
                    act.wait_ge(s.cols_in, n_cols)
                for b in range(NT // G):
                    act.wait_ge(s.turned, b + 1)
                    to = dst_t[:, b * G * P:(b + 1) * G * P]
                    if scale_col is not None:
                        nc.scalar.activation(to, g.ps[:, b, :], ACT.Identity, scale=cols[:, 0:1],
                                             bias=cols[:, 1:2]).then_inc(s.t_ready, 1)
                    else:
                        nc.scalar.copy(to, g.ps[:, b, :]).then_inc(s.t_ready, 1)
                act.wait_ge(s.t_ready, NT // G)


def mamba_in(nc, g, t, u, gate):
    XZ = 8
    with section(nc, "conv", "w_in", "xz_ready", "conv_step", "act_done") as s:
        w = s.sb("w_in_sb", [P, 2 * DI])
        taps = s.sb("taps", [P, DC, TAPS])
        bc = s.sb("b_conv", [P, DC])
        acc = s.sb("conv_acc", [P, 2, DC, T])
        with nc.Block() as block:

            @block.sync
            def _(sp):
                for dst, src in ((w, "m_w_in"), (taps, "m_taps"), (bc, "m_b_conv")):
                    sp.dma_start(dst[:], t[src]).then_inc(s.w_in, 16)

            def batches(eng, body):
                with eng.Fori(0, BATCH // 2) as it:
                    for p in range(2):
                        body(it * 2 + p, p)

            @block.tensor
            def _(pe):
                pe.wait_ge(s.w_in, 48)

                def body(b, p):
                    pe.wait_ge(s.conv_step, b * XZ + XZ)
                    pe.wait_ge(s.act_done, b + 1)
                    for c in range(2 * DC):
                        ins = nc.tensor.matmul(g.ps[:, 2 * p + c // DC, (c % DC) * T:(c % DC + 1) * T],
                                               w[:, c * P:(c + 1) * P], g.xn_t[:, bass.ds(b * T, T)],
                                               start=True, stop=True)
                    ins.then_inc(s.xz_ready, 1)
                batches(pe, body)

            @block.vector
            def _(dve):
                dve.wait_ge(s.w_in, 48)
                dve.sem_inc(s.conv_step, 2 * XZ)

                def body(b, p):
                    dve.wait_ge(s.xz_ready, b + 1)
                    dve.wait_ge(s.act_done, b + 1)
                    step = Chain(dve, s.conv_step, b * XZ + 2 * XZ)
                    for k, shift in ((1, 0), (0, -1), (2, 1), (3, 2)):
                        for c in range(DC):
                            x = g.ps[:, 2 * p, c * T:(c + 1) * T]
                            a = acc[:, p, c, :]
                            if shift == 0:
                                ins = nc.vector.tensor_scalar(a, x, taps[:, c, k:k + 1], None, ALU.mult)
                            else:
                                lo, hi = max(0, -shift), T - max(0, shift)
                                ins = nc.vector.scalar_tensor_tensor(
                                    out=a[:, lo:hi], in0=x[:, lo + shift:hi + shift], scalar=taps[:, c, k:k + 1],
                                    in1=a[:, lo:hi], op0=ALU.mult, op1=ALU.add)
                            step.add(ins)
                        if shift != 2:
                            step.wait()
                    assert step.n == XZ
                batches(dve, body)

            @block.scalar
            def _(act):
                act.wait_ge(s.w_in, 48)
                nc.scalar.preload_act_table(ACT.Silu)
                act.sem_inc(s.act_done, 2)

                def body(b, p):
                    act.wait_ge(s.xz_ready, b + 1)
                    nc.scalar.activation(gate[:, :, bass.ds(b * T, T)],
                                         g.ps[:, 2 * p + 1, :].rearrange("p (c t) -> p c t", c=DC), ACT.Silu)
                    act.wait_ge(s.conv_step, b * XZ + 3 * XZ)
                    for c in range(DC):
                        ins = nc.scalar.activation(u[:, c, bass.ds(b * T, T)], acc[:, p, c, :], ACT.Silu,
                                                   bias=bc[:, c:c + 1])
                    ins.then_inc(s.act_done, 1)
                batches(act, body)


def mamba_scan(nc, g, t, u, gate):
    NG, GN = 4, DS // 4
    KBC = 3 * 2 * DS
    with section(nc, "scan", "w_in", "sel_fill", "sel_done", "neg_a", "dtbc_ready", "dtx_ready", "bc_step", "z_ready",
                 "act_step", "zr_step", "b_ready", "c_ready", "bu_used", "da_ready", "scan_step", "hc_ready",
                 "y_ready", "yg_ready", "o_ready", "x_done", "z_free", "hc_free") as s:
        w_dt_in = s.sb("w_dt_in", [P, DTR])
        w_bc = s.sb("w_bc", [P, KBC])
        w_dt = s.sb("w_dt", [DTR, DI])
        b_dt = s.sb("b_dt", [P, DC])
        a_neg = s.sb("a_neg", [P, DC, DS])
        d_col = s.sb("d_col", [P, DC])
        w_out = s.sb("w_out_m", [P, DC, D])
        b_out = s.sb("b_out_m", [1, D])
        sel = s.sb("state_sel", [KBC, 2 * DS, P], BF16)
        dtx = s.sb("dtx", [DTR, T])
        bc3 = s.sb("bc3", [KBC, T], BF16)
        rem = s.sb("bc_rem", [KBC, T])
        zr = s.sb("zr", [P, DC, T])
        e1 = s.sb("e1", [P, DC, T])
        exp_centre = s.sb("exp_centre", [P, 1])
        delta = s.sb("delta", [P, DC, T])
        du = s.sb("du", [P, DC, T])
        da = s.sb("da", [P, 2, GN, T])
        bu = s.sb("bu", [P, 2, GN, T])
        h = s.sb("h", [P, 2, GN, T])
        hc = s.sb("hc", [P, 2, GN, T])
        yg = s.sb("yg", [P, DC, T])
        b_ps = g.ps[:, 0:2, :].rearrange("p k (n t) -> p (k n) t", t=T)
        c_ps = g.ps[:, 2:4, :].rearrange("p k (n t) -> p (k n) t", t=T)
        with nc.Block() as block:

            @block.sync
            def _(sp):
                for dst, src in ((w_dt_in, "m_w_dt_in"), (w_bc, "m_w_bc"), (w_dt, "m_w_dt"), (b_dt, "m_b_dt"),
                                 (a_neg, "m_a_log"), (d_col, "m_d"), (w_out, "m_w_out"), (b_out, "m_b_out")):
                    sp.dma_start(dst[:], t[src]).then_inc(s.w_in, 16)

            W_IN = 8 * 16

            @block.gpsimd
            def _(pool):
                nc.gpsimd.memset(sel[:], 0.0).then_inc(s.sel_fill, 1)
                pool.wait_ge(s.sel_fill, 1)
                for q in range(3):
                    v = sel[2 * DS * q:2 * DS * (q + 1), :, :]
                    nc.gpsimd.affine_select(out=v, in_=v, compare_op=ALU.not_equal, fill=1.0, base=0,
                                            pattern=[[-1, 2 * DS], [0, P]],
                                            channel_multiplier=1).then_inc(s.sel_done, 1)
                    pool.wait_ge(s.sel_done, q + 1)
                nc.gpsimd.memset(exp_centre[:], EXP_CENTRE); nc.gpsimd.memset(da[:, :, :, 0:1], 0.0).then_inc(s.sel_done, 1)

            @block.tensor
            def _(pe):
                pe.wait_ge(s.w_in, W_IN)
                pe.wait_ge(s.sel_done, 4)
                with pe.Fori(0, BATCH) as b:
                    x = g.xn_t[:, bass.ds(b * T, T)]
                    pe.wait_ge(s.z_free, b + 1)
                    nc.tensor.matmul(g.ps[0:DTR, 6, 0:T], w_dt_in[:], x, start=True, stop=True)
                    nc.tensor.matmul(g.ps[0:KBC, 6, T:2 * T], w_bc[:], x, start=True,
                                     stop=True).then_inc(s.dtbc_ready, 1)
                    pe.wait_ge(s.dtx_ready, b + 1)
                    pe.wait_ge(s.x_done, b + 1)
                    for c in range(DC):
                        ins = nc.tensor.matmul(g.ps[:, 7, c * T:(c + 1) * T], w_dt[:, c * P:(c + 1) * P], dtx[:],
                                               start=True, stop=True)
                    ins.then_inc(s.z_ready, 1)
                    pe.wait_ge(s.bc_step, b * 5 + 5)
                    for gi in range(NG + 1):
                        if gi < NG:
                            pe.wait_ge(s.bu_used, b * 2 * NG + 2 * gi + 2)
                            for n in range(GN):
                                ins = nc.tensor.matmul(b_ps[:, n, :], sel[:, gi * GN + n, :], bc3[:],
                                                       start=True, stop=True)
                            ins.then_inc(s.b_ready, 1)
                        if gi > 0:
                            for c in range(DC):
                                pe.wait_ge(s.hc_ready, b * 2 * NG + 2 * (gi - 1) + c + 1 + 2)
                                for n in range(GN):
                                    ins = nc.tensor.matmul(g.ps[:, 4 + c, 0:T], g.ident[:], hc[:, c, n, :],
                                                           start=(gi == 1 and n == 0), stop=(gi == NG and n == GN - 1))
                                ins.then_inc(s.y_ready, 1)
                        if gi < NG:
                            pe.wait_ge(s.hc_ready, b * 2 * NG + 2 * gi + 2)
                            for n in range(GN):
                                ins = nc.tensor.matmul(c_ps[:, n, :], sel[:, DS + gi * GN + n, :], bc3[:],
                                                       start=True, stop=True)
                            ins.then_inc(s.c_ready, 1)
                    pe.wait_ge(s.yg_ready, (b + 1) * DC)
                    for k in range(QT):
                        o = g.ps[:, 7, k * D:(k + 1) * D]
                        for c in range(DC):
                            nc.tensor.matmul(o, yg[:, c, k * P:(k + 1) * P], w_out[:, c, :], start=(c == 0), stop=False)
                        ins = nc.tensor.matmul(o, g.ones_row[:], b_out[:], start=False, stop=True)
                    ins.then_inc(s.o_ready, 1)

            @block.scalar
            def _(act):
                act.wait_ge(s.w_in, W_IN)
                nc.scalar.preload_act_table(ACT.Exp)
                nc.scalar.activation(a_neg[:], a_neg[:], ACT.Exp).then_inc(s.neg_a, 1)
                act.wait_ge(s.neg_a, 2)
                act.wait_ge(s.sel_done, 4)
                with act.Fori(0, BATCH) as b:
                    act.wait_ge(s.zr_step, b * 4 + 2)
                    step = Chain(act, s.act_step, b * 3)
                    step.step(nc.scalar.activation(e1[:], zr[:], ACT.Abs))
                    step.step(nc.scalar.activation(e1[:], e1[:], ACT.Exp, scale=-1.0))
                    step.add(nc.scalar.activation(e1[:], e1[:], ACT.Ln, bias=1.0))
                    act.wait_ge(s.zr_step, b * 4 + 3)
                    for gi in range(NG):
                        for c in range(DC):
                            act.wait_ge(s.scan_step, b * 2 * NG + 2 * gi + c + 1)
                            for n in range(GN):
                                ins = nc.scalar.activation(da[:, c, n, 1:T], delta[:, c, 1:T], ACT.Exp,
                                                           scale=a_neg[:, c, gi * GN + n:gi * GN + n + 1], bias=exp_centre[:])
                            ins.then_inc(s.da_ready, 1)

            @block.vector
            def _(dve):
                dve.wait_ge(s.w_in, W_IN)
                dve.wait_ge(s.neg_a, 1)
                nc.vector.tensor_scalar(a_neg[:], a_neg[:], -1.0, None, ALU.mult).then_inc(s.neg_a, 1)
                for sem, n in ((s.x_done, 1), (s.bu_used, 2), (s.hc_ready, 2), (s.scan_step, 2), (s.z_free, 1),
                               (s.hc_free, 2)):
                    dve.sem_inc(sem, n)
                with dve.Fori(0, BATCH) as b:
                    dve.wait_ge(s.dtbc_ready, b + 1)
                    dve.wait_ge(s.c_ready, b * NG)
                    nc.vector.tensor_copy(dtx[:], g.ps[0:DTR, 6, 0:T]).then_inc(s.dtx_ready, 1)
                    raw = g.ps[0:KBC, 6, T:2 * T]
                    step = Chain(dve, s.bc_step, b * 5)
                    W = 2 * DS
                    step.step(nc.vector.tensor_copy(bc3[:], raw))
                    step.step(nc.vector.tensor_tensor(rem[:], raw, bc3[:], ALU.subtract))
                    step.step(nc.vector.tensor_copy(bc3[W:2 * W, :], rem[W:2 * W, :]))
                    step.step(nc.vector.tensor_copy(bc3[2 * W:3 * W, :], rem[2 * W:3 * W, :]))
                    step.step(nc.vector.tensor_tensor(bc3[2 * W:3 * W, :], rem[2 * W:3 * W, :], bc3[2 * W:3 * W, :],
                                                      ALU.subtract))
                    dve.wait_ge(s.z_ready, b + 1)
                    zs = Chain(dve, s.zr_step, b * 4)
                    for c in range(DC):
                        zs.add(nc.vector.tensor_scalar(zr[:, c, :], g.ps[:, 7, c * T:(c + 1) * T], b_dt[:, c:c + 1],
                                                       None, ALU.add))
                    zs.wait()
                    dve.wait_ge(s.act_step, b * 3 + 3)
                    zs.step(nc.vector.scalar_tensor_tensor(out=delta[:], in0=zr[:], scalar=0.0, in1=e1[:],
                                                           op0=ALU.max, op1=ALU.add))
                    zs.step(nc.vector.tensor_tensor(du[:], delta[:], u[:, :, bass.ds(b * T, T)], ALU.mult))
                    dve.sem_inc(s.z_free, 1)
                    for gi in range(NG):
                        for c in range(DC):
                            k = b * 2 * NG + 2 * gi + c + 1
                            if c == 0:
                                dve.wait_ge(s.b_ready, b * NG + gi + 1)
                            nc.vector.tensor_tensor(bu[:, c, :, :], b_ps,
                                                    du[:, c:c + 1, :].to_broadcast([P, GN, T]),
                                                    ALU.mult).then_inc(s.bu_used, 1)
                            dve.wait_ge(s.bu_used, k + 2)
                            dve.wait_ge(s.da_ready, k)
                            nc.vector.tensor_tensor_scan(h[:, c].rearrange("p n t -> p (n t)"),
                                                         da[:, c].rearrange("p n t -> p (n t)"),
                                                         bu[:, c].rearrange("p n t -> p (n t)"), 0.0,
                                                         ALU.mult, ALU.add).then_inc(s.scan_step, 1)
                            dve.wait_ge(s.scan_step, k + 2)
                            if c == 0:
                                dve.wait_ge(s.c_ready, b * NG + gi + 1)
                            dve.wait_ge(s.y_ready, b * 2 * NG + 2 * gi + c if gi else b * 2 * NG)
                            nc.vector.tensor_tensor(hc[:, c, :, :], h[:, c, :, :], c_ps,
                                                    ALU.mult).then_inc(s.hc_ready, 1)
                    for c in range(DC):
                        dve.wait_ge(s.y_ready, b * 2 * NG + 2 * (NG - 1) + c + 1)
                        nc.vector.scalar_tensor_tensor(out=zr[:, c, :], in0=u[:, c, bass.ds(b * T, T)],
                                                       scalar=d_col[:, c:c + 1], in1=g.ps[:, 4 + c, 0:T],
                                                       op0=ALU.mult, op1=ALU.add).then_inc(s.hc_free, 1)
                    dve.wait_ge(s.hc_free, b * 2 + 4)
                    for c in range(DC):
                        nc.vector.tensor_tensor(yg[:, c, :], zr[:, c, :], gate[:, c, bass.ds(b * T, T)],
                                                ALU.mult).then_inc(s.yg_ready, 1)
                    dve.wait_ge(s.o_ready, b + 1)
                    xs = g.x[:, bass.ds(b * QT, QT), :]
                    nc.vector.tensor_tensor(xs, xs, g.ps[:, 7, 0:QT * D].rearrange("p (k d) -> p k d", k=QT),
                                            ALU.add).then_inc(s.x_done, 1)


def route(nc, g, t, title, src, src_t, router, n_exp, top, cap, first, disp, r):
    E, K = n_exp, top
    n_rows = disp.shape[0]
    with section(nc, title, "w_in", "zeroed", "iota_done", "logits_ready", "step", "shift_ready", "exp_ready",
                 "chosen_ready", "pos_ready", "rows_ready", "scattered") as s:
        W = s.sb("router", [P, E])
        bias = s.sb("bias", [P, E])
        rev = s.sb("rev", [P, E])
        lg = s.sb("lg", [P, NT, E])
        p = s.sb("p", [P, NT, E])
        tmp = s.sb("tmp", [P, NT, E])
        oh = s.sb("onehot", [P, K, NT, E])
        chosen = s.sb("chosen", [P, NT, E], BF16)
        mx = s.sb("mx", [P, NT])
        val = s.sb("val", [P, K, NT])
        rm = s.sb("rm", [P, K, NT])
        sm = s.sb("sm", [P, NT])
        tot = s.sb("tot", [P, E, NT])
        inc = s.sb("inc", [P, E, NT])
        cont = s.sb("cont", [P, E, NT])
        pos = s.sb("pos", [P, NT, E])
        slot = s.sb("slot", [P, K, NT])
        keep = s.sb("keep", [P, K, NT])
        scat = s.sb("scat", [P, K, NT])
        scat_i = s.sb("scat_i", [P, K, NT], I32)
        cnt = s.sb("cnt", [P, E])
        cnt_i = s.sb("cnt_i", [P, E], I32)
        n_tiles = s.sb("n_tiles", [P, E])
        ends = s.sb("ends", [P, E])
        ones_e = s.sb("ones_e", [P, E])
        jot = s.sb("jot", [1, TILES1])
        cmp = s.sb("cmp", [1, TILES1, E])
        te = s.sb("te", [1, TILES1])

        def per_token(ap):
            return ap[:, :, None].to_broadcast([P, NT, E])

        def per_expert(ap):
            return ap[:, None, :].to_broadcast([P, NT, E])

        with nc.Block() as block:

            @block.sync
            def _(sp):
                sp.dma_start(W[:], t[router]).then_inc(s.w_in, 16)
                if title == "route0":
                    sp.dma_start(bias[:], t["f0_router_b"].to_broadcast([P, E])).then_inc(s.w_in, 16)
                if title == "route1":
                    sp.dma_start(bias[:], t["f1_gate_b"].to_broadcast([P, E])).then_inc(s.w_in, 16)
                rep = n_rows * D // P // 512
                sp.dma_start(disp.rearrange("(p r) d -> p (r d)", p=P).rearrange("p (r c) -> p r c", c=512),
                             g.zeros[:, None, :].to_broadcast([P, rep, 512])).then_inc(s.zeroed, 16)

            n_w = 32 if title in ("route0", "route1") else 16

            @block.tensor
            def _(pe):
                pe.wait_ge(s.w_in, n_w)
                for i in range(NT):
                    ins = nc.tensor.matmul(g.ps[:, 0, i * E:(i + 1) * E], src_t[:, i * P:(i + 1) * P], W[:],
                                           start=True, stop=True)
                ins.then_inc(s.logits_ready, 1)
                pe.wait_ge(s.chosen_ready, 1)
                ch = chosen[:].rearrange("p t e -> p (t e)")
                nc.tensor.matmul(g.ps[:, 1, 0:NT * E], g.before[:], ch, start=True, stop=True)
                nc.tensor.matmul(g.ps[:, 2, 0:NT * E], g.ones_b[:], ch, start=True, stop=True).then_inc(s.pos_ready, 1)

            @block.scalar
            def _(act):
                if title == "route0":
                    nc.scalar.preload_act_table(ACT.Sigmoid)
                    act.wait_ge(s.shift_ready, 1)
                    nc.scalar.activation(val[:, 0, :], sm[:], ACT.Sigmoid)
                    nc.scalar.activation(val[:, 1, :], sm[:], ACT.Sigmoid, scale=-1.0).then_inc(s.exp_ready, 1)
                else:
                    act.wait_ge(s.shift_ready, 1)
                    nc.scalar.activation(p[:], lg[:], ACT.Sigmoid if title == "route1" else ACT.Exp
                                         ).then_inc(s.exp_ready, 1)

            @block.vector
            def _(dve):
                c = Chain(dve, s.step)
                v = nc.vector
                dve.wait_ge(s.w_in, n_w)
                dve.wait_ge(s.iota_done, 2)
                c.add(v.memset(cont[:], 1.0))
                c.add(v.memset(ones_e[:], 1.0))
                c.wait()
                c.add(v.memset(cont[:, :, 0:1], 0.0))
                dve.wait_ge(s.logits_ready, 1)
                lps = g.ps[:, 0, 0:NT * E].rearrange("p (t e) -> p t e", e=E)
                if n_w == 32:
                    c.step(v.tensor_tensor(p[:] if title == "route0" else lg[:], lps, per_expert(bias[:]), ALU.add))
                else:
                    c.step(v.tensor_copy(lg[:], lps))
                if title == "route3":
                    c.step(v.tensor_reduce(mx[:], lg[:], AX_X, ALU.max))
                    c.step(v.tensor_tensor(lg[:], lg[:], per_token(mx[:]), ALU.subtract))
                if title != "route0":
                    dve.sem_inc(s.shift_ready, 1)
                    dve.wait_ge(s.exp_ready, 1)
                if title == "route3":
                    c.step(v.tensor_reduce(sm[:], p[:], AX_X, ALU.add))
                    c.step(v.reciprocal(sm[:], sm[:]))
                    c.step(v.tensor_tensor(p[:], p[:], per_token(sm[:]), ALU.mult))
                for k in range(K):
                    c.step(v.tensor_reduce(val[:, k, :], p[:], AX_X, ALU.max))
                    c.step(v.tensor_tensor(tmp[:], p[:], per_token(val[:, k, :]), ALU.is_ge))
                    c.step(v.tensor_tensor(tmp[:], tmp[:], per_expert(rev[:]), ALU.mult))
                    c.step(v.tensor_reduce(rm[:, k, :], tmp[:], AX_X, ALU.max))
                    c.step(v.tensor_tensor(oh[:, k], per_token(rm[:, k, :]), per_expert(rev[:]), ALU.is_equal))
                    if k + 1 < K:
                        c.step(v.scalar_tensor_tensor(out=p[:], in0=oh[:, k], scalar=TAKEN, in1=p[:],
                                                      op0=ALU.mult, op1=ALU.add))
                if title == "route0":
                    c.step(v.tensor_tensor(sm[:], val[:, 0, :], val[:, 1, :], ALU.subtract))
                    dve.sem_inc(s.shift_ready, 1)
                    dve.wait_ge(s.exp_ready, 1)
                if K == 2:
                    c.step(v.tensor_tensor(chosen[:], oh[:, 0], oh[:, 1], ALU.add))
                else:
                    c.step(v.tensor_copy(chosen[:], oh[:, 0]))
                dve.sem_inc(s.chosen_ready, 1)
                dve.wait_ge(s.pos_ready, 1)
                c.step(v.tensor_copy(tot[:], g.ps[:, 2, 0:NT * E].rearrange("p (t e) -> p e t", e=E)))
                c.step(v.tensor_tensor_scan(rows(inc[:]), rows(cont[:]), rows(tot[:]), 0.0, ALU.mult, ALU.add))
                c.step(v.tensor_tensor(tot[:], inc[:], tot[:], ALU.subtract))
                c.step(v.tensor_tensor(pos[:], g.ps[:, 1, 0:NT * E].rearrange("p (t e) -> p t e", e=E),
                                       tot[:].rearrange("p e t -> p t e"), ALU.add))
                if cap is None:
                    c.step(v.tensor_scalar(cnt_i[:], inc[:, :, NT - 1], float(P - 1), None, ALU.add))
                    c.step(v.tensor_scalar(cnt_i[:], cnt_i[:], 7, None, ALU.arith_shift_right))
                    c.step(v.tensor_copy(n_tiles[:], cnt_i[:]))
                    c.step(v.tensor_tensor_scan(ends[:], ones_e[:], n_tiles[:], 0.0, ALU.mult, ALU.add))
                    c.step(v.tensor_tensor(cnt[:], ends[:], n_tiles[:], ALU.subtract))
                    c.step(v.tensor_scalar(cnt[:], cnt[:], float(P), None, ALU.mult))
                    c.step(v.tensor_tensor(pos[:], pos[:], per_expert(cnt[:]), ALU.add))
                    c.step(v.tensor_tensor(cmp[:], jot[:, :, None].to_broadcast([1, TILES1, E]),
                                           ends[0:1, None, :].to_broadcast([1, TILES1, E]), ALU.is_ge))
                    c.step(v.tensor_reduce(te[:], cmp[:], AX_X, ALU.add))
                    c.step(v.tensor_scalar(r.tile_e[:], te[:], float(E - 1), None, ALU.min))
                for k in range(K):
                    c.step(v.tensor_tensor(tmp[:], oh[:, k], pos[:], ALU.mult))
                    c.step(v.tensor_reduce(slot[:, k, :], tmp[:], AX_X, ALU.add))
                if cap is None:
                    c.add(v.tensor_copy(scat_i[:], slot[:]))
                    c.step(v.tensor_copy(r.rows_i[:], slot[:]))
                    dve.sem_inc(s.rows_ready, 1)
                    c.step(v.tensor_tensor(sm[:], val[:, 0, :], val[:, 1, :], ALU.add))
                    c.step(v.tensor_scalar(sm[:], sm[:], 1e-20, None, ALU.add))
                    c.step(v.reciprocal(sm[:], sm[:]))
                    c.step(v.tensor_tensor(r.w[:], val[:], sm[:, None, :].to_broadcast([P, K, NT]), ALU.mult))
                else:
                    c.step(v.tensor_scalar(keep[:], slot[:], float(cap), None, ALU.is_lt))
                    c.step(v.tensor_tensor(val[:], val[:], keep[:], ALU.mult))
                    c.step(v.scalar_tensor_tensor(out=slot[:], in0=rm[:], scalar=-float(cap), in1=slot[:],
                                                  op0=ALU.mult, op1=ALU.add))
                    c.step(v.tensor_scalar(slot[:], slot[:], float((E - first) * cap), None, ALU.add))
                    if first:
                        c.step(v.scalar_tensor_tensor(out=keep[:], in0=rm[:], scalar=float(E - first), in1=keep[:],
                                                      op0=ALU.is_le, op1=ALU.mult))
                    c.step(v.scalar_tensor_tensor(out=scat[:], in0=keep[:], scalar=-OUT_OF_RANGE, in1=slot[:],
                                                  op0=ALU.mult, op1=ALU.add))
                    c.add(v.tensor_scalar(scat_i[:], scat[:], OUT_OF_RANGE, None, ALU.add))
                    c.step(v.tensor_tensor(r.rows_i[:], slot[:], keep[:], ALU.mult))
                    dve.sem_inc(s.rows_ready, 1)
                    if K == 1:
                        c.step(v.tensor_copy(r.w[:], val[:]))
                    else:
                        c.step(v.tensor_tensor(sm[:], val[:, 0, :], val[:, 1, :], ALU.add))
                        c.step(v.scalar_tensor_tensor(out=sm[:], in0=sm[:], scalar=0.0, in1=sm[:],
                                                      op0=ALU.is_le, op1=ALU.add))
                        c.step(v.reciprocal(sm[:], sm[:]))
                        c.step(v.tensor_tensor(val[:], val[:], sm[:, None, :].to_broadcast([P, K, NT]), ALU.mult))
                        c.add(v.tensor_tensor(r.w[:], val[:], keep[:], ALU.mult))
                        F = first
                        for k in range(K):
                            c.step(v.tensor_tensor(oh[:, k, :, 0:F], oh[:, k, :, 0:F],
                                                   val[:, k, :, None].to_broadcast([P, NT, F]), ALU.mult))
                        c.step(v.tensor_tensor(r.near[:], oh[:, 0, :, 0:F], oh[:, 1, :, 0:F], ALU.add))

            @block.gpsimd
            def _(pool):
                nc.gpsimd.iota(rev[:], pattern=[[-1, E]], base=E, channel_multiplier=0,
                               allow_small_or_imprecise_dtypes=True).then_inc(s.iota_done, 1)
                nc.gpsimd.iota(jot[:], pattern=[[1, TILES1]], base=0, channel_multiplier=0,
                               allow_small_or_imprecise_dtypes=True).then_inc(s.iota_done, 1)
                pool.wait_ge(s.rows_ready, 1)
                pool.wait_ge(s.zeroed, 16)
                for i in range(NT):
                    for k in range(K):
                        pool.indirect_dma_start(disp, bass.IndirectOffsetOnAxis(ap=scat_i[:, k, i:i + 1], axis=0),
                                                src[:, i, :], None, bounds_check=n_rows - 1,
                                                oob_is_err=False).then_inc(s.scattered, 16)
                pool.wait_ge(s.scattered, 16 * NT * K)


def experts(nc, g, t, title, packed, n_exp, cap, disp, ybuf, func):
    CT, HC = cap // P, cap // 2
    W2, B1, B2, WN = FC * P, 2 * FC * P, 2 * FC * P + FC, 2 * FC * P + FC + D
    H = 2 * FC
    with section(nc, title, "w_in0", "w_in1", "x_in0", "x_in1", "turned", "xt_ready", "h_ready", "act_done",
                 "y_ready", "y_out", "stored0", "stored1") as s:
        w = s.sb("w", [P, 2, WN])
        xin = s.sb("xin", [P, 2, CT, D])
        xt = s.sb("xt", [P, 2, cap])
        ht = s.sb("ht", [P, FC, cap])
        yo = s.sb("yo", [P, 2, CT, D])
        w_in, x_in, stored = (s.w_in0, s.w_in1), (s.x_in0, s.x_in1), (s.stored0, s.stored1)
        y_ps = g.ps[:, 6:8, :].rearrange("p k c -> p (k c)")[:, 0:CT * D].rearrange("p (t d) -> p t d", d=D)
        t_ps = g.ps[:, 4:6, :].rearrange("p k c -> p (k c)")[:, 0:cap]

        def each(eng, body):
            with eng.Fori(0, n_exp // 2 - 1) as it:
                for p in range(2):
                    body(it * 2 + p, it, p, False)
            body(n_exp - 2, n_exp // 2 - 1, 0, False)
            body(n_exp - 1, n_exp // 2 - 1, 1, True)

        with nc.Block() as block:

            @block.sync
            def _(sp):
                def body(e, it, p, last):
                    sp.wait_ge(s.turned, e + 1)
                    sp.dma_start(xin[:, p], disp[bass.ds(e * cap, cap), :].rearrange("(t p) d -> p t d", p=P)
                                 ).then_inc(x_in[p], 16)
                    sp.wait_ge(s.y_out, e + 1)
                    sp.dma_start(w[:, p], t[packed][bass.ds(e, 1)].rearrange("a p n -> (a p) n")).then_inc(w_in[p], 16)
                each(sp, body)

            @block.tensor
            def _(pe):
                pe.sem_inc(s.turned, 2)
                def transpose(e, it, p):
                    pe.wait_ge(x_in[p], (it + 1) * 16)
                    pe.wait_ge(s.xt_ready, e)
                    for i in range(CT):
                        ins = nc.tensor.transpose(t_ps[:, i * P:(i + 1) * P], xin[:, p, i, :], g.ident[:])
                    ins.then_inc(s.turned, 1)

                def body(e, it, p, last):
                    pe.wait_ge(w_in[p], (it + 1) * 16)
                    pe.wait_ge(s.xt_ready, e + 1)
                    for k in range(H):
                        hf, f = k // FC, k % FC
                        pe.wait_ge(s.act_done, e * H + k + 1)
                        nc.tensor.matmul(g.ps[:, f, 0:HC], w[:, p, f * P:(f + 1) * P], xt[:, p, hf * HC:(hf + 1) * HC],
                                         start=True, stop=True).then_inc(s.h_ready, 1)
                    if not last:
                        transpose(e + 1, it + p, 1 - p)
                    pe.wait_ge(s.act_done, e * H + H + FC)
                    pe.wait_ge(s.y_out, e + 2)
                    for i in range(CT):
                        for f in range(FC):
                            ins = nc.tensor.matmul(y_ps[:, i, :], ht[:, f, i * P:(i + 1) * P],
                                                   w[:, p, W2 + f * P:W2 + (f + 1) * P],
                                                   start=(f == 0), stop=(f == FC - 1))
                    ins.then_inc(s.y_ready, 1)

                transpose(0, 0, 0)
                each(pe, body)

            @block.scalar
            def _(act):
                nc.scalar.preload_act_table(func)
                act.sem_inc(s.act_done, FC)

                def body(e, it, p, last):
                    act.wait_ge(s.y_ready, e)
                    for k in range(H):
                        hf, f = k // FC, k % FC
                        act.wait_ge(s.h_ready, e * H + k + 1)
                        nc.scalar.activation(ht[:, f, hf * HC:(hf + 1) * HC], g.ps[:, f, 0:HC], func,
                                             bias=w[:, p, B1 + f:B1 + f + 1]).then_inc(s.act_done, 1)
                each(act, body)

            @block.vector
            def _(dve):
                dve.sem_inc(s.y_out, 2)

                def take(e, p):
                    dve.wait_ge(s.turned, e + 3)
                    nc.vector.tensor_copy(xt[:, p], t_ps).then_inc(s.xt_ready, 1)

                def body(e, it, p, last):
                    if not last:
                        take(e + 1, 1 - p)
                    dve.wait_ge(s.y_ready, e + 1)
                    dve.wait_ge(stored[p], it * 16)
                    nc.vector.tensor_tensor(yo[:, p], y_ps, w[:, p, None, B2:B2 + D].to_broadcast([P, CT, D]),
                                            ALU.add).then_inc(s.y_out, 1)
                take(0, 0)
                each(dve, body)

            @block.gpsimd
            def _(pool):
                def body(e, it, p, last):
                    pool.wait_ge(s.y_out, e + 3)
                    pool.dma_start(ybuf[bass.ds(e * cap, cap), :].rearrange("(t p) d -> p t d", p=P),
                                   yo[:, p]).then_inc(stored[p], 16)
                each(pool, body)
                for p in range(2):
                    pool.wait_ge(stored[p], n_exp // 2 * 16)


def combine(nc, g, t, title, ybuf, top, r, xr=None):
    GRP = 8
    names = [f"gathered{q}" for q in range(NT // GRP)]
    with section(nc, title, *names, "cv_in", "step") as s:
        gb = s.sb("gb", [P, top, NT, D])
        cv = s.sb("cv", [P, 2, D])
        gathered = s.sems[:NT // GRP]
        with nc.Block() as block:

            @block.sync
            def _(sp):
                if xr is not None:
                    sp.dma_start(cv[:], t["f0_const"].to_broadcast([P, 2, D])).then_inc(s.cv_in, 16)

            @block.gpsimd
            def _(pool):
                for i in range(NT):
                    for k in range(top):
                        pool.indirect_dma_start(gb[:, k, i, :], None, ybuf,
                                                bass.IndirectOffsetOnAxis(ap=r.rows_i[:, k, i:i + 1], axis=0),
                                                bounds_check=ybuf.shape[0] - 1,
                                                oob_is_err=False).then_inc(gathered[i // GRP], 16)

            @block.vector
            def _(dve):
                c = Chain(dve, s.step)
                if xr is not None:
                    dve.wait_ge(s.cv_in, 16)
                    for a, src in ((1, None), (2, cv[:, 0, :]), (3, cv[:, 1, :])):
                        for i in range(NT):
                            c.add(nc.vector.scalar_tensor_tensor(out=g.x[:, i, :],
                                                                 in0=xr[:, i, :] if src is None else src,
                                                                 scalar=r.near[:, i, a:a + 1], in1=g.x[:, i, :],
                                                                 op0=ALU.mult, op1=ALU.add))
                        c.wait()
                for q in range(NT // GRP):
                    dve.wait_ge(gathered[q], 16 * GRP * top)
                    for k in range(top):
                        for i in range(q * GRP, (q + 1) * GRP):
                            c.add(nc.vector.scalar_tensor_tensor(out=g.x[:, i, :], in0=gb[:, k, i, :],
                                                                 scalar=r.w[:, k, i:i + 1], in1=g.x[:, i, :],
                                                                 op0=ALU.mult, op1=ALU.add))
                        c.wait()


def grouped(nc, g, t, disp, ybuf, r):
    NJ = TILES1
    with section(nc, "grouped", "w_in", "x_in0", "x_in1", "turned", "xt_ready", "ab_ready", "a_ready", "h_ready",
                 "ht_turned", "ht_ready", "y_ready", "y_out", "stored0", "stored1") as s:
        w13 = s.sb("w13", [P, E1, 2 * H1])
        w2 = s.sb("w2", [P, E1, len(H1_CUTS) * D])
        xin = s.sb("xin", [P, 2, D])
        xt = s.sb("xt", [P, 2, P])
        a = s.sb("a", [P, 2, H1])
        h = s.sb("h", [P, 2, H1])
        ht = s.sb("ht", [P, 2, len(H1_CUTS), P])
        yo = s.sb("yo", [P, 2, D])
        x_in, stored = (s.x_in0, s.x_in1), (s.stored0, s.stored1)

        def each(eng, body):
            with eng.Fori(0, NJ // 2 - 1) as it:
                for p in range(2):
                    body(it * 2 + p, it, p, False)
            body(NJ - 2, NJ // 2 - 1, 0, False)
            body(NJ - 1, NJ // 2 - 1, 1, True)

        with nc.Block() as block:

            @block.sync
            def _(sp):
                sp.dma_start(w13[:], t["f1_w13"]).then_inc(s.w_in, 16)
                sp.dma_start(w2[:], t["f1_w2"]).then_inc(s.w_in, 16)

                def body(j, it, p, last):
                    sp.wait_ge(s.turned, j + 1)
                    sp.dma_start(xin[:, p, :], disp[bass.ds(j * P, P), :]).then_inc(x_in[p], 16)
                each(sp, body)

            @block.tensor
            def _(pe):
                pe.sem_inc(s.turned, 2)
                pe.wait_ge(s.w_in, 32)

                def tile_expert(j):
                    return pe.value_load(r.tile_e[0:1, bass.ds(j, 1)], min_val=0, max_val=E1 - 1)

                def transpose(j, it, p):
                    pe.wait_ge(x_in[p], (it + 1) * 16)
                    pe.wait_ge(s.y_out, j + 1)
                    nc.tensor.transpose(g.ps[:, 4 * p, 0:P], xin[:, p, :], g.ident[:]).then_inc(s.turned, 1)

                def up(j, p):
                    e = tile_expert(j)
                    pe.wait_ge(s.xt_ready, j + 1)
                    pe.wait_ge(s.h_ready, j + 1)
                    for m in range(2):
                        ins = nc.tensor.matmul(g.ps[:, 4 * p + 1 + m, 0:H1], xt[:, p, :],
                                               rows(w13[:, bass.ds(e, 1), m * H1:(m + 1) * H1]), start=True, stop=True)
                    ins.then_inc(s.ab_ready, 1)

                def body(j, it, p, last):
                    if not last:
                        transpose(j + 1, it + p, 1 - p)
                    pe.wait_ge(s.h_ready, j + 3)
                    pe.wait_ge(s.ht_ready, j + 1)
                    for c, (lo, n) in enumerate(H1_CUTS):
                        ins = nc.tensor.transpose(g.ps[0:n, 4 * p + 3, c * P:(c + 1) * P], h[:, p, lo:lo + n],
                                                  g.ident[:])
                    ins.then_inc(s.ht_turned, 1)
                    if not last:
                        up(j + 1, 1 - p)
                    e = tile_expert(j)
                    pe.wait_ge(s.ht_ready, j + 3)
                    for c, (lo, n) in enumerate(H1_CUTS):
                        ins = nc.tensor.matmul(g.ps[:, 4 * p, P:2 * P], ht[0:n, p, c, :],
                                               rows(w2[0:n, bass.ds(e, 1), c * D:(c + 1) * D]),
                                               start=(c == 0), stop=(c == len(H1_CUTS) - 1))
                    ins.then_inc(s.y_ready, 1)

                transpose(0, 0, 0)
                up(0, 0)
                each(pe, body)

            @block.scalar
            def _(act):
                nc.scalar.preload_act_table(ACT.Silu)
                act.sem_inc(s.ht_ready, 2)

                def body(j, it, p, last):
                    act.wait_ge(s.ab_ready, j + 1)
                    act.wait_ge(s.h_ready, j + 1)
                    nc.scalar.activation(a[:, p, :], g.ps[:, 4 * p + 1, 0:H1], ACT.Silu).then_inc(s.a_ready, 1)
                    act.wait_ge(s.ht_turned, j + 1)
                    act.wait_ge(s.y_out, j + 1)
                    n = H1_CUTS[-1][1]
                    nc.scalar.copy(ht[:, p, 0:2, :], g.ps[:, 4 * p + 3, 0:2 * P].rearrange("p (c t) -> p c t", c=2))
                    nc.scalar.copy(ht[0:n, p, 2, :], g.ps[0:n, 4 * p + 3, 2 * P:3 * P]).then_inc(s.ht_ready, 1)
                each(act, body)

            @block.vector
            def _(dve):
                dve.sem_inc(s.y_out, 2)
                dve.sem_inc(s.h_ready, 2)

                def take(j, p):
                    dve.wait_ge(s.turned, j + 3)
                    nc.vector.tensor_copy(xt[:, p, :], g.ps[:, 4 * p, 0:P]).then_inc(s.xt_ready, 1)

                def body(j, it, p, last):
                    if not last:
                        take(j + 1, 1 - p)
                    dve.wait_ge(s.a_ready, j + 1)
                    dve.wait_ge(s.ht_turned, j)
                    nc.vector.tensor_tensor(h[:, p, :], g.ps[:, 4 * p + 2, 0:H1], a[:, p, :],
                                            ALU.mult).then_inc(s.h_ready, 1)
                    dve.wait_ge(s.y_ready, j + 1)
                    dve.wait_ge(stored[p], it * 16)
                    nc.vector.tensor_copy(yo[:, p, :], g.ps[:, 4 * p, P:2 * P]).then_inc(s.y_out, 1)
                take(0, 0)
                each(dve, body)

            @block.gpsimd
            def _(pool):
                def body(j, it, p, last):
                    pool.wait_ge(s.y_out, j + 3)
                    pool.dma_start(ybuf[bass.ds(j * P, P), :], yo[:, p, :]).then_inc(stored[p], 16)
                each(pool, body)
                for p in range(2):
                    pool.wait_ge(stored[p], NJ // 2 * 16)


def moe0(nc, g, t):
    with ExitStack() as c:
        xr = c.enter_context(nc.sbuf_tensor("xr", [P, NT, D], F32))
        xr_t = c.enter_context(nc.sbuf_tensor("xr_t", [P, N], F32))
        r = Names()
        r.rows_i = c.enter_context(nc.sbuf_tensor("rows0", [P, 2, NT], I32))
        r.w = c.enter_context(nc.sbuf_tensor("w0", [P, 2, NT], F32))
        r.near = c.enter_context(nc.sbuf_tensor("near0", [P, NT, FIRST_MLP0], F32))
        n = (E0 - FIRST_MLP0) * CAP0
        disp = nc.dram_tensor("disp0", (n, D), F32, kind="Internal").ap()
        ybuf = nc.dram_tensor("ybuf0", (n, D), F32, kind="Internal").ap()
        normalise(nc, g, "rms0", g.xn, xr, xr_t, "rms", w_row=t["f0_norm"])
        route(nc, g, t, "route0", xr, xr_t, "f0_router", E0, 2, CAP0, FIRST_MLP0, disp, r)
        experts(nc, g, t, "mlp0", "f0_packed", E0 - FIRST_MLP0, CAP0, disp, ybuf, ACT.Gelu)
        combine(nc, g, t, "comb0", ybuf, 2, r, xr)


def moe1(nc, g, t):
    with ExitStack() as c:
        r = Names()
        r.rows_i = c.enter_context(nc.sbuf_tensor("rows1", [P, 2, NT], I32))
        r.w = c.enter_context(nc.sbuf_tensor("w1", [P, 2, NT], F32))
        r.tile_e = c.enter_context(nc.sbuf_tensor("tile_e", [1, TILES1], I32))
        disp = nc.dram_tensor("disp1", (TILES1 * P, D), F32, kind="Internal").ap()
        ybuf = nc.dram_tensor("ybuf1", (TILES1 * P, D), F32, kind="Internal").ap()
        route(nc, g, t, "route1", g.xn, g.xn_t, "f1_gate", E1, 2, None, 0, disp, r)
        grouped(nc, g, t, disp, ybuf, r)
        combine(nc, g, t, "comb1", ybuf, 2, r)


def moe3(nc, g, t):
    with ExitStack() as c:
        r = Names()
        r.rows_i = c.enter_context(nc.sbuf_tensor("rows3", [P, 1, NT], I32))
        r.w = c.enter_context(nc.sbuf_tensor("w3", [P, 1, NT], F32))
        disp = nc.dram_tensor("disp3", (E3 * CAP3, D), F32, kind="Internal").ap()
        ybuf = nc.dram_tensor("ybuf3", (E3 * CAP3, D), F32, kind="Internal").ap()
        route(nc, g, t, "route3", g.xn, g.xn_t, "f3_gate", E3, 1, CAP3, 0, disp, r)
        experts(nc, g, t, "mlp3", "f3_packed", E3, CAP3, disp, ybuf, ACT.Relu)
        combine(nc, g, t, "comb3", ybuf, 1, r)


N_PAIRS = 6


def project_parts(nc, g, t, title, wq, bq, wk, bk, q_parts, k_parts, lora=None):
    CH = 512
    NCH = N // CH
    with section(nc, title, "w_in", "mm_ready", "step", "act_step", "stored0", "stored1") as s:
        w = s.sb("w", [P, 2, D])
        b = s.sb("b", [P, 2])
        y = s.sb("y", [P, 2, CH])
        r1 = s.sb("r1", [P, 2, CH])
        parts = s.sb("parts", [P, 2, 3, CH], BF16)
        stored = (s.stored0, s.stored1)
        with nc.Block() as block:

            @block.sync
            def _(sp):
                for i, (wn, bn) in enumerate(((wq, bq), (wk, bk))):
                    sp.dma_start(w[:, i, :], wn).then_inc(s.w_in, 16)
                    sp.dma_start(b[:, i:i + 1], bn).then_inc(s.w_in, 16)
                with sp.Fori(0, NCH) as ch:
                    for m, out in ((0, q_parts), (1, k_parts)):
                        at, made = sp.snap(ch * CH), sp.snap(ch * 6 + m * 3 + 3)
                        sp.wait_ge(s.step, made)
                        sp.dma_start(out[:, :, bass.ds(at, CH)].rearrange("a r t -> r a t"),
                                     parts[:, m]).then_inc(stored[m], 16)
                for m in range(2):
                    sp.wait_ge(stored[m], NCH * 16)

            @block.tensor
            def _(pe):
                pe.wait_ge(s.w_in, 64)
                with pe.Fori(0, NCH) as ch:
                    for m in range(2):
                        pe.wait_ge(s.step, ch * 6 + m * 3)
                        nc.tensor.matmul(g.ps[:, m, :], w[:, m, :], g.xn_t[:, bass.ds(ch * CH, CH)], start=True,
                                         stop=True).then_inc(s.mm_ready, 1)

            @block.vector
            def _(dve):
                dve.wait_ge(s.w_in, 64)
                with dve.Fori(0, NCH) as ch:
                    for m in range(2):
                        c = Chain(dve, s.step, ch * 6 + m * 3)
                        dve.wait_ge(s.mm_ready, ch * 2 + m + 1)
                        dve.wait_ge(s.act_step, ch * 4 + m * 2)
                        dve.wait_ge(stored[m], ch * 16)
                        c.step(nc.vector.tensor_scalar(y[:, m, :], g.ps[:, m, :], b[:, m:m + 1], None, ALU.add))
                        dve.wait_ge(s.act_step, ch * 4 + m * 2 + 1)
                        c.step(nc.vector.tensor_tensor(r1[:, m, :], y[:, m, :], parts[:, m, 0, :], ALU.subtract))
                        dve.wait_ge(s.act_step, ch * 4 + m * 2 + 2)
                        c.step(nc.vector.tensor_tensor(parts[:, m, 2, :], r1[:, m, :], parts[:, m, 1, :],
                                                       ALU.subtract))

            @block.scalar
            def _(act):
                with act.Fori(0, NCH) as ch:
                    for m in range(2):
                        c = Chain(act, s.act_step, ch * 4 + m * 2)
                        act.wait_ge(stored[m], ch * 16)
                        act.wait_ge(s.step, ch * 6 + m * 3 + 1)
                        c.add(nc.scalar.copy(parts[:, m, 0, :], y[:, m, :]))
                        act.wait_ge(s.step, ch * 6 + m * 3 + 2)
                        c.add(nc.scalar.copy(parts[:, m, 1, :], r1[:, m, :]))


def attention(nc, g, title, wv, bv, wo, bo, q_parts, k_parts, causal, scale, pool_job=None):
    NB = 3 if causal else 4
    KR = N_PAIRS * HD
    HP = HEADS // 2
    with section(nc, title, "w_in", "vx_one", "qk_in0", "qk_in1", "xb_ready", "v_ready", "vx_ready", "m_ready",
                 "m_taken", "m_step", "nm_ready", "turned_nm", "nmt_ready", "s_ready", "p_ready", "o_step",
                 "ot_ready", "otc_ready", "out_ready", "out_done", "pv_done") as s:
        wv_s = s.sb("wv", [P, D])
        wo_s = s.sb("wo", [P, D])
        bv_s = s.sb("bv", [1, D])
        bo_s = s.sb("bo", [1, D])
        qs = s.sb("qs", [KR, 2, HEADS, T], BF16)
        ks = s.sb("ks", [KR, 2, HEADS, T], BF16)
        xb = s.sb("xb", [P, T])
        vx = s.sb("vx", [P, 2, QT, HEADS, HD + 1])
        mb = s.sb("mb", [P, HEADS, 3 if causal else 2])
        m = s.sb("m", [P, QT, HEADS])
        m2 = s.sb("m2", [P, QT, 2, HEADS], BF16)
        mt = s.sb("mt", [2 * HEADS, 2, T], BF16)
        pr = s.sb("pr", [P, 2, 2, NB * P])
        rc = s.sb("rc", [P, QT, HEADS])
        o = s.sb("o", [P, QT, HEADS, HD])
        ot = s.sb("ot", [P, QT, P])
        qk_in = (s.qk_in0, s.qk_in1)
        QK_IN = 9 * 16
        HALF = BATCH // 2

        def each(eng, stage):
            stage(-1, 0, 1, False, True, False)
            stage(0, 0, 0, True, True, False)
            stage(1, 1, 1, True, True, True)
            with eng.Fori(1, HALF - 1) as it:
                for p in range(2):
                    stage(it * 2 + p, it + p, p, True, True, True)
            stage(BATCH - 2, HALF - 1, 0, True, True, True)
            stage(BATCH - 1, 0, 1, True, False, True)
            stage(BATCH, 0, 0, False, False, True)

        O = g.ps[:, 6, 0:QT * HEADS * (HD + 1)].rearrange("p (q h d) -> p q h d", q=QT, h=HEADS)

        with nc.Block() as block:

            @block.sync
            def _(sp):
                for dst, src in ((wv_s, wv), (wo_s, wo), (bv_s, bv), (bo_s, bo)):
                    sp.dma_start(dst[:], src).then_inc(s.w_in, 16)

                def load(at, p):
                    tok = bass.ds(at, T)
                    for row, part, n in ((0, 0, 3), (3, 0, 2), (5, 0, 1)):
                        sp.dma_start(qs[row * HD:(row + n) * HD, p], q_parts[part:part + n, :, tok].rearrange(
                            "a (d h) t -> (a d) h t", h=HEADS)).then_inc(qk_in[p], 16)
                    for row, part, n in ((0, 0, 3), (3, 1, 2), (5, 2, 1)):
                        for i in range(n):
                            sp.dma_start(ks[(row + i) * HD:(row + i + 1) * HD, p],
                                         k_parts[part, :, tok].rearrange("(d h) t -> d h t", h=HEADS)
                                         ).then_inc(qk_in[p], 16)

                load(0, 0)
                load(T, 1)
                with sp.Fori(0, HALF - 1) as it:
                    for p in range(2):
                        at = sp.snap((it * 2 + p + 2) * T)
                        sp.wait_ge(s.s_ready, (it * 2 + p + 1) * HP)
                        load(at, p)

            @block.gpsimd
            def _(pool):
                nc.gpsimd.memset(vx[:], 1.0).then_inc(s.vx_one, 1)
                if pool_job:
                    pool.wait_ge(s.vx_one, 1)
                    pool_job(pool)

            @block.tensor
            def _(pe):
                pe.wait_ge(s.w_in, 64)

                def maximum(nb, p, h):
                    pe.wait_ge(s.m_taken, nb * HEADS + h + 1)
                    bank = h % 2
                    if causal:
                        runs = ((0, 0, P), (1, P, 3 * P))
                    else:
                        runs = ((0, 0, T), (1, T, 2 * T))
                    for q, lo, hi in runs:
                        ins = nc.tensor.matmul(g.ps[:, bank, lo:hi], qs[:, p, h, q * P:(q + 1) * P],
                                               ks[:, p, h, 0:hi - lo], start=True, stop=not causal)
                        if causal:
                            ins = nc.tensor.matmul(g.ps[:, bank, hi - P:hi], g.ident_b[:], g.future_q[:],
                                                   start=False, stop=True)
                    ins.then_inc(s.m_ready, 1)

                def scores(b, p, j):
                    pe.wait_ge(s.p_ready, b * HP + j + 1)
                    for i in range(2):
                        h, bank = 2 * j + i, 2 + 2 * (j % 2) + i
                        for k in range(QT):
                            q0 = k * P if causal else 0
                            out = g.ps[:, bank, k * T:k * T + T - q0]
                            nc.tensor.matmul(out, ks[:, p, h, k * P:(k + 1) * P], qs[:, p, h, q0:T],
                                             start=True, stop=False)
                            ins = nc.tensor.matmul(out, g.head_sel[:, h, :], mt[:, p, q0:T], start=False,
                                                   stop=not causal)
                            if causal:
                                ins = nc.tensor.matmul(g.ps[:, bank, k * T:k * T + P], g.ident_b[:],
                                                       g.after_neg[:], start=False, stop=True)
                    ins.then_inc(s.s_ready, 1)

                def values(b, p, j):
                    pe.wait_ge(s.p_ready, b * HP + j + 3)
                    for i in range(2):
                        h = 2 * j + i
                        for q in range(QT):
                            keys = range(q + 1) if causal else range(QT)
                            for k in keys:
                                at = k * T + (q - (k if causal else 0)) * P
                                ins = nc.tensor.matmul(O[:, q, h, :], pr[:, j % 2, i, at:at + P],
                                                       vx[:, p, k, h, :], start=(k == 0), stop=(k == keys[-1]))
                    ins.then_inc(s.pv_done, 1)

                def with_ones(out, lhs_t, rhs, bias):
                    nc.tensor.matmul(out, lhs_t, rhs, start=True, stop=False)
                    return nc.tensor.matmul(out, g.ones_row[:], bias, start=False, stop=True)

                def stage(b, loads, p, now, ahead, prev):
                    nb, np_ = b + 1, 1 - p
                    if ahead:
                        pe.wait_ge(qk_in[np_], (loads + 1) * QK_IN)
                        pe.wait_ge(s.xb_ready, nb + 1)
                        pe.wait_ge(s.nmt_ready, nb)
                        for k in range(QT):
                            ins = with_ones(g.ps[:, 7, k * D:(k + 1) * D], xb[:, k * P:(k + 1) * P], wv_s[:], bv_s[:])
                        ins.then_inc(s.v_ready, 1)
                    elif now:
                        pe.wait_ge(s.nmt_ready, nb)
                    for j in range(HP):
                        if ahead:
                            maximum(nb, np_, 2 * j)
                            maximum(nb, np_, 2 * j + 1)
                        if now:
                            scores(b, p, j)
                        if prev and j == 1:
                            pe.wait_ge(s.o_step, b * 2)
                            if ahead:
                                pe.wait_ge(s.vx_ready, nb + 1)
                            for q in range(QT):
                                ins = nc.tensor.transpose(g.ps[:, 7, q * P:(q + 1) * P],
                                                          o[:, q].rearrange("p h d -> p (h d)"), g.ident[:])
                            ins.then_inc(s.ot_ready, 1)
                        if now and j > 0:
                            values(b, p, j - 1)
                        if prev and j == 2:
                            pe.wait_ge(s.otc_ready, b)
                            for q in range(QT):
                                ins = with_ones(g.ps[:, 7, q * D:(q + 1) * D], ot[:, q, :], wo_s[:], bo_s[:])
                            ins.then_inc(s.out_ready, 1)
                    if now:
                        values(b, p, HP - 1)
                    if ahead:
                        pe.wait_ge(s.nm_ready, nb + 1)
                        if prev:
                            pe.wait_ge(s.out_done, b)
                        for q in range(QT):
                            ins = nc.tensor.matmul(g.ps[0:2 * HEADS, 7, q * P:(q + 1) * P],
                                                   m2[:, q].rearrange("p a h -> p (a h)"), g.ident_b[:],
                                                   start=True, stop=True)
                        ins.then_inc(s.turned_nm, 1)
                each(pe, stage)

            @block.scalar
            def _(act):
                nc.scalar.preload_act_table(ACT.Exp)
                act.sem_inc(s.p_ready, 2)
                nc.scalar.copy(xb[:], g.xn_t[:, 0:T]).then_inc(s.xb_ready, 1)

                def stage(b, loads, p, now, ahead, prev):
                    nb, np_ = b + 1, 1 - p
                    for j in range(HP):
                        if now:
                            act.wait_ge(s.s_ready, b * HP + j + 1)
                            act.wait_ge(s.pv_done, b * HP + j - 1 if j else b * HP)
                            nc.scalar.activation(pr[:, j % 2], g.ps[:, 2 + 2 * (j % 2):4 + 2 * (j % 2), 0:NB * P],
                                                 ACT.Exp, scale=scale).then_inc(s.p_ready, 1)
                        if prev and j == 1:
                            act.wait_ge(s.ot_ready, b)
                            nc.scalar.copy(ot[:], g.ps[:, 7, 0:T].rearrange("p (q t) -> p q t", q=QT)
                                           ).then_inc(s.otc_ready, 1)
                        if ahead and j == 3:
                            act.wait_ge(s.v_ready, nb + 1)
                            nxt = min(nb + 1, BATCH - 1) if isinstance(nb, int) else nb + 1
                            nc.scalar.copy(xb[:], g.xn_t[:, bass.ds(nxt * T, T)]).then_inc(s.xb_ready, 1)
                    if ahead:
                        act.wait_ge(s.turned_nm, nb + 1)
                        nc.scalar.copy(mt[:, np_, :], g.ps[0:2 * HEADS, 7, 0:T]).then_inc(s.nmt_ready, 1)
                each(act, stage)

            @block.vector
            def _(dve):
                v = nc.vector
                dve.sem_inc(s.m_taken, 2)
                dve.wait_ge(s.vx_one, 1)

                def stage(b, loads, p, now, ahead, prev):
                    nb, np_ = b + 1, 1 - p
                    if prev:
                        dve.wait_ge(s.pv_done, b * HP)
                        v.reciprocal(rc[:], O[:, :, :, HD]).then_inc(s.o_step, 1)
                        dve.wait_ge(s.o_step, b * 2 - 1)
                        v.tensor_tensor(o[:], O[:, :, :, 0:HD],
                                        rc[:, :, :, None].to_broadcast([P, QT, HEADS, HD]),
                                        ALU.mult).then_inc(s.o_step, 1)
                    if ahead:
                        dve.wait_ge(s.v_ready, nb + 1)
                        v.tensor_copy(vx[:, np_, :, :, 0:HD],
                                      g.ps[:, 7, 0:QT * D].rearrange("p (k h d) -> p k h d", k=QT, h=HEADS)
                                      ).then_inc(s.vx_ready, 1)
                    for h in range(HEADS):
                        if ahead:
                            dve.wait_ge(s.m_ready, nb * HEADS + h + 1)
                            w = P if causal else T
                            v.tensor_reduce(mb[:, h, :], g.ps[:, h % 2, 0:NB * P].rearrange("p (n k) -> p n k", k=w),
                                            AX_X, ALU.max).then_inc(s.m_taken, 1)
                        if prev and h == 7:
                            dve.wait_ge(s.out_ready, b)
                            xs = g.x[:, bass.ds((b - 1) * QT, QT), :]
                            v.tensor_tensor(xs, xs, g.ps[:, 7, 0:QT * D].rearrange("p (k d) -> p k d", k=QT),
                                            ALU.add).then_inc(s.out_done, 1)
                    if ahead:
                        dve.wait_ge(s.m_taken, (nb + 1) * HEADS + 2)
                        top = mb[:].rearrange("p h q -> p q h")
                        c = Chain(dve, s.m_step, nb * (3 if causal else 1))
                        if causal:
                            c.add(v.tensor_copy(m[:, 0, :], mb[:, :, 0]))
                            c.step(v.tensor_tensor(m[:, 1, :], mb[:, :, 1], mb[:, :, 2], ALU.max))
                            top = m[:]
                        c.step(v.tensor_copy(m2[:, :, 0, :], top))
                        v.tensor_tensor(m2[:, :, 1, :], top, m2[:, :, 0, :], ALU.subtract).then_inc(s.nm_ready, 1)
                each(dve, stage)


def attn1(nc, g, t):
    qp = nc.dram_tensor("q1_parts", (3, D, N), BF16, kind="Internal").ap()
    kp = nc.dram_tensor("k1_parts", (3, D, N), BF16, kind="Internal").ap()
    project_parts(nc, g, t, "qk1", t["a1_wq"], t["a1_bq"], t["a1_wk"], t["a1_bk"], qp, kp)
    attention(nc, g, "att1", t["a1_wv"], t["a1_bv"], t["a1_wo"], t["a1_bo"], qp, kp, True, HD ** -0.5)


def lora_mix(nc, g, t, m, which, wt, b, out_w, out_b):
    LORA_SCALE = 2.0
    with section(nc, "lora_" + which, "in_done", "mm_done", "mixed", "taken") as s:
        a = s.sb("a", [P, 2, P])
        bb = s.sb("b", [P, 2, P])
        eye = s.sb("eye", [P, P])
        mix = s.sb("mix", [P, P])
        w = s.sb("w", [P, P])
        bi = s.sb("bi", [P, 1])
        with nc.Block() as block:

            @block.sync
            def _(sp):
                for dst, src in ((a, t[m + "_a"]), (bb, t[m + "_b"]), (eye, t[m + "_eye"]), (w, wt), (bi, b)):
                    sp.dma_start(dst[:], src).then_inc(s.in_done, 16)

            @block.tensor
            def _(pe):
                pe.wait_ge(s.in_done, 80)
                for c in range(2):
                    ins = nc.tensor.matmul(g.ps[:, 0, 0:P], a[:, c, :], bb[:, c, :], start=(c == 0), stop=(c == 1))
                ins.then_inc(s.mm_done, 1)
                pe.wait_ge(s.mixed, 1)
                nc.tensor.matmul(g.ps[:, 1, 0:P], w[:], mix[:], start=True, stop=True)
                if which == "q":
                    ins = nc.tensor.matmul(g.ps[:, 2, 0:1], mix[:], bi[:], start=True, stop=True)
                else:
                    ins = nc.tensor.matmul(g.ps[0:1, 2, 0:P], bi[:], mix[:], start=True, stop=True)
                ins.then_inc(s.mm_done, 1)

            @block.vector
            def _(dve):
                dve.wait_ge(s.mm_done, 1)
                nc.vector.scalar_tensor_tensor(out=mix[:], in0=g.ps[:, 0, 0:P], scalar=LORA_SCALE, in1=eye[:],
                                               op0=ALU.mult, op1=ALU.add).then_inc(s.mixed, 1)
                dve.wait_ge(s.mm_done, 2)
                nc.vector.tensor_copy(out_w, g.ps[:, 1, 0:P]).then_inc(s.taken, 1)
                nc.vector.tensor_copy(out_b, g.ps[:, 2, 0:1] if which == "q" else g.ps[0:1, 2, 0:P]
                                      ).then_inc(s.taken, 1)
                dve.wait_ge(s.taken, 2)


def attn2(nc, g, t):
    qp = nc.dram_tensor("q2_parts", (3, D, N), BF16, kind="Internal").ap()
    kp = nc.dram_tensor("k2_parts", (3, D, N), BF16, kind="Internal").ap()
    with ExitStack() as c:
        wq = c.enter_context(nc.sbuf_tensor("wq2", [P, D], F32))
        wv = c.enter_context(nc.sbuf_tensor("wv2", [P, D], F32))
        bq = c.enter_context(nc.sbuf_tensor("bq2", [P, 1], F32))
        bv = c.enter_context(nc.sbuf_tensor("bv2", [1, D], F32))
        lora_mix(nc, g, t, "lq", "q", t["a2_wq_t"], t["a2_bq"], wq[:], bq[:])
        lora_mix(nc, g, t, "lv", "v", t["a2_wv_t"], t["a2_bv"], wv[:], bv[:])
        project_parts(nc, g, t, "qk2", wq[:], bq[:], t["a2_wk"], t["a2_bk"], qp, kp)
        attention(nc, g, "att2", wv[:], bv[:], t["a2_wo"], t["a2_bo"], qp, kp, False, HD ** -0.5)


def ffn2(nc, g, t):
    MB, RUN, H = 2, N // 2 // E2, FC
    C = MB * RUN
    W2, B1, B2, WN = FC * P, 2 * FC * P, 2 * FC * P + FC, 2 * FC * P + FC + 1
    with ExitStack() as ctx:
        x2 = ctx.enter_context(nc.sbuf_tensor("x2", [P, NT, D], F32))
        x2_t = ctx.enter_context(nc.sbuf_tensor("x2_t", [P, N], F32))
        normalise(nc, g, "ln2", g.xn, x2, x2_t, "ln", t["f2_g"], t["f2_b"])
        with section(nc, "mlp2", "c_in", "w_in0", "w_in1", "a_ready", "xa_ready", "h_ready", "act_done", "y_ready",
                     "yt_ready", "z_ready", "z_done", "x_done") as s:
            aw = s.sb("aw", [P, D])
            nw = s.sb("nw", [P, D])
            ab = s.sb("ab", [P, 1])
            nb = s.sb("nb", [1, D])
            w = s.sb("w", [P, 2, WN])
            xa = s.sb("xa", [P, 2, C])
            ht = s.sb("ht", [P, FC, C])
            yt = s.sb("yt", [P, C])
            z = s.sb("z", [P, MB, RUN // P, D])
            w_in = (s.w_in0, s.w_in1)

            def run_of(ap, e):
                return ap.rearrange("p (m t) -> p m t", m=MB)[:, :, bass.ds(e * RUN, RUN)]

            def each(eng, body):
                with eng.Fori(0, E2 // 2 - 1) as it:
                    for p in range(2):
                        body(it * 2 + p, it, p, False)
                body(E2 - 2, E2 // 2 - 1, 0, False)
                body(E2 - 1, E2 // 2 - 1, 1, True)

            with nc.Block() as block:

                @block.sync
                def _(sp):
                    for dst, src in ((aw, "f2_aw"), (nw, "f2_nw"), (ab, "f2_ab"), (nb, "f2_nb")):
                        sp.dma_start(dst[:], t[src]).then_inc(s.c_in, 16)

                    def body(e, it, p, last):
                        sp.wait_ge(s.yt_ready, e + 1)
                        sp.dma_start(w[:, p], t["f2_packed"][bass.ds(e, 1)].rearrange("a p n -> (a p) n")
                                     ).then_inc(w_in[p], 16)
                    each(sp, body)

                @block.tensor
                def _(pe):
                    pe.wait_ge(s.c_in, 64)

                    def attend(e):
                        pe.wait_ge(s.xa_ready, e)
                        nc.tensor.matmul(g.ps[:, 0, 0:C].rearrange("p (m t) -> p m t", m=MB), aw[:],
                                         run_of(x2_t[:], e), start=True, stop=True).then_inc(s.a_ready, 1)

                    def body(e, it, p, last):
                        pe.wait_ge(w_in[p], (it + 1) * 16)
                        pe.wait_ge(s.xa_ready, e + 1)
                        pe.wait_ge(s.act_done, e * H)
                        for f in range(FC):
                            nc.tensor.matmul(g.ps[:, 1 + f, 0:C], w[:, p, f * P:(f + 1) * P], xa[:, p, :],
                                             start=True, stop=True).then_inc(s.h_ready, 1)
                        if not last:
                            attend(e + 1)
                        pe.wait_ge(s.yt_ready, e + 2)
                        for f in range(FC):
                            pe.wait_ge(s.act_done, e * H + f + 1)
                            ins = nc.tensor.matmul(g.ps[:, 5, 0:C], w[:, p, W2 + f * P:W2 + (f + 1) * P], ht[:, f, :],
                                                   start=(f == 0), stop=(f == FC - 1))
                        ins.then_inc(s.y_ready, 1)
                        pe.wait_ge(s.yt_ready, e + 3)
                        pe.wait_ge(s.z_done, e)
                        for k in range(C // P):
                            out = g.ps[:, 6, k * D:(k + 1) * D]
                            nc.tensor.matmul(out, yt[:, k * P:(k + 1) * P], nw[:], start=True, stop=False)
                            ins = nc.tensor.matmul(out, g.ones_row[:], nb[:], start=False, stop=True)
                        ins.then_inc(s.z_ready, 1)
                    attend(0)
                    each(pe, body)

                @block.scalar
                def _(act):
                    nc.scalar.preload_act_table(ACT.Gelu)

                    def body(e, it, p, last):
                        act.wait_ge(s.y_ready, e)
                        for f in range(FC):
                            act.wait_ge(s.h_ready, e * H + f + 1)
                            nc.scalar.activation(ht[:, f, :], g.ps[:, 1 + f, 0:C], ACT.Gelu,
                                                 bias=w[:, p, B1 + f:B1 + f + 1]).then_inc(s.act_done, 1)
                        act.wait_ge(s.z_ready, e + 1)
                        act.wait_ge(s.x_done, e)
                        nc.scalar.activation(z[:].rearrange("p m k d -> p (m k d)"), g.ps[:, 6, 0:C],
                                             ACT.Gelu).then_inc(s.z_done, 1)
                    each(act, body)

                @block.vector
                def _(dve):
                    dve.wait_ge(s.c_in, 64)
                    dve.sem_inc(s.yt_ready, 2)

                    def take(e, p):
                        dve.wait_ge(s.a_ready, e + 1)
                        nc.vector.scalar_tensor_tensor(
                            out=xa[:, p].rearrange("p (m t) -> p m t", m=MB),
                            in0=g.ps[:, 0, 0:C].rearrange("p (m t) -> p m t", m=MB), scalar=ab[:],
                            in1=run_of(g.xn_t[:], e), op0=ALU.add, op1=ALU.add).then_inc(s.xa_ready, 1)

                    def body(e, it, p, last):
                        if not last:
                            take(e + 1, 1 - p)
                        dve.wait_ge(s.y_ready, e + 1)
                        dve.wait_ge(s.z_ready, e)
                        nc.vector.tensor_scalar(yt[:], g.ps[:, 5, 0:C], w[:, p, B2:B2 + 1], None,
                                                ALU.add).then_inc(s.yt_ready, 1)
                        dve.wait_ge(s.z_done, e + 1)
                        xs = g.x[:].rearrange("p (m t) d -> p m (t d)", m=MB)[:, :, bass.ds(e * RUN, RUN)]
                        nc.vector.tensor_tensor(xs, xs, z[:].rearrange("p m k d -> p m (k d)"),
                                                ALU.add).then_inc(s.x_done, 1)
                    take(0, 0)
                    each(dve, body)


def attn3(nc, g, t):
    EC = EG // P
    with ExitStack() as ctx:
        x3 = ctx.enter_context(nc.sbuf_tensor("x3", [P, NT, D], F32))
        x3_t = ctx.enter_context(nc.sbuf_tensor("x3_t", [P, N], F32))
        normalise(nc, g, "ln3", g.xn, x3, x3_t, "ln", t["a3_g"], t["a3_b"])
        with section(nc, "gau", "w_in", "xb_ready", "p_ready", "act_done", "qk_ready", "s_ready", "relu_done",
                     "a_ready", "o_ready", "g_ready", "f_ready", "x_step") as s:
            w = s.sb("w", [P, 2 * EG + D])
            bu = s.sb("bu", [P, EC])
            bz = s.sb("bz", [P, 1])
            bv = s.sb("bv", [1, EG])
            qk = s.sb("qk", [P, 4])
            wo = s.sb("wo", [P, EC, D])
            bo = s.sb("bo", [1, D])
            xb = s.sb("xb", [P, T])
            ut = s.sb("ut", [P, 2, EC, T])
            v = s.sb("v", [P, 2, QT, EG])
            zt = s.sb("zt", [P, T])
            q = s.sb("q", [P, 2, T])
            k = s.sb("k", [P, 2, T])
            rl = s.sb("rl", [P, QT, T])
            at = s.sb("at", [P, QT, T])
            gt = s.sb("gt", [P, EC, T])

            def each(eng, stage):
                stage(0, 1, False, True)
                with eng.Fori(0, BATCH // 2 - 1) as it:
                    for p in range(2):
                        stage(it * 2 + p, p, True, True)
                stage(BATCH - 2, 0, True, True)
                stage(BATCH - 1, 1, True, False)

            with nc.Block() as block:

                @block.sync
                def _(sp):
                    for dst, src in ((w, "a3_w"), (bu, "a3_bu"), (bz, "a3_bz"), (bv, "a3_bv"), (qk, "a3_qk"),
                                     (wo, "a3_wo"), (bo, "a3_bo")):
                        sp.dma_start(dst[:], t[src]).then_inc(s.w_in, 16)

                @block.gpsimd
                def _(pool):
                    def stage(b, p, now, ahead):
                        if ahead:
                            nb = b + 1 if now else b
                            pool.wait_ge(s.p_ready, nb)
                            nc.gpsimd.tensor_copy(xb[:], x3_t[:, bass.ds(nb * T, T)]).then_inc(s.xb_ready, 1)
                    each(pool, stage)

                @block.tensor
                def _(pe):
                    pe.wait_ge(s.w_in, 112)

                    def stage(b, p, now, ahead):
                        nb, np_ = (b + 1, 1 - p) if now else (b, 0)
                        if now:
                            pe.wait_ge(s.qk_ready, b + 1)
                            pe.wait_ge(s.relu_done, b)
                            for kt in range(QT):
                                ins = nc.tensor.matmul(g.ps[:, 3, kt * T:(kt + 1) * T], k[:, p, kt * P:(kt + 1) * P],
                                                       q[:, p, :], start=True, stop=True)
                            ins.then_inc(s.s_ready, 1)
                        if ahead:
                            pe.wait_ge(s.xb_ready, nb + 1)
                            pe.wait_ge(s.act_done, nb)
                            for c in range(EC):
                                nc.tensor.matmul(g.ps[:, 0, c * T:(c + 1) * T], w[:, c * P:(c + 1) * P], xb[:],
                                                 start=True, stop=True)
                            nc.tensor.matmul(g.ps[:, 1, 0:T], w[:, 2 * EG:2 * EG + D], xb[:], start=True, stop=True)
                            for kt in range(QT):
                                out = g.ps[:, 2, kt * EG:(kt + 1) * EG]
                                nc.tensor.matmul(out, xb[:, kt * P:(kt + 1) * P], w[:, EG:2 * EG], start=True,
                                                 stop=False)
                                ins = nc.tensor.matmul(out, g.ones_row[:], bv[:], start=False, stop=True)
                            ins.then_inc(s.p_ready, 1)
                        if now:
                            pe.wait_ge(s.a_ready, b + 1)
                            pe.wait_ge(s.g_ready, b)
                            for c in range(EC):
                                for kt in range(QT):
                                    ins = nc.tensor.matmul(g.ps[:, 4, c * T:(c + 1) * T],
                                                           v[:, p, kt, c * P:(c + 1) * P], at[:, kt, :],
                                                           start=(kt == 0), stop=(kt == QT - 1))
                            ins.then_inc(s.o_ready, 1)
                            pe.wait_ge(s.g_ready, b + 1)
                            pe.wait_ge(s.x_step, b * 2)
                            for qt in range(QT):
                                out = g.ps[:, 5, qt * D:(qt + 1) * D]
                                for c in range(EC):
                                    nc.tensor.matmul(out, gt[:, c, qt * P:(qt + 1) * P], wo[:, c, :], start=(c == 0),
                                                     stop=False)
                                ins = nc.tensor.matmul(out, g.ones_row[:], bo[:], start=False, stop=True)
                            ins.then_inc(s.f_ready, 1)
                    each(pe, stage)

                @block.scalar
                def _(act):
                    act.wait_ge(s.w_in, 112)
                    nc.scalar.preload_act_table(ACT.Silu)

                    def stage(b, p, now, ahead):
                        if ahead:
                            nb, np_ = (b + 1, 1 - p) if now else (b, 0)
                            act.wait_ge(s.p_ready, nb + 1)
                            act.wait_ge(s.qk_ready, nb)
                            if now:
                                act.wait_ge(s.g_ready, b)
                            nc.scalar.activation(zt[:], g.ps[:, 1, 0:T], ACT.Silu, bias=bz[:])
                            for c in range(EC):
                                nc.scalar.activation(ut[:, np_, c, :], g.ps[:, 0, c * T:(c + 1) * T], ACT.Silu,
                                                     bias=bu[:, c:c + 1])
                            nc.scalar.activation(v[:, np_].rearrange("p k e -> p (k e)"), g.ps[:, 2, :],
                                                 ACT.Silu).then_inc(s.act_done, 1)
                    each(act, stage)

                @block.vector
                def _(dve):
                    dve.wait_ge(s.w_in, 112)
                    vv = nc.vector

                    def stage(b, p, now, ahead):
                        nb, np_ = (b + 1, 1 - p) if now else (b, 0)
                        if now:
                            dve.wait_ge(s.s_ready, b + 1)
                            vv.tensor_scalar(rl[:].rearrange("p k t -> p (k t)"), g.ps[:, 3, :], 1.0 / T, 0.0,
                                             ALU.mult, ALU.max).then_inc(s.relu_done, 1)
                            dve.wait_ge(s.relu_done, b + 1)
                            dve.wait_ge(s.o_ready, b)
                            vv.tensor_tensor(at[:], rl[:], rl[:], ALU.mult).then_inc(s.a_ready, 1)
                        if ahead:
                            dve.wait_ge(s.act_done, nb + 1)
                            vv.tensor_scalar(q[:, np_, :], zt[:], qk[:, 0:1], qk[:, 1:2], ALU.mult, ALU.add)
                            vv.tensor_scalar(k[:, np_, :], zt[:], qk[:, 2:3], qk[:, 3:4], ALU.mult,
                                             ALU.add).then_inc(s.qk_ready, 1)
                        if now:
                            dve.wait_ge(s.o_ready, b + 1)
                            dve.wait_ge(s.f_ready, b)
                            vv.tensor_tensor(gt[:].rearrange("p c t -> p (c t)"), g.ps[:, 4, :],
                                             ut[:, p].rearrange("p c t -> p (c t)"), ALU.mult).then_inc(s.g_ready, 1)
                            dve.wait_ge(s.f_ready, b + 1)
                            xs = g.x[:, bass.ds(b * QT, QT), :]
                            vv.tensor_tensor(xs, xs, g.ps[:, 5, 0:QT * D].rearrange("p (k d) -> p k d", k=QT),
                                             ALU.add).then_inc(s.x_step, 1)
                            dve.wait_ge(s.x_step, b * 2 + 1)
                            vv.tensor_tensor(xs, xs, g.xn[:, bass.ds(b * QT, QT), :], ALU.add).then_inc(s.x_step, 1)
                    each(dve, stage)


def mamba(nc, g, t):
    with ExitStack() as c:
        u = c.enter_context(nc.sbuf_tensor("u", [P, DC, N], F32))
        gate = c.enter_context(nc.sbuf_tensor("gate", [P, DC, N], F32))
        mamba_in(nc, g, t, u, gate)
        mamba_scan(nc, g, t, u, gate)


def store(nc, g, out):
    with section(nc, "store", "stored") as s, nc.Block() as block:

        @block.sync
        def _(sp):
            sp.dma_start(out.rearrange("(t p) d -> p t d", p=P), g.x[:]).then_inc(s.stored, 16)
            sp.wait_ge(s.stored, 16)


def program(nc, t, out, parts=None):
    with ExitStack() as ctx:
        def sb(name, shape, dt=F32):
            return ctx.enter_context(nc.sbuf_tensor(name, shape, dt))

        g = Names()
        g.ps = ctx.enter_context(nc.psum_tensor("banks", [P, 8, 512], F32))
        g.x = sb("x_tok", [P, NT, D])
        g.xn = sb("xn_tok", [P, NT, D])
        g.xn_t = sb("xn_t", [P, N])
        g.ident = sb("ident", [P, P])
        g.ident_b = sb("ident_b", [P, P], BF16)
        g.ones_b = sb("ones_b", [P, P], BF16)
        g.before = sb("before", [P, P], BF16)
        g.after_neg = sb("after_neg", [P, P], BF16)
        g.future_q = sb("future_q", [P, P], BF16)
        g.head_sel = sb("head_sel", [2 * HEADS, HEADS, P], BF16)
        g.ones_row = sb("ones_row", [1, P])
        g.zeros = sb("zeros", [P, 512])
        setup(nc, g, t)
        for layer, blocks in enumerate(((mamba, moe0), (attn1, moe1), (attn2, ffn2), (attn3, moe3))):
            wanted = [f for f, kind in zip(blocks, "af") if parts is None or f"{layer}{kind}" in parts]
            if wanted:
                normalise(nc, g, f"norm{layer}", g.x, g.xn, g.xn_t, "ln")
            for f in wanted:
                f(nc, g, t)
        store(nc, g, out)


def layouts(i):
    import numpy as np

    def c(a):
        return np.ascontiguousarray(a)

    def cols(a):
        return c(np.asarray(a).reshape(-1, P).T)

    o = {"x": c(np.asarray(i["L0_attn_inputs"]).reshape(N, D))}
    w_x = np.asarray(i["L0_attn_W_x"])
    o["m_w_in"] = c(i["L0_attn_W_in"])
    o["m_taps"] = c(np.asarray(i["L0_attn_K_conv"])[:, 0, :].reshape(TAPS, DC, P).transpose(2, 1, 0))
    o["m_b_conv"] = cols(i["L0_attn_b_conv"])
    o["m_w_dt_in"] = c(w_x[:, :DTR])
    o["m_w_bc"] = c(np.concatenate([w_x[:, DTR:]] * 3, axis=1))
    o["m_w_dt"] = c(i["L0_attn_W_dt"])
    o["m_b_dt"] = cols(i["L0_attn_b_dt"])
    o["m_a_log"] = c(np.asarray(i["L0_attn_A_log"]).reshape(DC, P, DS).transpose(1, 0, 2))
    o["m_d"] = cols(i["L0_attn_D"])
    o["m_w_out"] = c(np.asarray(i["L0_attn_W_out"]).reshape(DC, P, D).transpose(1, 0, 2))
    o["m_b_out"] = c(np.asarray(i["L0_attn_b_out"])[None, :])

    def pack(w1, b1, w2, b2):
        w1, b1, w2, b2 = (np.asarray(a) for a in (w1, b1, w2, b2))
        e, _, f = w1.shape
        return c(np.concatenate([
            w1, w2.reshape(e, f // P, P, D).transpose(0, 2, 1, 3).reshape(e, P, -1),
            b1.reshape(e, f // P, P).transpose(0, 2, 1), np.broadcast_to(b2[:, None, :], (e, P, D))], axis=2))

    o["f0_norm"] = c(np.asarray(i["L0_ffn_norm_weight"])[None, :])
    o["f0_router"] = c(np.asarray(i["L0_ffn_router_weight"]).T)
    o["f0_router_b"] = c(np.asarray(i["L0_ffn_router_bias"])[None, :])
    o["f0_const"] = c(np.asarray(i["L0_ffn_constant_vectors"])[None])
    o["f0_packed"] = pack(np.asarray(i["L0_ffn_fc1_weight"]).transpose(0, 2, 1), i["L0_ffn_fc1_bias"],
                          np.asarray(i["L0_ffn_fc2_weight"]).transpose(0, 2, 1), i["L0_ffn_fc2_bias"])
    w1, w2, w3, gate = (np.concatenate([np.asarray(i["L1_ffn_" + k]), np.asarray(i["L1_ffn_new_" + k])])
                        for k in ("w1", "w2", "w3", "gate_weight"))
    o["f1_gate"] = c(gate.T)
    o["f1_gate_b"] = c(np.concatenate([np.zeros(E1 - 1, np.float32), np.asarray(i["L1_ffn_gate_bias"])])[None, :])
    o["f1_w13"] = c(np.concatenate([w1.transpose(2, 0, 1), w3.transpose(2, 0, 1)], axis=2))
    w2 = np.pad(w2.transpose(0, 2, 1), ((0, 0), (0, len(H1_CUTS) * P - H1), (0, 0)))
    o["f1_w2"] = c(w2.reshape(E1, len(H1_CUTS), P, D).transpose(2, 0, 1, 3).reshape(P, E1, -1))
    by_d = np.arange(D).reshape(HEADS, HD).T.ravel()
    for m in "qk":
        o["a1_w" + m] = c(np.asarray(i["L1_attn_W" + m]).T[:, by_d])
        o["a1_b" + m] = c(np.asarray(i["L1_attn_b" + m])[by_d][:, None])
    for m in "vo":
        o["a1_w" + m] = c(np.asarray(i["L1_attn_W" + m]).T)
        o["a1_b" + m] = c(np.asarray(i["L1_attn_b" + m])[None, :])
    w_qkv, b_qkv = np.asarray(i["L2_attn_w_qkv"]), np.asarray(i["L2_attn_b_qkv"])
    o["a2_wq_t"], o["a2_wv_t"] = c(w_qkv[:, :D].T), c(w_qkv[:, 2 * D:].T)
    o["a2_wk"], o["a2_bk"] = c(w_qkv[:, D:2 * D][:, by_d]), c(b_qkv[D:2 * D][by_d][:, None])
    o["a2_bq"], o["a2_bv"] = c(b_qkv[:D][:, None]), c(b_qkv[2 * D:][:, None])
    o["a2_wo"], o["a2_bo"] = c(i["L2_attn_w_proj"]), c(np.asarray(i["L2_attn_b_proj"])[None, :])
    for m, order in (("q", by_d), ("v", np.arange(D))):
        a, b = np.asarray(i["L2_attn_a_" + m]), np.asarray(i["L2_attn_b_" + m])
        rank = a.shape[1]
        big_a = np.zeros((HEADS, rank, HEADS, HD), a.dtype)
        big_b = np.zeros((HEADS, rank, HEADS, HD), b.dtype)
        for h in range(HEADS):
            big_a[h, :, h, :] = a.T
            big_b[h, :, h, :] = b
        o["l" + m + "_a"] = c(big_a.reshape(2, P, D).transpose(1, 0, 2))
        o["l" + m + "_b"] = c(big_b.reshape(2, P, D)[:, :, order].transpose(1, 0, 2))
        o["l" + m + "_eye"] = c(np.eye(D, dtype=np.float32)[:, order])
    o["f2_g"], o["f2_b"] = cols(i["L2_ffn_ln_g"]), cols(i["L2_ffn_ln_b"])
    o["f2_aw"], o["f2_ab"] = c(i["L2_ffn_attn_w"]), cols(i["L2_ffn_attn_b"])
    o["f2_nw"], o["f2_nb"] = c(i["L2_ffn_next_w"]), c(np.asarray(i["L2_ffn_next_b"])[None, :])
    packed = pack(i["L2_ffn_w1"], i["L2_ffn_b1"], i["L2_ffn_w2"], i["L2_ffn_b2"])
    o["f2_packed"] = c(np.concatenate([packed[:, :, :-P], np.asarray(i["L2_ffn_b2"])[:, :, None]], axis=2))
    w_in, b_in = np.asarray(i["L3_attn_W_in"]), np.asarray(i["L3_attn_b_in"])
    o["a3_g"], o["a3_b"] = cols(i["L3_attn_ln_g"]), cols(i["L3_attn_ln_b"])
    o["a3_w"] = c(w_in)
    o["a3_bu"], o["a3_bz"] = cols(b_in[:EG]), cols(b_in[2 * EG:])
    o["a3_bv"] = c(b_in[None, EG:2 * EG])
    o["a3_qk"] = c(np.stack([np.asarray(i["L3_attn_" + n]) for n in ("gamma_q", "beta_q", "gamma_k", "beta_k")], axis=1))
    o["a3_wo"] = c(np.asarray(i["L3_attn_W_out"]).reshape(EG // P, P, D).transpose(1, 0, 2))
    o["a3_bo"] = c(np.asarray(i["L3_attn_b_out"])[None, :])
    o["f3_gate"] = c(i["L3_ffn_wg"])
    o["f3_packed"] = pack(i["L3_ffn_w1"], i["L3_ffn_b1"], i["L3_ffn_w2"], i["L3_ffn_b2"])
    return o


def kernel(**inputs):
    import numpy as np
    import concourse.bacc as bacc
    from concourse.bass_utils import run_bass_kernel_spmd

    nc = bacc.Bacc("TRN2", target_bir_lowering=False, num_devices=1)
    arrays = layouts(inputs)
    t = {name: nc.dram_tensor(name, a.shape, mybir.dt.from_np(a.dtype), kind="ExternalInput").ap()
         for name, a in arrays.items()}
    out = nc.dram_tensor("out", (N, D), F32, kind="ExternalOutput").ap()
    program(nc, t, out)
    res = run_bass_kernel_spmd(nc, [arrays], core_ids=[0])
    return np.asarray(res.results[0]["out"]).reshape(BATCH, T, D)
```

```python
from collections import namedtuple
from contextlib import ExitStack, contextmanager

import concourse.bass as bass
from concourse import mybir

F32 = mybir.dt.float32
BF16 = mybir.dt.bfloat16
I32 = mybir.dt.int32
ALU = mybir.AluOpType
ACT = mybir.ActivationFunctionType
AX_X = mybir.AxisListType.X

P = 128
D = 128
BATCH, T = 16, 256
N = BATCH * T
NT = N // P
QT = T // P
HEADS = 16
HD = D // HEADS
LN_EPS = 1e-5
OUT_OF_RANGE = 65536.0
TAKEN = -1e30
EXP_CENTRE = 2e-6

DI, DS, DTR, TAPS = 256, 16, 64, 4
DC = DI // P
E0, CAP0, F0, FIRST_MLP0 = 16, 512, 512, 4
E1, H1 = 9, 352
H1_CUTS = [(0, 128), (128, 128), (256, 96)]
TILES1 = (2 * N + E1 * (P - 1)) // P
E2, F2 = 8, 512
EG = 256
E3, CAP3, F3 = 8, 640, 512
FC = F0 // P


class Names:
    pass


class Chain:

    def __init__(self, eng, sem, base=0):
        self.eng, self.sem, self.base, self.n = eng, sem, base, 0

    def add(self, ins):
        self.n += 1
        ins.then_inc(self.sem, 1)

    def wait(self):
        self.eng.wait_ge(self.sem, self.base + self.n)

    def step(self, ins):
        self.add(ins)
        self.wait()


@contextmanager
def section(nc, title, *names):
    sems = [nc.alloc_semaphore(f"{title}_{n}") for n in names]
    with ExitStack() as ctx:
        def sb(name, shape, dt=F32):
            return ctx.enter_context(nc.sbuf_tensor(f"{title}_{name}", shape, dt))

        yield namedtuple("Section", names + ("sems", "sb"))(*sems, sems, sb)
    nc.clear_and_free_semaphores(sems)
    nc.all_engine_barrier()


def rows(ap):
    return ap.rearrange("p a b -> p (a b)")


def setup(nc, g, t):
    with section(nc, "setup", "x_in", "filled", "consts") as s, nc.Block() as block:

        @block.sync
        def _(sp):
            sp.dma_start(g.x[:], t["x"].rearrange("(t p) d -> p t d", p=P)).then_inc(s.x_in, 16)
            sp.wait_ge(s.x_in, 16)

        @block.gpsimd
        def _(pool):
            for b, v in ((g.ident, 0.0), (g.ident_b, 0.0), (g.ones_b, 1.0), (g.before, 0.0), (g.after_neg, 0.0),
                         (g.ones_row, 1.0), (g.zeros, 0.0), (g.head_sel, 0.0), (g.future_q, 0.0)):
                nc.gpsimd.memset(b[:], v).then_inc(s.filled, 1)
            pool.wait_ge(s.filled, 9)
            for b in (g.ident, g.ident_b):
                nc.gpsimd.affine_select(out=b[:], in_=b[:], compare_op=ALU.not_equal, fill=1.0, base=0,
                                        pattern=[[-1, P]], channel_multiplier=1).then_inc(s.consts, 1)
            nc.gpsimd.affine_select(out=g.before[:], in_=g.before[:], compare_op=ALU.is_ge, fill=1.0, base=0,
                                    pattern=[[-1, P]], channel_multiplier=1).then_inc(s.consts, 1)
            nc.gpsimd.affine_select(out=g.after_neg[:], in_=g.after_neg[:], compare_op=ALU.is_ge, fill=-1e30, base=0,
                                    pattern=[[1, P]], channel_multiplier=-1).then_inc(s.consts, 1)
            nc.gpsimd.affine_select(out=g.future_q[:], in_=g.future_q[:], compare_op=ALU.is_ge, fill=-1e30, base=0,
                                    pattern=[[-1, P]], channel_multiplier=1).then_inc(s.consts, 1)
            for half in range(2):
                v = g.head_sel[:]
                nc.gpsimd.affine_select(out=v, in_=v, compare_op=ALU.not_equal, fill=-1.0, base=-HEADS * half,
                                        pattern=[[-1, HEADS], [0, P]], channel_multiplier=1).then_inc(s.consts, 1)
                pool.wait_ge(s.consts, 6 + half)


def normalise(nc, g, title, src, dst, dst_t, kind, scale_col=None, bias_col=None, w_row=None, pool_job=None):
    G = 4
    with section(nc, title, "cols_in", "stats_done", "aggr_done", "var_ready", "std_ready", "rstd_step", "xn_ready",
                 "turned", "t_ready", "job_done") as s:
        stats = s.sb("stats", [P, NT, 6])
        mv = s.sb("mv", [P, NT, 2])
        std = s.sb("std", [P, NT])
        rstd = s.sb("rstd", [P, NT])
        inv = s.sb("inv", [P, NT])
        cols = s.sb("norm_cols", [P, 2])
        wr = s.sb("norm_row", [P, D])
        n_cols = 0
        with nc.Block() as block:

            @block.sync
            def _(sp):
                nonlocal n_cols
                for c, col in enumerate((scale_col, bias_col)):
                    if col is not None:
                        sp.dma_start(cols[:, c:c + 1], col).then_inc(s.cols_in, 16)
                        n_cols += 16
                if w_row is not None:
                    sp.dma_start(wr[:], w_row.to_broadcast([P, D])).then_inc(s.cols_in, 16)
                    n_cols += 16

            @block.gpsimd
            def _(pool):
                if pool_job:
                    pool_job(pool, s.job_done)

            @block.vector
            def _(dve):
                for i in range(NT):
                    nc.vector.bn_stats(stats[:, i, :], src[:, i, :]).then_inc(s.stats_done, 1)
                for i in range(NT):
                    dve.wait_ge(s.stats_done, i + 1)
                    nc.vector.bn_aggr(mv[:, i, :], stats[:, i, :]).then_inc(s.aggr_done, 1)
                dve.wait_ge(s.aggr_done, NT)
                step = Chain(dve, s.rstd_step)
                var = mv[:, :, 1]
                if kind == "rms":
                    step.step(nc.vector.tensor_tensor(std[:], mv[:, :, 0], mv[:, :, 0], ALU.mult))
                    step.step(nc.vector.tensor_tensor(std[:], std[:], mv[:, :, 1], ALU.add))
                    var = std[:]
                nc.vector.tensor_scalar(rstd[:], var, LN_EPS, None, ALU.add).then_inc(s.var_ready, 1)
                dve.wait_ge(s.std_ready, 1)
                step.step(nc.vector.reciprocal(inv[:], std[:]))
                step.step(nc.vector.tensor_tensor(rstd[:], rstd[:], inv[:], ALU.mult))
                step.step(nc.vector.tensor_tensor(rstd[:], rstd[:], inv[:], ALU.mult))
                step.step(nc.vector.tensor_scalar(rstd[:], rstd[:], -0.5, 1.5, ALU.mult, ALU.add))
                step.step(nc.vector.tensor_tensor(rstd[:], rstd[:], inv[:], ALU.mult))
                if n_cols:
                    dve.wait_ge(s.cols_in, n_cols)
                for i in range(NT):
                    if kind == "ln":
                        ins = nc.vector.tensor_scalar(dst[:, i, :], src[:, i, :], mv[:, i, 0:1], rstd[:, i:i + 1],
                                                      ALU.subtract, ALU.mult)
                    else:
                        ins = nc.vector.scalar_tensor_tensor(out=dst[:, i, :], in0=src[:, i, :],
                                                             scalar=rstd[:, i:i + 1], in1=wr[:],
                                                             op0=ALU.mult, op1=ALU.mult)
                    ins.then_inc(s.xn_ready, 1)

            @block.tensor
            def _(pe):
                for i in range(NT):
                    pe.wait_ge(s.xn_ready, i + 1)
                    ins = nc.tensor.transpose(g.ps[:, i // G, (i % G) * P:(i % G + 1) * P], dst[:, i, :], g.ident[:])
                    if i % G == G - 1:
                        ins.then_inc(s.turned, 1)

            @block.scalar
            def _(act):
                act.wait_ge(s.var_ready, 1)
                nc.scalar.activation(std[:], rstd[:], ACT.Sqrt).then_inc(s.std_ready, 1)
                if n_cols:
                    act.wait_ge(s.cols_in, n_cols)
                for b in range(NT // G):
                    act.wait_ge(s.turned, b + 1)
                    to = dst_t[:, b * G * P:(b + 1) * G * P]
                    if scale_col is not None:
                        nc.scalar.activation(to, g.ps[:, b, :], ACT.Identity, scale=cols[:, 0:1],
                                             bias=cols[:, 1:2]).then_inc(s.t_ready, 1)
                    else:
                        nc.scalar.copy(to, g.ps[:, b, :]).then_inc(s.t_ready, 1)
                act.wait_ge(s.t_ready, NT // G)


def mamba_in(nc, g, t, u, gate, pool_job):
    XZ = 8
    with section(nc, "conv", "w_in", "xz_ready", "conv_step", "act_done", "job_done") as s:
        w = s.sb("w_in_sb", [P, 2 * DI])
        taps = s.sb("taps", [P, DC, TAPS])
        bc = s.sb("b_conv", [P, DC])
        acc = s.sb("conv_acc", [P, 2, DC, T])
        with nc.Block() as block:

            @block.sync
            def _(sp):
                for dst, src in ((w, "m_w_in"), (taps, "m_taps"), (bc, "m_b_conv")):
                    sp.dma_start(dst[:], t[src]).then_inc(s.w_in, 16)

            def batches(eng, body):
                with eng.Fori(0, BATCH // 2) as it:
                    for p in range(2):
                        body(it * 2 + p, p)

            @block.gpsimd
            def _(pool):
                pool_job(pool, s.job_done)

            @block.tensor
            def _(pe):
                pe.wait_ge(s.w_in, 48)

                def body(b, p):
                    pe.wait_ge(s.conv_step, b * XZ + XZ)
                    pe.wait_ge(s.act_done, b + 1)
                    for c in range(2 * DC):
                        ins = nc.tensor.matmul(g.ps[:, 2 * p + c // DC, (c % DC) * T:(c % DC + 1) * T],
                                               w[:, c * P:(c + 1) * P], g.xn_t[:, bass.ds(b * T, T)],
                                               start=True, stop=True)
                    ins.then_inc(s.xz_ready, 1)
                batches(pe, body)

            @block.vector
            def _(dve):
                dve.wait_ge(s.w_in, 48)
                dve.sem_inc(s.conv_step, 2 * XZ)

                def body(b, p):
                    dve.wait_ge(s.xz_ready, b + 1)
                    dve.wait_ge(s.act_done, b + 1)
                    step = Chain(dve, s.conv_step, b * XZ + 2 * XZ)
                    for k, shift in ((1, 0), (0, -1), (2, 1), (3, 2)):
                        for c in range(DC):
                            x = g.ps[:, 2 * p, c * T:(c + 1) * T]
                            a = acc[:, p, c, :]
                            if shift == 0:
                                ins = nc.vector.tensor_scalar(a, x, taps[:, c, k:k + 1], None, ALU.mult)
                            else:
                                lo, hi = max(0, -shift), T - max(0, shift)
                                ins = nc.vector.scalar_tensor_tensor(
                                    out=a[:, lo:hi], in0=x[:, lo + shift:hi + shift], scalar=taps[:, c, k:k + 1],
                                    in1=a[:, lo:hi], op0=ALU.mult, op1=ALU.add)
                            step.add(ins)
                        if shift != 2:
                            step.wait()
                    assert step.n == XZ
                batches(dve, body)

            @block.scalar
            def _(act):
                act.wait_ge(s.w_in, 48)
                nc.scalar.preload_act_table(ACT.Silu)
                act.sem_inc(s.act_done, 2)

                def body(b, p):
                    act.wait_ge(s.xz_ready, b + 1)
                    nc.scalar.activation(gate[:, :, bass.ds(b * T, T)],
                                         g.ps[:, 2 * p + 1, :].rearrange("p (c t) -> p c t", c=DC), ACT.Silu)
                    act.wait_ge(s.conv_step, b * XZ + 3 * XZ)
                    for c in range(DC):
                        ins = nc.scalar.activation(u[:, c, bass.ds(b * T, T)], acc[:, p, c, :], ACT.Silu,
                                                   bias=bc[:, c:c + 1])
                    ins.then_inc(s.act_done, 1)
                batches(act, body)


def in_turn(eng, n, stage):
    stage(0, 0, 0, True, False)
    stage(1, 0, 1, True, True)
    with eng.Fori(1, n // 2) as it:
        for p in range(2):
            stage(it * 2 + p, it, p, True, True)
    stage(n, 0, 0, False, True)


def mamba_delta(nc, g, t, delta, bc3):
    CH = 512
    NCH = N // CH
    KBC = 3 * 2 * DS
    W = 2 * DS
    with section(nc, "delta", "w_in", "dt_ready", "dtx_done", "z_ready", "zb_done", "high_done", "rem_done",
                 "copied", "split_done", "abs_done", "exp_done", "ln_done", "delta_done") as s:
        w_dt_in = s.sb("w_dt_in", [P, P])
        w_bc = s.sb("w_bc", [P, KBC])
        w_dt = s.sb("w_dt", [P, DI])
        b_dt = s.sb("b_dt", [P, DC])
        dtx = s.sb("dtx", [P, 2, CH])
        rem = s.sb("rem", [KBC, 2, CH])
        e = s.sb("e", [P, DC, N])
        with nc.Block() as block:

            @block.sync
            def _(sp):
                for dst, src in ((w_dt_in, "m_w_dt_in"), (w_bc, "m_w_bc"), (w_dt, "m_w_dt"), (b_dt, "m_b_dt")):
                    sp.dma_start(dst[:], t[src]).then_inc(s.w_in, 16)

            @block.tensor
            def _(pe):
                pe.wait_ge(s.w_in, 64)
                pe.sem_inc(s.rem_done, 2)
                pe.sem_inc(s.zb_done, 2)

                def stage(ch, turn, p, now, prev):
                    if now:
                        x = g.xn_t[:, bass.ds(ch * CH, CH)]
                        pe.wait_ge(s.rem_done, ch + 1)
                        nc.tensor.matmul(g.ps[:, 4 * p, :], w_dt_in[:], x, start=True, stop=True)
                        nc.tensor.matmul(g.ps[0:KBC, 4 * p + 1, :], w_bc[:], x, start=True,
                                         stop=True).then_inc(s.dt_ready, 1)
                    if prev:
                        q = 1 - p
                        pe.wait_ge(s.dtx_done, ch)
                        pe.wait_ge(s.zb_done, ch)
                        for c in range(DC):
                            ins = nc.tensor.matmul(g.ps[:, 4 * q + 2 + c, :], w_dt[:, c * P:(c + 1) * P], dtx[:, q],
                                                   start=True, stop=True)
                        ins.then_inc(s.z_ready, 1)
                in_turn(pe, NCH, stage)

            @block.vector
            def _(dve):
                dve.wait_ge(s.w_in, 64)
                dve.sem_inc(s.split_done, 1)

                def stage(ch, turn, p, now, prev):
                    q = 1 - p
                    if now:
                        dve.wait_ge(s.dt_ready, ch + 1)
                        nc.vector.tensor_copy(dtx[:, p], g.ps[:, 4 * p, :]).then_inc(s.dtx_done, 1)
                    if prev:
                        dve.wait_ge(s.z_ready, ch)
                        for c in range(DC):
                            ins = nc.vector.tensor_scalar(delta[:, c, bass.ds((ch - 1) * CH, CH)],
                                                          g.ps[:, 4 * q + 2 + c, :], b_dt[:, c:c + 1], None, ALU.add)
                        ins.then_inc(s.zb_done, 1)
                    if now:
                        if prev:
                            dve.wait_ge(s.split_done, ch)
                        dve.wait_ge(s.high_done, ch + 1)
                        nc.vector.tensor_tensor(rem[:, p], g.ps[0:KBC, 4 * p + 1, :], bc3[:, bass.ds(ch * CH, CH)],
                                                ALU.subtract).then_inc(s.rem_done, 1)
                    if prev:
                        dve.wait_ge(s.copied, ch)
                        low = bc3[2 * W:3 * W, bass.ds((ch - 1) * CH, CH)]
                        nc.vector.tensor_tensor(low, rem[2 * W:3 * W, q], low, ALU.subtract).then_inc(s.split_done, 1)
                in_turn(dve, NCH, stage)
                with dve.Fori(0, NCH) as ch:
                    dve.wait_ge(s.ln_done, ch + 1)
                    d = delta[:, :, bass.ds(ch * CH, CH)]
                    nc.vector.scalar_tensor_tensor(out=d, in0=d, scalar=0.0, in1=e[:, :, bass.ds(ch * CH, CH)],
                                                   op0=ALU.max, op1=ALU.add).then_inc(s.delta_done, 1)

            @block.scalar
            def _(act):
                nc.scalar.preload_act_table(ACT.Exp)

                def stage(ch, turn, p, now, prev):
                    if now:
                        act.wait_ge(s.dt_ready, ch + 1)
                        to = bass.ds(ch * CH, CH)
                        nc.scalar.copy(bc3[:, to], g.ps[0:KBC, 4 * p + 1, :]).then_inc(s.high_done, 1)
                    if prev:
                        act.wait_ge(s.zb_done, ch + 2)
                        at = bass.ds((ch - 1) * CH, CH)
                        nc.scalar.activation(e[:, :, at], delta[:, :, at], ACT.Abs).then_inc(s.abs_done, 1)
                    if now:
                        act.wait_ge(s.rem_done, ch + 3)
                        to = bass.ds(ch * CH, CH)
                        nc.scalar.copy(bc3[W:2 * W, to], rem[W:2 * W, p])
                        nc.scalar.copy(bc3[2 * W:3 * W, to], rem[2 * W:3 * W, p]).then_inc(s.copied, 1)
                    if prev:
                        act.wait_ge(s.z_ready, 1)
                        act.wait_ge(s.abs_done, ch)
                        nc.scalar.activation(e[:, :, at], e[:, :, at], ACT.Exp, scale=-1.0).then_inc(s.exp_done, 1)
                in_turn(act, NCH, stage)
                act.wait_ge(s.exp_done, NCH)
                nc.scalar.preload_act_table(ACT.Ln)
                with act.Fori(0, NCH) as ch:
                    at = bass.ds(ch * CH, CH)
                    nc.scalar.activation(e[:, :, at], e[:, :, at], ACT.Ln, bias=1.0).then_inc(s.ln_done, 1)


def mamba_scan(nc, g, t, u, gate, delta, bc3):
    NG, GN = 4, DS // 4
    KBC = 3 * 2 * DS
    with section(nc, "scan", "w_in", "sel_fill", "sel_done", "neg_a", "b_ready", "c_ready", "b_copied", "bu0_made", "bu1_made", "diag_done",
                 "da_ready", "scan_step", "hc_ready", "y_ready", "yg_ready", "o_ready", "x_done", "du_ready") as s:
        a_neg = s.sb("a_neg", [P, DC, DS])
        d_col = s.sb("d_col", [P, DC])
        d_diag = s.sb("d_diag", [P, DC, P])
        w_out = s.sb("w_out_m", [P, DC, D])
        b_out = s.sb("b_out_m", [1, D])
        sel = s.sb("state_sel", [KBC, 2 * DS, P], BF16)
        exp_centre = s.sb("exp_centre", [P, 1])
        dl = s.sb("dl", [P, 2, DC, T])
        du = s.sb("du", [P, 2, DC, T])
        da = s.sb("da", [P, DC, GN, T])
        bu0 = s.sb("bu0", [P, GN, T])
        free = g.xn_t[:].rearrange("p (k n t) -> p k n t", n=GN, t=T)
        bu1, b_sb, h = free[:, 0], free[:, 1], free[:, 2:4]
        hc = s.sb("hc", [P, DC, GN, T])
        yg = s.sb("yg", [P, DC, T])
        b_ps = g.ps[:, 0:2, :].rearrange("p k (n t) -> p (k n) t", t=T)
        c_ps = g.ps[:, 2:4, :].rearrange("p k (n t) -> p (k n) t", t=T)
        W_IN = 4 * 16
        SEL = 5

        def y_ps(c):
            return g.ps[:, 4 + c, 0:T]

        def each(eng, stage):
            stage(0, 0, True, False)
            with eng.Fori(0, BATCH // 2 - 1) as it:
                for q in range(2):
                    stage(it * 2 + 1 + q, (1 + q) % 2, False, False)
            stage(BATCH - 1, 1, False, True)

        with nc.Block() as block:

            @block.sync
            def _(sp):
                for dst, src in ((a_neg, "m_a_log"), (d_col, "m_d"), (w_out, "m_w_out"), (b_out, "m_b_out")):
                    sp.dma_start(dst[:], t[src]).then_inc(s.w_in, 16)

            @block.gpsimd
            def _(pool):
                nc.gpsimd.memset(sel[:], 0.0).then_inc(s.sel_fill, 1)
                pool.wait_ge(s.sel_fill, 1)
                for q in range(3):
                    v = sel[2 * DS * q:2 * DS * (q + 1), :, :]
                    nc.gpsimd.affine_select(out=v, in_=v, compare_op=ALU.not_equal, fill=1.0, base=0,
                                            pattern=[[-1, 2 * DS], [0, P]],
                                            channel_multiplier=1).then_inc(s.sel_done, 1)
                    pool.wait_ge(s.sel_done, q + 1)
                nc.gpsimd.memset(da[:, :, :, 0:1], 0.0).then_inc(s.sel_done, 1)
                nc.gpsimd.memset(exp_centre[:], EXP_CENTRE).then_inc(s.sel_done, 1)

                def inputs(b, p):
                    d, to = delta[:, :, bass.ds(b * T, T)], bass.ds(b * T, T)
                    nc.gpsimd.tensor_copy(dl[:, p], d)
                    nc.gpsimd.tensor_tensor(du[:, p], d, u[:, :, to], ALU.mult).then_inc(s.du_ready, 1)

                def stage(b, p, first, last):
                    pool.wait_ge(s.du_ready, b + 1)
                    for gi in range(NG):
                        k = b * NG + gi
                        pool.wait_ge(s.b_copied, k + 1)
                        pool.wait_ge(s.scan_step, k * 2 + 2)
                        nc.gpsimd.tensor_tensor(bu1, b_sb, du[:, p, 1:2, :].to_broadcast([P, GN, T]),
                                                ALU.mult).then_inc(s.bu1_made, 1)
                        if gi == 1 and not last:
                            inputs(b + 1, 1 - p)
                inputs(0, 0)
                each(pool, stage)

            @block.tensor
            def _(pe):
                pe.wait_ge(s.w_in, W_IN)
                pe.wait_ge(s.sel_done, SEL)
                pe.wait_ge(s.diag_done, 1)

                def spread_b(b, gi):
                    for n in range(GN):
                        ins = nc.tensor.matmul(b_ps[:, n, :], sel[:, gi * GN + n, :], bc3[:, bass.ds(b * T, T)],
                                               start=True, stop=True)
                    ins.then_inc(s.b_ready, 1)

                def sum_states(b, gi, c):
                    if gi == 0:
                        pe.wait_ge(s.yg_ready, b)
                        nc.tensor.matmul(y_ps(c), d_diag[:, c, :], u[:, c, bass.ds(b * T, T)], start=True,
                                         stop=False)
                    for n in range(GN):
                        ins = nc.tensor.matmul(y_ps(c), g.ident[:], hc[:, c, n, :], start=False,
                                               stop=(gi == NG - 1 and n == GN - 1))
                    ins.then_inc(s.y_ready, 1)

                def project(b):
                    pe.wait_ge(s.yg_ready, b)
                    pe.wait_ge(s.x_done, b)
                    for k in range(QT):
                        o = g.ps[:, 7, k * D:(k + 1) * D]
                        for c in range(DC):
                            nc.tensor.matmul(o, yg[:, c, k * P:(k + 1) * P], w_out[:, c, :], start=(c == 0), stop=False)
                        ins = nc.tensor.matmul(o, g.ones_row[:], b_out[:], start=False, stop=True)
                    ins.then_inc(s.o_ready, 1)

                def stage(b, p, first, last):
                    for gi in range(NG):
                        k = b * NG + gi
                        pe.wait_ge(s.hc_ready, k * 2 + 2)
                        for n in range(GN):
                            ins = nc.tensor.matmul(c_ps[:, n, :], sel[:, DS + gi * GN + n, :],
                                                   bc3[:, bass.ds(b * T, T)], start=True, stop=True)
                        ins.then_inc(s.c_ready, 1)
                        if gi > 0:
                            sum_states(b, gi - 1, 1)
                        elif not first:
                            sum_states(b - 1, NG - 1, 1)
                        if not (last and gi == NG - 1):
                            pe.wait_ge(s.bu0_made, k + 1)
                            pe.wait_ge(s.b_copied, k + 1)
                            if gi < NG - 1:
                                spread_b(b, gi + 1)
                            else:
                                spread_b(b + 1, 0)
                        pe.wait_ge(s.hc_ready, k * 2 + 3)
                        sum_states(b, gi, 0)
                        if gi == 1 and not first:
                            project(b)

                spread_b(0, 0)
                each(pe, stage)
                pe.wait_ge(s.hc_ready, BATCH * NG * 2 + 2)
                sum_states(BATCH - 1, NG - 1, 1)
                project(BATCH)

            @block.scalar
            def _(act):
                act.wait_ge(s.w_in, W_IN)
                nc.scalar.preload_act_table(ACT.Exp)
                nc.scalar.activation(a_neg[:], a_neg[:], ACT.Exp).then_inc(s.neg_a, 1)
                act.wait_ge(s.neg_a, 2)
                act.wait_ge(s.sel_done, SEL)

                def stage(b, p, first, last):
                    act.wait_ge(s.du_ready, b + 1)
                    for gi in range(NG):
                        for c in range(DC):
                            act.wait_ge(s.scan_step, b * 2 * NG + 2 * gi + c + 1)
                            for n in range(GN):
                                ins = nc.scalar.activation(da[:, c, n, 1:T], dl[:, p, c, 1:T],
                                                           ACT.Exp, scale=a_neg[:, c, gi * GN + n:gi * GN + n + 1],
                                                           bias=exp_centre[:])
                            ins.then_inc(s.da_ready, 1)
                            if c == 0:
                                k = b * NG + gi
                                act.wait_ge(s.b_ready, k + 1)
                                if not (first and gi == 0):
                                    act.wait_ge(s.bu1_made, k)
                                nc.scalar.copy(b_sb, b_ps).then_inc(s.b_copied, 1)
                each(act, stage)

            @block.vector
            def _(dve):
                dve.wait_ge(s.w_in, W_IN)
                for c in range(DC):
                    ins = nc.vector.tensor_scalar(d_diag[:, c, :], g.ident[:], d_col[:, c:c + 1], None, ALU.mult)
                ins.then_inc(s.diag_done, 1)
                dve.wait_ge(s.neg_a, 1)
                nc.vector.tensor_scalar(a_neg[:], a_neg[:], -1.0, None, ALU.mult).then_inc(s.neg_a, 1)
                for sem, n in ((s.x_done, 1), (s.hc_ready, 2), (s.scan_step, 2), (s.y_ready, 2)):
                    dve.sem_inc(sem, n)

                def gated(b):
                    dve.wait_ge(s.y_ready, b * 2 * NG + 2)
                    nc.vector.tensor_tensor(yg[:], g.ps[:, 4:6, 0:T],
                                            gate[:, :, bass.ds((b - 1) * T, T)], ALU.mult).then_inc(s.yg_ready, 1)

                def add(b):
                    dve.wait_ge(s.o_ready, b)
                    xs = g.x[:, bass.ds((b - 1) * QT, QT), :]
                    nc.vector.tensor_tensor(xs, xs, g.ps[:, 7, 0:QT * D].rearrange("p (k d) -> p k d", k=QT),
                                            ALU.add).then_inc(s.x_done, 1)

                def stage(b, p, first, last):
                    dve.wait_ge(s.du_ready, b + 1)
                    for gi in range(NG):
                        for c in range(DC):
                            k = b * 2 * NG + 2 * gi + c + 1
                            if c == 0:
                                dve.wait_ge(s.b_ready, b * NG + gi + 1)
                                dve.wait_ge(s.b_copied, b * NG + gi + 1)
                                nc.vector.tensor_tensor(bu0[:], b_ps, du[:, p, 0:1, :].to_broadcast([P, GN, T]),
                                                        ALU.mult).then_inc(s.bu0_made, 1)
                                dve.wait_ge(s.bu0_made, b * NG + gi + 1)
                            else:
                                dve.wait_ge(s.bu1_made, b * NG + gi + 1)
                            dve.wait_ge(s.da_ready, k)
                            bu = bu1 if c else bu0[:]
                            nc.vector.tensor_tensor_scan(rows(h[:, c]), rows(da[:, c]), rows(bu), 0.0,
                                                         ALU.mult, ALU.add).then_inc(s.scan_step, 1)
                            dve.wait_ge(s.scan_step, k + 2)
                            if c == 0:
                                if gi == 0 and not first:
                                    gated(b)
                                dve.wait_ge(s.c_ready, b * NG + gi + 1)
                            dve.wait_ge(s.y_ready, k)
                            nc.vector.tensor_tensor(hc[:, c, :, :], h[:, c], c_ps, ALU.mult).then_inc(s.hc_ready, 1)
                        if gi == 1 and not first:
                            add(b)
                each(dve, stage)
                gated(BATCH)
                add(BATCH)


def scatter(nc, pool, done, src, disp, r, top):
    for i in range(NT):
        for k in range(top):
            pool.indirect_dma_start(disp, bass.IndirectOffsetOnAxis(ap=r.scat_i[:, k, i:i + 1], axis=0),
                                    src[:, i, :], None, bounds_check=disp.shape[0] - 1,
                                    oob_is_err=False).then_inc(done, 16)
    pool.wait_ge(done, 16 * NT * top)


def route(nc, g, t, title, src, src_t, router, n_exp, top, cap, first, disp, r):
    E, K = n_exp, top
    n_rows = disp.shape[0]
    with section(nc, title, "w_in", "zeroed", "iota_done", "logits_ready", "step", "shift_ready", "exp_ready",
                 "chosen_ready", "pos_ready") as s:
        W = s.sb("router", [P, E])
        bias = s.sb("bias", [P, E])
        rev = s.sb("rev", [P, E])
        lg = s.sb("lg", [P, NT, E])
        p = s.sb("p", [P, NT, E])
        tmp = s.sb("tmp", [P, NT, E])
        oh = s.sb("onehot", [P, K, NT, E])
        chosen = s.sb("chosen", [P, NT, E], BF16)
        mx = s.sb("mx", [P, NT])
        val = s.sb("val", [P, K, NT])
        rm = s.sb("rm", [P, K, NT])
        sm = s.sb("sm", [P, NT])
        tot = s.sb("tot", [P, E, NT])
        inc = s.sb("inc", [P, E, NT])
        cont = s.sb("cont", [P, E, NT])
        pos = s.sb("pos", [P, NT, E])
        slot = s.sb("slot", [P, K, NT])
        keep = s.sb("keep", [P, K, NT])
        scat = s.sb("scat", [P, K, NT])
        cnt = s.sb("cnt", [P, E])
        cnt_i = s.sb("cnt_i", [P, E], I32)
        n_tiles = s.sb("n_tiles", [P, E])
        ends = s.sb("ends", [P, E])
        ones_e = s.sb("ones_e", [P, E])
        jot = s.sb("jot", [1, TILES1])
        cmp = s.sb("cmp", [1, TILES1, E])
        te = s.sb("te", [1, TILES1])

        def per_token(ap):
            return ap[:, :, None].to_broadcast([P, NT, E])

        def per_expert(ap):
            return ap[:, None, :].to_broadcast([P, NT, E])

        with nc.Block() as block:

            @block.sync
            def _(sp):
                sp.dma_start(W[:], t[router]).then_inc(s.w_in, 16)
                if title == "route0":
                    sp.dma_start(bias[:], t["f0_router_b"].to_broadcast([P, E])).then_inc(s.w_in, 16)
                if title == "route1":
                    sp.dma_start(bias[:], t["f1_gate_b"].to_broadcast([P, E])).then_inc(s.w_in, 16)
                rep = n_rows * D // P // 512
                sp.dma_start(disp.rearrange("(p r) d -> p (r d)", p=P).rearrange("p (r c) -> p r c", c=512),
                             g.zeros[:, None, :].to_broadcast([P, rep, 512])).then_inc(s.zeroed, 16)

            n_w = 32 if title in ("route0", "route1") else 16

            @block.tensor
            def _(pe):
                pe.wait_ge(s.w_in, n_w)
                for i in range(NT):
                    ins = nc.tensor.matmul(g.ps[:, 0, i * E:(i + 1) * E], src_t[:, i * P:(i + 1) * P], W[:],
                                           start=True, stop=True)
                ins.then_inc(s.logits_ready, 1)
                pe.wait_ge(s.chosen_ready, 1)
                ch = chosen[:].rearrange("p t e -> p (t e)")
                nc.tensor.matmul(g.ps[:, 1, 0:NT * E], g.before[:], ch, start=True, stop=True)
                nc.tensor.matmul(g.ps[:, 2, 0:NT * E], g.ones_b[:], ch, start=True, stop=True).then_inc(s.pos_ready, 1)

            @block.scalar
            def _(act):
                if title == "route0":
                    nc.scalar.preload_act_table(ACT.Sigmoid)
                    act.wait_ge(s.shift_ready, 1)
                    nc.scalar.activation(val[:, 0, :], sm[:], ACT.Sigmoid)
                    nc.scalar.activation(val[:, 1, :], sm[:], ACT.Sigmoid, scale=-1.0).then_inc(s.exp_ready, 1)
                else:
                    act.wait_ge(s.shift_ready, 1)
                    nc.scalar.activation(p[:], lg[:], ACT.Sigmoid if title == "route1" else ACT.Exp
                                         ).then_inc(s.exp_ready, 1)

            @block.vector
            def _(dve):
                c = Chain(dve, s.step)
                v = nc.vector
                dve.wait_ge(s.w_in, n_w)
                dve.wait_ge(s.iota_done, 2)
                c.add(v.memset(cont[:], 1.0))
                c.add(v.memset(ones_e[:], 1.0))
                c.wait()
                c.add(v.memset(cont[:, :, 0:1], 0.0))
                dve.wait_ge(s.logits_ready, 1)
                lps = g.ps[:, 0, 0:NT * E].rearrange("p (t e) -> p t e", e=E)
                if n_w == 32:
                    c.step(v.tensor_tensor(p[:] if title == "route0" else lg[:], lps, per_expert(bias[:]), ALU.add))
                else:
                    c.step(v.tensor_copy(lg[:], lps))
                if title == "route3":
                    c.step(v.tensor_reduce(mx[:], lg[:], AX_X, ALU.max))
                    c.step(v.tensor_tensor(lg[:], lg[:], per_token(mx[:]), ALU.subtract))
                if title != "route0":
                    dve.sem_inc(s.shift_ready, 1)
                    dve.wait_ge(s.exp_ready, 1)
                if title == "route3":
                    c.step(v.tensor_reduce(sm[:], p[:], AX_X, ALU.add))
                    c.step(v.reciprocal(sm[:], sm[:]))
                    c.step(v.tensor_tensor(p[:], p[:], per_token(sm[:]), ALU.mult))
                for k in range(K):
                    c.step(v.tensor_reduce(val[:, k, :], p[:], AX_X, ALU.max))
                    c.step(v.tensor_tensor(tmp[:], p[:], per_token(val[:, k, :]), ALU.is_ge))
                    c.step(v.tensor_tensor(tmp[:], tmp[:], per_expert(rev[:]), ALU.mult))
                    c.step(v.tensor_reduce(rm[:, k, :], tmp[:], AX_X, ALU.max))
                    c.step(v.tensor_tensor(oh[:, k], per_token(rm[:, k, :]), per_expert(rev[:]), ALU.is_equal))
                    if k + 1 < K:
                        c.step(v.scalar_tensor_tensor(out=p[:], in0=oh[:, k], scalar=TAKEN, in1=p[:],
                                                      op0=ALU.mult, op1=ALU.add))
                if title == "route0":
                    c.step(v.tensor_tensor(sm[:], val[:, 0, :], val[:, 1, :], ALU.subtract))
                    dve.sem_inc(s.shift_ready, 1)
                    dve.wait_ge(s.exp_ready, 1)
                if K == 2:
                    c.step(v.tensor_tensor(chosen[:], oh[:, 0], oh[:, 1], ALU.add))
                else:
                    c.step(v.tensor_copy(chosen[:], oh[:, 0]))
                dve.sem_inc(s.chosen_ready, 1)
                dve.wait_ge(s.pos_ready, 1)
                c.step(v.tensor_copy(tot[:], g.ps[:, 2, 0:NT * E].rearrange("p (t e) -> p e t", e=E)))
                c.step(v.tensor_tensor_scan(rows(inc[:]), rows(cont[:]), rows(tot[:]), 0.0, ALU.mult, ALU.add))
                c.step(v.tensor_tensor(tot[:], inc[:], tot[:], ALU.subtract))
                c.step(v.tensor_tensor(pos[:], g.ps[:, 1, 0:NT * E].rearrange("p (t e) -> p t e", e=E),
                                       tot[:].rearrange("p e t -> p t e"), ALU.add))
                if cap is None:
                    c.step(v.tensor_scalar(cnt_i[:], inc[:, :, NT - 1], float(P - 1), None, ALU.add))
                    c.step(v.tensor_scalar(cnt_i[:], cnt_i[:], 7, None, ALU.arith_shift_right))
                    c.step(v.tensor_copy(n_tiles[:], cnt_i[:]))
                    c.step(v.tensor_tensor_scan(ends[:], ones_e[:], n_tiles[:], 0.0, ALU.mult, ALU.add))
                    c.step(v.tensor_tensor(cnt[:], ends[:], n_tiles[:], ALU.subtract))
                    c.step(v.tensor_scalar(cnt[:], cnt[:], float(P), None, ALU.mult))
                    c.step(v.tensor_tensor(pos[:], pos[:], per_expert(cnt[:]), ALU.add))
                    c.step(v.tensor_tensor(cmp[:], jot[:, :, None].to_broadcast([1, TILES1, E]),
                                           ends[0:1, None, :].to_broadcast([1, TILES1, E]), ALU.is_ge))
                    c.step(v.tensor_reduce(te[:], cmp[:], AX_X, ALU.add))
                    c.step(v.tensor_scalar(r.tile_e[:], te[:], float(E - 1), None, ALU.min))
                for k in range(K):
                    c.step(v.tensor_tensor(tmp[:], oh[:, k], pos[:], ALU.mult))
                    c.step(v.tensor_reduce(slot[:, k, :], tmp[:], AX_X, ALU.add))
                if cap is None:
                    c.add(v.tensor_copy(r.scat_i[:], slot[:]))
                    c.step(v.tensor_copy(r.rows_i[:], slot[:]))
                    c.step(v.tensor_tensor(sm[:], val[:, 0, :], val[:, 1, :], ALU.add))
                    c.step(v.tensor_scalar(sm[:], sm[:], 1e-20, None, ALU.add))
                    c.step(v.reciprocal(sm[:], sm[:]))
                    c.step(v.tensor_tensor(r.w[:], val[:], sm[:, None, :].to_broadcast([P, K, NT]), ALU.mult))
                else:
                    c.step(v.tensor_scalar(keep[:], slot[:], float(cap), None, ALU.is_lt))
                    c.step(v.tensor_tensor(val[:], val[:], keep[:], ALU.mult))
                    c.step(v.scalar_tensor_tensor(out=slot[:], in0=rm[:], scalar=-float(cap), in1=slot[:],
                                                  op0=ALU.mult, op1=ALU.add))
                    c.step(v.tensor_scalar(slot[:], slot[:], float((E - first) * cap), None, ALU.add))
                    if first:
                        c.step(v.scalar_tensor_tensor(out=keep[:], in0=rm[:], scalar=float(E - first), in1=keep[:],
                                                      op0=ALU.is_le, op1=ALU.mult))
                    c.step(v.scalar_tensor_tensor(out=scat[:], in0=keep[:], scalar=-OUT_OF_RANGE, in1=slot[:],
                                                  op0=ALU.mult, op1=ALU.add))
                    c.add(v.tensor_scalar(r.scat_i[:], scat[:], OUT_OF_RANGE, None, ALU.add))
                    c.step(v.tensor_tensor(r.rows_i[:], slot[:], keep[:], ALU.mult))
                    if K == 1:
                        c.step(v.tensor_copy(r.w[:], val[:]))
                    else:
                        c.step(v.tensor_tensor(sm[:], val[:, 0, :], val[:, 1, :], ALU.add))
                        c.step(v.scalar_tensor_tensor(out=sm[:], in0=sm[:], scalar=0.0, in1=sm[:],
                                                      op0=ALU.is_le, op1=ALU.add))
                        c.step(v.reciprocal(sm[:], sm[:]))
                        c.step(v.tensor_tensor(val[:], val[:], sm[:, None, :].to_broadcast([P, K, NT]), ALU.mult))
                        c.add(v.tensor_tensor(r.w[:], val[:], keep[:], ALU.mult))
                        F = first
                        for k in range(K):
                            c.step(v.tensor_tensor(oh[:, k, :, 0:F], oh[:, k, :, 0:F],
                                                   val[:, k, :, None].to_broadcast([P, NT, F]), ALU.mult))
                        c.step(v.tensor_tensor(r.near[:], oh[:, 0, :, 0:F], oh[:, 1, :, 0:F], ALU.add))

            @block.gpsimd
            def _(pool):
                nc.gpsimd.iota(rev[:], pattern=[[-1, E]], base=E, channel_multiplier=0,
                               allow_small_or_imprecise_dtypes=True).then_inc(s.iota_done, 1)
                nc.gpsimd.iota(jot[:], pattern=[[1, TILES1]], base=0, channel_multiplier=0,
                               allow_small_or_imprecise_dtypes=True).then_inc(s.iota_done, 1)
                pool.wait_ge(s.zeroed, 16)


def experts(nc, g, t, title, packed, n_exp, cap, disp, ybuf, func):
    CT, HC = cap // P, cap // 2
    W2, B1, B2, WN = FC * P, 2 * FC * P, 2 * FC * P + FC, 2 * FC * P + FC + D
    H = 2 * FC
    with section(nc, title, "w_in0", "w_in1", "x_in0", "x_in1", "turned", "xt_ready", "h_ready", "act_done",
                 "y_ready", "y_out", "stored0", "stored1") as s:
        w = s.sb("w", [P, 2, WN])
        xin = s.sb("xin", [P, 2, CT, D])
        xt = s.sb("xt", [P, 2, cap])
        ht = s.sb("ht", [P, FC, cap])
        yo = s.sb("yo", [P, 2, CT, D])
        w_in, x_in, stored = (s.w_in0, s.w_in1), (s.x_in0, s.x_in1), (s.stored0, s.stored1)
        y_ps = g.ps[:, 6:8, :].rearrange("p k c -> p (k c)")[:, 0:CT * D].rearrange("p (t d) -> p t d", d=D)
        t_ps = g.ps[:, 4:6, :].rearrange("p k c -> p (k c)")[:, 0:cap]

        def each(eng, body):
            with eng.Fori(0, n_exp // 2 - 1) as it:
                for p in range(2):
                    body(it * 2 + p, it, p, False)
            body(n_exp - 2, n_exp // 2 - 1, 0, False)
            body(n_exp - 1, n_exp // 2 - 1, 1, True)

        with nc.Block() as block:

            @block.sync
            def _(sp):
                def body(e, it, p, last):
                    sp.wait_ge(s.turned, e + 1)
                    sp.dma_start(xin[:, p], disp[bass.ds(e * cap, cap), :].rearrange("(t p) d -> p t d", p=P)
                                 ).then_inc(x_in[p], 16)
                    sp.wait_ge(s.y_out, e + 1)
                    sp.dma_start(w[:, p], t[packed][bass.ds(e, 1)].rearrange("a p n -> (a p) n")).then_inc(w_in[p], 16)
                each(sp, body)

            @block.tensor
            def _(pe):
                pe.sem_inc(s.turned, 2)
                def transpose(e, it, p):
                    pe.wait_ge(x_in[p], (it + 1) * 16)
                    pe.wait_ge(s.xt_ready, e)
                    for i in range(CT):
                        ins = nc.tensor.transpose(t_ps[:, i * P:(i + 1) * P], xin[:, p, i, :], g.ident[:])
                    ins.then_inc(s.turned, 1)

                def body(e, it, p, last):
                    pe.wait_ge(w_in[p], (it + 1) * 16)
                    pe.wait_ge(s.xt_ready, e + 1)
                    for k in range(H):
                        hf, f = k // FC, k % FC
                        pe.wait_ge(s.act_done, e * H + k + 1)
                        nc.tensor.matmul(g.ps[:, f, 0:HC], w[:, p, f * P:(f + 1) * P], xt[:, p, hf * HC:(hf + 1) * HC],
                                         start=True, stop=True).then_inc(s.h_ready, 1)
                    if not last:
                        transpose(e + 1, it + p, 1 - p)
                    pe.wait_ge(s.act_done, e * H + H + FC)
                    pe.wait_ge(s.y_out, e + 2)
                    for i in range(CT):
                        for f in range(FC):
                            ins = nc.tensor.matmul(y_ps[:, i, :], ht[:, f, i * P:(i + 1) * P],
                                                   w[:, p, W2 + f * P:W2 + (f + 1) * P],
                                                   start=(f == 0), stop=(f == FC - 1))
                    ins.then_inc(s.y_ready, 1)

                transpose(0, 0, 0)
                each(pe, body)

            @block.scalar
            def _(act):
                nc.scalar.preload_act_table(func)
                act.sem_inc(s.act_done, FC)

                def body(e, it, p, last):
                    act.wait_ge(s.y_ready, e)
                    for k in range(H):
                        hf, f = k // FC, k % FC
                        act.wait_ge(s.h_ready, e * H + k + 1)
                        nc.scalar.activation(ht[:, f, hf * HC:(hf + 1) * HC], g.ps[:, f, 0:HC], func,
                                             bias=w[:, p, B1 + f:B1 + f + 1]).then_inc(s.act_done, 1)
                each(act, body)

            @block.vector
            def _(dve):
                dve.sem_inc(s.y_out, 2)

                def take(e, p):
                    dve.wait_ge(s.turned, e + 3)
                    nc.vector.tensor_copy(xt[:, p], t_ps).then_inc(s.xt_ready, 1)

                def body(e, it, p, last):
                    if not last:
                        take(e + 1, 1 - p)
                    dve.wait_ge(s.y_ready, e + 1)
                    dve.wait_ge(stored[p], it * 16)
                    nc.vector.tensor_tensor(yo[:, p], y_ps, w[:, p, None, B2:B2 + D].to_broadcast([P, CT, D]),
                                            ALU.add).then_inc(s.y_out, 1)
                take(0, 0)
                each(dve, body)

            @block.gpsimd
            def _(pool):
                def body(e, it, p, last):
                    pool.wait_ge(s.y_out, e + 3)
                    pool.dma_start(ybuf[bass.ds(e * cap, cap), :].rearrange("(t p) d -> p t d", p=P),
                                   yo[:, p]).then_inc(stored[p], 16)
                each(pool, body)
                for p in range(2):
                    pool.wait_ge(stored[p], n_exp // 2 * 16)


def gather(nc, pool, done, gb, ybuf, r, top):
    for i in range(NT):
        for k in range(top):
            pool.indirect_dma_start(gb[:, k, i, :], None, ybuf,
                                    bass.IndirectOffsetOnAxis(ap=r.rows_i[:, k, i:i + 1], axis=0),
                                    bounds_check=ybuf.shape[0] - 1, oob_is_err=False).then_inc(done, 16)
    pool.wait_ge(done, 16 * NT * top)


def add_results(nc, g, title, gb, r, top):
    with section(nc, title, "step") as s, nc.Block() as block:

        @block.vector
        def _(dve):
            c = Chain(dve, s.step)
            for k in range(top):
                for i in range(NT):
                    c.add(nc.vector.scalar_tensor_tensor(out=g.x[:, i, :], in0=gb[:, k, i, :],
                                                         scalar=r.w[:, k, i:i + 1], in1=g.x[:, i, :],
                                                         op0=ALU.mult, op1=ALU.add))
                c.wait()


def combine(nc, g, t, title, ybuf, top, r, xr=None):
    GRP = 8
    names = [f"gathered{q}" for q in range(NT // GRP)]
    with section(nc, title, *names, "cv_in", "step") as s:
        gb = s.sb("gb", [P, top, NT, D])
        cv = s.sb("cv", [P, 2, D])
        gathered = s.sems[:NT // GRP]
        with nc.Block() as block:

            @block.sync
            def _(sp):
                if xr is not None:
                    sp.dma_start(cv[:], t["f0_const"].to_broadcast([P, 2, D])).then_inc(s.cv_in, 16)

            @block.gpsimd
            def _(pool):
                for i in range(NT):
                    for k in range(top):
                        pool.indirect_dma_start(gb[:, k, i, :], None, ybuf,
                                                bass.IndirectOffsetOnAxis(ap=r.rows_i[:, k, i:i + 1], axis=0),
                                                bounds_check=ybuf.shape[0] - 1,
                                                oob_is_err=False).then_inc(gathered[i // GRP], 16)

            @block.vector
            def _(dve):
                c = Chain(dve, s.step)
                if xr is not None:
                    dve.wait_ge(s.cv_in, 16)
                    for a, src in ((1, None), (2, cv[:, 0, :]), (3, cv[:, 1, :])):
                        for i in range(NT):
                            c.add(nc.vector.scalar_tensor_tensor(out=g.x[:, i, :],
                                                                 in0=xr[:, i, :] if src is None else src,
                                                                 scalar=r.near[:, i, a:a + 1], in1=g.x[:, i, :],
                                                                 op0=ALU.mult, op1=ALU.add))
                        c.wait()
                for q in range(NT // GRP):
                    dve.wait_ge(gathered[q], 16 * GRP * top)
                    for k in range(top):
                        for i in range(q * GRP, (q + 1) * GRP):
                            c.add(nc.vector.scalar_tensor_tensor(out=g.x[:, i, :], in0=gb[:, k, i, :],
                                                                 scalar=r.w[:, k, i:i + 1], in1=g.x[:, i, :],
                                                                 op0=ALU.mult, op1=ALU.add))
                        c.wait()


def grouped(nc, g, t, disp, ybuf, r):
    NJ = TILES1
    with section(nc, "grouped", "w_in", "x_in0", "x_in1", "turned", "xt_ready", "ab_ready", "a_ready", "h_ready",
                 "ht_turned", "ht_ready", "y_ready", "y_out", "stored0", "stored1") as s:
        w13 = s.sb("w13", [P, E1, 2 * H1])
        w2 = s.sb("w2", [P, E1, len(H1_CUTS) * D])
        xin = s.sb("xin", [P, 2, D])
        xt = s.sb("xt", [P, 2, P])
        a = s.sb("a", [P, 2, H1])
        h = s.sb("h", [P, 2, H1])
        ht = s.sb("ht", [P, 2, len(H1_CUTS), P])
        yo = s.sb("yo", [P, 2, D])
        x_in, stored = (s.x_in0, s.x_in1), (s.stored0, s.stored1)

        def each(eng, body):
            body(0, 0, 0, 0, 2)
            body(1, 0, 1, 1, 2)
            with eng.Fori(1, NJ // 2 - 1) as it:
                for p in range(2):
                    body(it * 2 + p, it, p, 2, 2)
            body(NJ - 2, NJ // 2 - 1, 0, 2, 1)
            body(NJ - 1, NJ // 2 - 1, 1, 2, 0)

        with nc.Block() as block:

            @block.sync
            def _(sp):
                sp.dma_start(w13[:], t["f1_w13"]).then_inc(s.w_in, 16)
                sp.dma_start(w2[:], t["f1_w2"]).then_inc(s.w_in, 16)

                def body(j, it, p, before, after):
                    sp.wait_ge(s.turned, j + 1)
                    sp.dma_start(xin[:, p, :], disp[bass.ds(j * P, P), :]).then_inc(x_in[p], 16)
                each(sp, body)

            @block.tensor
            def _(pe):
                pe.sem_inc(s.turned, 2)
                pe.wait_ge(s.w_in, 32)

                def tile_expert(j):
                    return pe.value_load(r.tile_e[0:1, bass.ds(j, 1)], min_val=0, max_val=E1 - 1)

                def transpose(j, turn, p):
                    pe.wait_ge(x_in[p], (turn + 1) * 16)
                    pe.wait_ge(s.y_out, j - 1)
                    nc.tensor.transpose(g.ps[:, 4 * p, 0:P], xin[:, p, :], g.ident[:]).then_inc(s.turned, 1)

                def up(j, p):
                    e = tile_expert(j)
                    pe.wait_ge(s.xt_ready, j + 1)
                    pe.wait_ge(s.h_ready, j + 1)
                    for m in range(2):
                        ins = nc.tensor.matmul(g.ps[:, 4 * p + 1 + m, 0:H1], xt[:, p, :],
                                               rows(w13[:, bass.ds(e, 1), m * H1:(m + 1) * H1]), start=True, stop=True)
                    ins.then_inc(s.ab_ready, 1)

                def down(j, p):
                    e = tile_expert(j)
                    pe.wait_ge(s.ht_ready, j + 3)
                    pe.wait_ge(s.y_out, j + 1)
                    for c, (lo, n) in enumerate(H1_CUTS):
                        ins = nc.tensor.matmul(g.ps[:, 4 * p, P:2 * P], ht[0:n, p, c, :],
                                               rows(w2[0:n, bass.ds(e, 1), c * D:(c + 1) * D]),
                                               start=(c == 0), stop=(c == len(H1_CUTS) - 1))
                    ins.then_inc(s.y_ready, 1)

                def body(j, it, p, before, after):
                    if after >= 1:
                        up(j + 1, 1 - p)
                    if after >= 2:
                        transpose(j + 2, it + 1, p)
                    pe.wait_ge(s.h_ready, j + 3)
                    pe.wait_ge(s.ht_ready, j + 1)
                    for c, (lo, n) in enumerate(H1_CUTS):
                        ins = nc.tensor.transpose(g.ps[0:n, 4 * p + 3, c * P:(c + 1) * P], h[:, p, lo:lo + n],
                                                  g.ident[:])
                    ins.then_inc(s.ht_turned, 1)
                    if before >= 1:
                        down(j - 1, 1 - p)

                pe.wait_ge(x_in[0], 16)
                nc.tensor.transpose(g.ps[:, 0, 0:P], xin[:, 0, :], g.ident[:]).then_inc(s.turned, 1)
                pe.wait_ge(x_in[1], 16)
                nc.tensor.transpose(g.ps[:, 4, 0:P], xin[:, 1, :], g.ident[:]).then_inc(s.turned, 1)
                up(0, 0)
                each(pe, body)
                down(NJ - 1, 1)

            @block.scalar
            def _(act):
                nc.scalar.preload_act_table(ACT.Silu)
                act.sem_inc(s.ht_ready, 2)

                def silu(j, p):
                    act.wait_ge(s.ab_ready, j + 1)
                    act.wait_ge(s.h_ready, j + 1)
                    nc.scalar.activation(a[:, p, :], g.ps[:, 4 * p + 1, 0:H1], ACT.Silu).then_inc(s.a_ready, 1)

                def body(j, it, p, before, after):
                    if after >= 1:
                        silu(j + 1, 1 - p)
                    act.wait_ge(s.ht_turned, j + 1)
                    if before >= 2:
                        act.wait_ge(s.y_ready, j - 1)
                    n = H1_CUTS[-1][1]
                    nc.scalar.copy(ht[:, p, 0:2, :], g.ps[:, 4 * p + 3, 0:2 * P].rearrange("p (c t) -> p c t", c=2))
                    nc.scalar.copy(ht[0:n, p, 2, :], g.ps[0:n, 4 * p + 3, 2 * P:3 * P]).then_inc(s.ht_ready, 1)
                silu(0, 0)
                each(act, body)

            @block.vector
            def _(dve):
                dve.sem_inc(s.y_out, 2)
                dve.sem_inc(s.h_ready, 2)

                def take(j, p):
                    dve.wait_ge(s.turned, j + 3)
                    nc.vector.tensor_copy(xt[:, p, :], g.ps[:, 4 * p, 0:P]).then_inc(s.xt_ready, 1)

                def gated(j, p, reader):
                    dve.wait_ge(s.a_ready, j + 1)
                    if reader:
                        dve.wait_ge(s.ht_turned, j - 1)
                    nc.vector.tensor_tensor(h[:, p, :], g.ps[:, 4 * p + 2, 0:H1], a[:, p, :],
                                            ALU.mult).then_inc(s.h_ready, 1)

                def give(j, turn, p):
                    dve.wait_ge(s.y_ready, j + 1)
                    if not isinstance(turn, int) or turn:
                        dve.wait_ge(stored[p], turn * 16)
                    nc.vector.tensor_copy(yo[:, p, :], g.ps[:, 4 * p, P:2 * P]).then_inc(s.y_out, 1)

                def body(j, it, p, before, after):
                    if before >= 2:
                        give(j - 2, it - 1, p)
                    if after >= 2:
                        take(j + 2, p)
                    if after >= 1:
                        gated(j + 1, 1 - p, before >= 1)
                take(0, 0)
                take(1, 1)
                gated(0, 0, False)
                each(dve, body)
                give(NJ - 2, NJ // 2 - 1, 0)
                give(NJ - 1, NJ // 2 - 1, 1)

            @block.gpsimd
            def _(pool):
                def body(j, it, p, before, after):
                    pool.wait_ge(s.y_out, j + 3)
                    pool.dma_start(ybuf[bass.ds(j * P, P), :], yo[:, p, :]).then_inc(stored[p], 16)
                each(pool, body)
                for p in range(2):
                    pool.wait_ge(stored[p], NJ // 2 * 16)


def layer1(nc, g, t):
    with ExitStack() as c:
        r = Names()
        r.rows_i = c.enter_context(nc.sbuf_tensor("rows1", [P, 2, NT], I32))
        r.scat_i = c.enter_context(nc.sbuf_tensor("places1", [P, 2, NT], I32))
        r.w = c.enter_context(nc.sbuf_tensor("w1", [P, 2, NT], F32))
        r.tile_e = c.enter_context(nc.sbuf_tensor("tile_e", [1, TILES1], I32))
        disp = nc.dram_tensor("disp1", (TILES1 * P, D), F32, kind="Internal").ap()
        ybuf = nc.dram_tensor("ybuf1", (TILES1 * P, D), F32, kind="Internal").ap()
        qp = nc.dram_tensor("q1_parts", (3, D, N), BF16, kind="Internal").ap()
        kp = nc.dram_tensor("k1_parts", (3, D, N), BF16, kind="Internal").ap()
        route(nc, g, t, "route1", g.xn, g.xn_t, "f1_gate", E1, 2, None, 0, disp, r)
        project_parts(nc, g, t, "qk1", t["a1_wq"], t["a1_bq"], t["a1_wk"], t["a1_bk"], qp, kp,
                      lambda pool, done: scatter(nc, pool, done, g.xn, disp, r, 2))
        grouped(nc, g, t, disp, ybuf, r)
        gb = c.enter_context(nc.sbuf_tensor("gathered", [P, 2, NT, D], F32))
        attention(nc, g, "att1", t["a1_wv"], t["a1_bv"], t["a1_wo"], t["a1_bo"], qp, kp, True, HD ** -0.5,
                  lambda pool, done: gather(nc, pool, done, gb, ybuf, r, 2))
        add_results(nc, g, "add1", gb, r, 2)


def layer3(nc, g, t):
    with ExitStack() as c:
        r = Names()
        r.rows_i = c.enter_context(nc.sbuf_tensor("rows3", [P, 1, NT], I32))
        r.scat_i = c.enter_context(nc.sbuf_tensor("places3", [P, 1, NT], I32))
        r.w = c.enter_context(nc.sbuf_tensor("w3", [P, 1, NT], F32))
        disp = nc.dram_tensor("disp3", (E3 * CAP3, D), F32, kind="Internal").ap()
        ybuf = nc.dram_tensor("ybuf3", (E3 * CAP3, D), F32, kind="Internal").ap()
        route(nc, g, t, "route3", g.xn, g.xn_t, "f3_gate", E3, 1, CAP3, 0, disp, r)
        attn3(nc, g, t, lambda pool, done: scatter(nc, pool, done, g.xn, disp, r, 1))
        experts(nc, g, t, "mlp3", "f3_packed", E3, CAP3, disp, ybuf, ACT.Relu)
        combine(nc, g, t, "comb3", ybuf, 1, r)


def project_parts(nc, g, t, title, wq, bq, wk, bk, q_parts, k_parts, pool_job=None):
    CH = 512
    NCH = N // CH
    with section(nc, title, "w_in", "mm_ready", "y_done", "high_done", "rem_done", "mid_done", "low_done", "stored0",
                 "stored1", "job_done") as s:
        w = s.sb("w", [P, 2, D])
        b = s.sb("b", [P, 2])
        y = s.sb("y", [P, 2, 2, CH])
        rem = s.sb("rem", [P, 2, 2, CH])
        parts = s.sb("parts", [P, 2, 3, 2, CH], BF16)
        stored = (s.stored0, s.stored1)

        with nc.Block() as block:

            @block.sync
            def _(sp):
                for i, (wn, bn) in enumerate(((wq, bq), (wk, bk))):
                    sp.dma_start(w[:, i, :], wn).then_inc(s.w_in, 16)
                    sp.dma_start(b[:, i:i + 1], bn).then_inc(s.w_in, 16)
                with sp.Fori(0, NCH // 2) as it:
                    for p in range(2):
                        at = sp.snap((it * 2 + p) * CH)
                        sp.wait_ge(s.low_done, it * 2 + p + 1)
                        for m, out in ((0, q_parts), (1, k_parts)):
                            sp.dma_start(out[:, :, bass.ds(at, CH)].rearrange("a r t -> r a t"),
                                         parts[:, p, :, m]).then_inc(stored[p], 16)
                for p in range(2):
                    sp.wait_ge(stored[p], NCH // 2 * 32)

            @block.gpsimd
            def _(pool):
                if pool_job:
                    pool_job(pool, s.job_done)

            @block.tensor
            def _(pe):
                pe.wait_ge(s.w_in, 64)
                pe.sem_inc(s.y_done, 2)

                def stage(ch, turn, p, now, prev):
                    if now:
                        pe.wait_ge(s.y_done, ch + 1)
                        for m in range(2):
                            ins = nc.tensor.matmul(g.ps[:, 2 * p + m, :], w[:, m, :], g.xn_t[:, bass.ds(ch * CH, CH)],
                                                   start=True, stop=True)
                        ins.then_inc(s.mm_ready, 1)
                in_turn(pe, NCH, stage)

            @block.vector
            def _(dve):
                dve.wait_ge(s.w_in, 64)

                def stage(ch, turn, p, now, prev):
                    if now:
                        dve.wait_ge(s.mm_ready, ch + 1)
                        for m in range(2):
                            ins = nc.vector.tensor_scalar(y[:, p, m, :], g.ps[:, 2 * p + m, :], b[:, m:m + 1], None,
                                                          ALU.add)
                        ins.then_inc(s.y_done, 1)
                    if prev:
                        dve.wait_ge(s.mid_done, ch)
                        nc.vector.tensor_tensor(parts[:, 1 - p, 2], rem[:, 1 - p], parts[:, 1 - p, 1],
                                                ALU.subtract).then_inc(s.low_done, 1)
                    if now:
                        dve.wait_ge(s.high_done, ch + 1)
                        nc.vector.tensor_tensor(rem[:, p], y[:, p], parts[:, p, 0], ALU.subtract
                                                ).then_inc(s.rem_done, 1)
                in_turn(dve, NCH, stage)

            @block.scalar
            def _(act):
                def stage(ch, turn, p, now, prev):
                    if now:
                        if not isinstance(turn, int):
                            act.wait_ge(stored[p], turn * 32)
                        act.wait_ge(s.y_done, ch + 3)
                        nc.scalar.copy(parts[:, p, 0], y[:, p]).then_inc(s.high_done, 1)
                        act.wait_ge(s.rem_done, ch + 1)
                        nc.scalar.copy(parts[:, p, 1], rem[:, p]).then_inc(s.mid_done, 1)
                in_turn(act, NCH, stage)


def attention(nc, g, title, wv, bv, wo, bo, q_parts, k_parts, causal, scale, pool_job=None):
    NB = 3 if causal else 4
    H = HEADS
    QH = P // 4
    NG = H // 4
    RING = 4
    AHEAD = 2
    FIRST_MAX = 5
    SPREADS = (0, 2, 4)
    PROJECTION = 5
    with section(nc, title, "w_in", "filled", "consts", "qk_in00", "qk_in01", "qk_in10", "qk_in11",
                 "xb_ready", "v_ready", "vx_ready",
                 "m_ready", "m_taken", "m_step", "nm_ready", "turned_nm", "nmt_ready", "s_ready", "p_ready",
                 "o_taken", "job_done", "r_ready", "r_step", "r_done", "out_ready", "out_done", "pv_done") as s:
        wv_s = s.sb("wv", [P, D])
        wo_s = s.sb("wo", [P, NG, D])
        bv_s = s.sb("bv", [1, D])
        bo_s = s.sb("bo", [1, D])
        qs = s.sb("qs", [P, 2, H, T], BF16)
        ks = s.sb("ks", [P, 2, H, T], BF16)
        xb = s.sb("xb", [P, T])
        vx = s.sb("vx", [P, 2, QT, H, QH])
        mb = s.sb("mb", [P, H, 3 if causal else 2])
        m = s.sb("m", [P, QT, H])
        m2 = s.sb("m2", [P, QT, 2, H], BF16)
        mt = s.sb("mt", [P, 2, T], BF16)
        pr = s.sb("pr", [P, RING, NB * P])
        den_sel = s.sb("den_sel", [P, P])
        ot = s.sb("ot", [P, NG, T])
        rc = s.sb("rc", [P, 2, T])
        otn = s.sb("otn", [P, NG, T])
        qk_in = ((s.qk_in00, s.qk_in01), (s.qk_in10, s.qk_in11))
        QK_IN = 9 * 16
        HALF = BATCH // 2
        FILLS = 5

        def each(eng, stage):
            stage(-1, 0, 1, False, True, False)
            stage(0, 0, 0, True, True, False)
            stage(1, 1, 1, True, True, True)
            with eng.Fori(1, HALF - 1) as it:
                for p in range(2):
                    stage(it * 2 + p, it + p, p, True, True, True)
            stage(BATCH - 2, HALF - 1, 0, True, True, True)
            stage(BATCH - 1, 0, 1, True, False, True)
            stage(BATCH, 0, 0, False, False, True)

        def s_bank(h):
            return 2 + h % 3

        def o_bank(gi):
            return 5 + gi % 2

        with nc.Block() as block:

            @block.sync
            def _(sp):
                for dst, src in ((wv_s, wv), (wo_s, wo), (bv_s, bv), (bo_s, bo)):
                    sp.dma_start(dst[:], src).then_inc(s.w_in, 16)

                def load(at, p, half):
                    tok, hs = bass.ds(at, T), slice(half * H // 2, (half + 1) * H // 2)
                    for row, part, n in ((0, 0, 3), (3, 0, 2), (5, 0, 1)):
                        sp.dma_start(qs[row * HD:(row + n) * HD, p, hs], q_parts[part:part + n, :, tok].rearrange(
                            "a (d h) t -> (a d) h t", h=H)[:, hs]).then_inc(qk_in[p][half], 16)
                    for row, part, n in ((0, 0, 3), (3, 1, 2), (5, 2, 1)):
                        for i in range(n):
                            sp.dma_start(ks[(row + i) * HD:(row + i + 1) * HD, p, hs],
                                         k_parts[part, :, tok].rearrange("(d h) t -> d h t", h=H)[:, hs]
                                         ).then_inc(qk_in[p][half], 16)

                sp.wait_ge(s.filled, FILLS)
                for p in range(2):
                    for half in range(2):
                        load(p * T, p, half)
                with sp.Fori(0, HALF - 1) as it:
                    for p in range(2):
                        at = sp.snap((it * 2 + p + 2) * T)
                        for half in range(2):
                            sp.wait_ge(s.s_ready, (it * 2 + p) * H + (half + 1) * H // 2)
                            load(at, p, half)

            @block.gpsimd
            def _(pool):
                for b in (vx, mt):
                    nc.gpsimd.memset(b[:], 0.0).then_inc(s.filled, 1)
                nc.gpsimd.memset(den_sel[:], 0.0).then_inc(s.filled, 1)
                pool.wait_ge(s.filled, FILLS)
                nc.gpsimd.memset(vx[:, :, :, :, HD:HD + 1], 1.0).then_inc(s.consts, 1)
                v = den_sel[:].rearrange("p (r i) -> p r i", i=QH)
                nc.gpsimd.affine_select(out=v, in_=v, compare_op=ALU.not_equal, fill=1.0, base=-HD,
                                        pattern=[[-QH, 4], [0, QH]], channel_multiplier=1).then_inc(s.consts, 1)
                if pool_job:
                    pool_job(pool, s.job_done)

            @block.tensor
            def _(pe):
                pe.wait_ge(s.w_in, 64)
                pe.wait_ge(s.consts, 2)
                pe.sem_inc(s.pv_done, RING)

                def maximum(nb, p, h):
                    pe.wait_ge(s.m_taken, nb * H + h + 1)
                    bank = h % 2
                    if causal:
                        runs = ((0, 0, P), (1, P, 3 * P))
                    else:
                        runs = ((0, 0, T), (1, T, 2 * T))
                    for q, lo, hi in runs:
                        ins = nc.tensor.matmul(g.ps[:, bank, lo:hi], qs[:, p, h, q * P:(q + 1) * P],
                                               ks[:, p, h, 0:hi - lo], start=True, stop=not causal)
                        if causal:
                            ins = nc.tensor.matmul(g.ps[:, bank, hi - P:hi], g.ident_b[:], g.future_q[:],
                                                   start=False, stop=True)
                    ins.then_inc(s.m_ready, 1)

                def scores(b, p, h):
                    pe.wait_ge(s.p_ready, b * H + max(h + 1, 3))
                    for k in range(QT):
                        q0 = k * P if causal else 0
                        out = g.ps[:, s_bank(h), k * T:k * T + T - q0]
                        nc.tensor.matmul(out, ks[:, p, h, k * P:(k + 1) * P], qs[:, p, h, q0:T],
                                         start=True, stop=False)
                        ins = nc.tensor.matmul(out, g.head_sel[:, h, :], mt[:, p, q0:T], start=False,
                                               stop=not causal)
                        if causal:
                            ins = nc.tensor.matmul(g.ps[:, s_bank(h), k * T:k * T + P], g.ident_b[:],
                                                   g.after_neg[:], start=False, stop=True)
                    ins.then_inc(s.s_ready, 1)

                def values(b, p, h):
                    gi, r = h // 4, h % 4
                    if r == 0:
                        pe.wait_ge(s.o_taken, b * NG + gi + 1)
                    pe.wait_ge(s.p_ready, b * H + h + 4)
                    for k in range(QT):
                        q0 = k * P if causal else 0
                        ins = nc.tensor.matmul(g.ps[r * QH:(r + 1) * QH, o_bank(gi), q0:T], vx[:, p, k, h, :],
                                               pr[:, h % RING, k * T:k * T + T - q0],
                                               start=(k == 0), stop=(k == QT - 1))
                    ins.then_inc(s.pv_done, 1)

                def spread(b, gi):
                    pe.wait_ge(s.o_taken, b * NG + gi + 3)
                    nc.tensor.matmul(g.ps[:, 7, 0:T], den_sel[:], ot[:, gi, :], start=True,
                                     stop=True).then_inc(s.r_ready, 1)

                def stage(b, loads, p, now, ahead, prev):
                    nb, np_ = b + 1, 1 - p
                    for h in range(H):
                        if ahead and h in (FIRST_MAX, FIRST_MAX + H // 4):
                            pe.wait_ge(qk_in[np_][h // (FIRST_MAX + 1)], (loads + 1) * QK_IN)
                        if ahead and FIRST_MAX <= h < FIRST_MAX + H // 2:
                            for i in range(2):
                                maximum(nb, np_, 2 * (h - FIRST_MAX) + i)
                        if now:
                            if h == 0:
                                pe.wait_ge(s.nmt_ready, nb)
                            scores(b, p, h)
                        if prev and h < AHEAD:
                            values(b - 1, 1 - p, H - AHEAD + h)
                        if now and h >= AHEAD:
                            values(b, p, h - AHEAD)
                        if prev and h in SPREADS:
                            pe.wait_ge(s.r_step, b * NG - 3 + SPREADS.index(h))
                            spread(b - 1, 1 + SPREADS.index(h))
                        if prev and h == PROJECTION:
                            pe.wait_ge(s.r_done, b * NG)
                            for q in range(QT):
                                for gi in range(NG):
                                    nc.tensor.matmul(g.ps[:, 7, q * D:(q + 1) * D], otn[:, gi, q * P:(q + 1) * P],
                                                     wo_s[:, gi, :], start=(gi == 0), stop=False)
                                ins = nc.tensor.matmul(g.ps[:, 7, q * D:(q + 1) * D], g.ones_row[:], bo_s[:],
                                                       start=False, stop=True)
                            ins.then_inc(s.out_ready, 1)
                        if ahead and h == 10:
                            pe.wait_ge(s.xb_ready, nb + 1)
                            if prev:
                                pe.wait_ge(s.out_done, b)
                            for k in range(QT):
                                nc.tensor.matmul(g.ps[:, 7, k * D:(k + 1) * D], xb[:, k * P:(k + 1) * P], wv_s[:],
                                                 start=True, stop=False)
                                ins = nc.tensor.matmul(g.ps[:, 7, k * D:(k + 1) * D], g.ones_row[:], bv_s[:],
                                                       start=False, stop=True)
                            ins.then_inc(s.v_ready, 1)
                        if ahead and h == 13:
                            pe.wait_ge(s.nm_ready, nb + 1)
                            pe.wait_ge(s.vx_ready, nb + 1)
                            for q in range(QT):
                                ins = nc.tensor.matmul(g.ps[0:2 * H, 7, q * P:(q + 1) * P],
                                                       m2[:, q].rearrange("p a h -> p (a h)"), g.ident_b[:],
                                                       start=True, stop=True)
                            ins.then_inc(s.turned_nm, 1)
                        if now and h == 14:
                            if ahead:
                                pe.wait_ge(s.nmt_ready, nb + 1)
                            elif prev:
                                pe.wait_ge(s.out_done, b)
                            spread(b, 0)
                each(pe, stage)

            @block.scalar
            def _(act):
                nc.scalar.preload_act_table(ACT.Exp)
                act.sem_inc(s.p_ready, 3)
                nc.scalar.copy(xb[:], g.xn_t[:, 0:T]).then_inc(s.xb_ready, 1)

                def stage(b, loads, p, now, ahead, prev):
                    nb, np_ = b + 1, 1 - p
                    for h in range(H):
                        if now:
                            act.wait_ge(s.s_ready, b * H + h + 1)
                            act.wait_ge(s.pv_done, b * H + h + 1)
                            nc.scalar.activation(pr[:, h % RING], g.ps[:, s_bank(h), 0:NB * P], ACT.Exp,
                                                 scale=scale).then_inc(s.p_ready, 1)
                        if ahead and h == 11:
                            act.wait_ge(s.v_ready, nb + 1)
                            nxt = min(nb + 1, BATCH - 1) if isinstance(nb, int) else nb + 1
                            nc.scalar.copy(xb[:], g.xn_t[:, bass.ds(nxt * T, T)]).then_inc(s.xb_ready, 1)
                        if ahead and h == 13:
                            act.wait_ge(s.turned_nm, nb + 1)
                            nc.scalar.copy(mt[0:2 * H, np_, :], g.ps[0:2 * H, 7, 0:T]).then_inc(s.nmt_ready, 1)
                each(act, stage)

            @block.vector
            def _(dve):
                v = nc.vector
                v.memset(qs[:], 0.0).then_inc(s.filled, 1)
                v.memset(ks[:], 0.0).then_inc(s.filled, 1)
                dve.sem_inc(s.m_taken, 2)
                dve.sem_inc(s.o_taken, 2)
                dve.wait_ge(s.consts, 2)

                def take(b, gi):
                    dve.wait_ge(s.pv_done, b * H + 4 * gi + 4 + RING)
                    v.tensor_copy(ot[:, gi, :], g.ps[:, o_bank(gi), 0:T]).then_inc(s.o_taken, 1)

                def norm(b, gi):
                    dve.wait_ge(s.r_ready, b * NG + gi + 1)
                    v.reciprocal(rc[:, gi % 2, :], g.ps[:, 7, 0:T]).then_inc(s.r_step, 1)
                    dve.wait_ge(s.r_step, b * NG + gi + 1)
                    v.tensor_tensor(otn[:, gi, :], ot[:, gi, :], rc[:, gi % 2, :], ALU.mult).then_inc(s.r_done, 1)

                def reduce(nb, h):
                    dve.wait_ge(s.m_ready, nb * H + h + 1)
                    w = P if causal else T
                    v.tensor_reduce(mb[:, h, :], g.ps[:, h % 2, 0:NB * P].rearrange("p (n k) -> p n k", k=w),
                                    AX_X, ALU.max).then_inc(s.m_taken, 1)

                def stage(b, loads, p, now, ahead, prev):
                    nb, np_ = b + 1, 1 - p
                    for h in range(H):
                        if prev and h == 2:
                            take(b - 1, 3)
                        if prev and h in SPREADS:
                            norm(b - 1, 1 + SPREADS.index(h))
                        if ahead and FIRST_MAX <= h < FIRST_MAX + H // 2:
                            for i in range(2):
                                reduce(nb, 2 * (h - FIRST_MAX) + i)
                        if now and h in (5, 9, 13):
                            take(b, h // 4 - 1)
                        if prev and h == PROJECTION:
                            dve.wait_ge(s.out_ready, b)
                            xs = g.x[:, bass.ds((b - 1) * QT, QT), :]
                            v.tensor_tensor(xs, xs, g.ps[:, 7, 0:QT * D].rearrange("p (k d) -> p k d", k=QT),
                                            ALU.add).then_inc(s.out_done, 1)
                        if now and h == 14:
                            norm(b, 0)
                        if ahead and h == 10:
                            dve.wait_ge(s.v_ready, nb + 1)
                            v.tensor_copy(vx[:, np_, :, :, 0:HD],
                                          g.ps[:, 7, 0:QT * D].rearrange("p (k h d) -> p k h d", k=QT, h=H)
                                          ).then_inc(s.vx_ready, 1)
                        if ahead and h == 13:
                            dve.wait_ge(s.m_taken, (nb + 1) * H + 2)
                            top = mb[:].rearrange("p h q -> p q h")
                            c = Chain(dve, s.m_step, nb * (3 if causal else 1))
                            if causal:
                                c.add(v.tensor_copy(m[:, 0, :], mb[:, :, 0]))
                                c.step(v.tensor_tensor(m[:, 1, :], mb[:, :, 1], mb[:, :, 2], ALU.max))
                                top = m[:]
                            c.step(v.tensor_copy(m2[:, :, 0, :], top))
                            v.tensor_tensor(m2[:, :, 1, :], top, m2[:, :, 0, :], ALU.subtract).then_inc(s.nm_ready, 1)
                each(dve, stage)


def lora_mix(nc, g, t, m, which, wt, b, out_w, out_b):
    LORA_SCALE = 2.0
    with section(nc, "lora_" + which, "in_done", "mm_done", "mixed", "taken") as s:
        a = s.sb("a", [P, 2, P])
        bb = s.sb("b", [P, 2, P])
        eye = s.sb("eye", [P, P])
        mix = s.sb("mix", [P, P])
        w = s.sb("w", [P, P])
        bi = s.sb("bi", [P, 1])
        with nc.Block() as block:

            @block.sync
            def _(sp):
                for dst, src in ((a, t[m + "_a"]), (bb, t[m + "_b"]), (eye, t[m + "_eye"]), (w, wt), (bi, b)):
                    sp.dma_start(dst[:], src).then_inc(s.in_done, 16)

            @block.tensor
            def _(pe):
                pe.wait_ge(s.in_done, 80)
                for c in range(2):
                    ins = nc.tensor.matmul(g.ps[:, 0, 0:P], a[:, c, :], bb[:, c, :], start=(c == 0), stop=(c == 1))
                ins.then_inc(s.mm_done, 1)
                pe.wait_ge(s.mixed, 1)
                nc.tensor.matmul(g.ps[:, 1, 0:P], w[:], mix[:], start=True, stop=True)
                if which == "q":
                    ins = nc.tensor.matmul(g.ps[:, 2, 0:1], mix[:], bi[:], start=True, stop=True)
                else:
                    ins = nc.tensor.matmul(g.ps[0:1, 2, 0:P], bi[:], mix[:], start=True, stop=True)
                ins.then_inc(s.mm_done, 1)

            @block.vector
            def _(dve):
                dve.wait_ge(s.mm_done, 1)
                nc.vector.scalar_tensor_tensor(out=mix[:], in0=g.ps[:, 0, 0:P], scalar=LORA_SCALE, in1=eye[:],
                                               op0=ALU.mult, op1=ALU.add).then_inc(s.mixed, 1)
                dve.wait_ge(s.mm_done, 2)
                nc.vector.tensor_copy(out_w, g.ps[:, 1, 0:P]).then_inc(s.taken, 1)
                nc.vector.tensor_copy(out_b, g.ps[:, 2, 0:1] if which == "q" else g.ps[0:1, 2, 0:P]
                                      ).then_inc(s.taken, 1)
                dve.wait_ge(s.taken, 2)


def attn2(nc, g, t):
    qp = nc.dram_tensor("q2_parts", (3, D, N), BF16, kind="Internal").ap()
    kp = nc.dram_tensor("k2_parts", (3, D, N), BF16, kind="Internal").ap()
    with ExitStack() as c:
        wq = c.enter_context(nc.sbuf_tensor("wq2", [P, D], F32))
        wv = c.enter_context(nc.sbuf_tensor("wv2", [P, D], F32))
        bq = c.enter_context(nc.sbuf_tensor("bq2", [P, 1], F32))
        bv = c.enter_context(nc.sbuf_tensor("bv2", [1, D], F32))
        lora_mix(nc, g, t, "lq", "q", t["a2_wq_t"], t["a2_bq"], wq[:], bq[:])
        lora_mix(nc, g, t, "lv", "v", t["a2_wv_t"], t["a2_bv"], wv[:], bv[:])
        project_parts(nc, g, t, "qk2", wq[:], bq[:], t["a2_wk"], t["a2_bk"], qp, kp)
        attention(nc, g, "att2", wv[:], bv[:], t["a2_wo"], t["a2_bo"], qp, kp, False, HD ** -0.5)


def ffn2(nc, g, t):
    MB, RUN, H = 2, N // 2 // E2, FC
    C = MB * RUN
    W2, B1, B2, WN = FC * P, 2 * FC * P, 2 * FC * P + FC, 2 * FC * P + FC + 1
    with ExitStack() as ctx:
        x2 = ctx.enter_context(nc.sbuf_tensor("x2", [P, NT, D], F32))
        x2_t = ctx.enter_context(nc.sbuf_tensor("x2_t", [P, N], F32))
        normalise(nc, g, "ln2", g.xn, x2, x2_t, "ln", t["f2_g"], t["f2_b"])
        with section(nc, "mlp2", "c_in", "w_in0", "w_in1", "a_ready", "xa_ready", "h_ready", "act_done", "y_ready",
                     "yt_ready", "z_ready", "z_done", "x_done") as s:
            aw = s.sb("aw", [P, D])
            nw = s.sb("nw", [P, D])
            ab = s.sb("ab", [P, 1])
            nb = s.sb("nb", [1, D])
            w = s.sb("w", [P, 2, WN])
            xa = s.sb("xa", [P, 2, C])
            ht = s.sb("ht", [P, FC, C])
            yt = s.sb("yt", [P, C])
            z = s.sb("z", [P, MB, RUN // P, D])
            w_in = (s.w_in0, s.w_in1)

            def run_of(ap, e):
                return ap.rearrange("p (m t) -> p m t", m=MB)[:, :, bass.ds(e * RUN, RUN)]

            def each(eng, body):
                with eng.Fori(0, E2 // 2 - 1) as it:
                    for p in range(2):
                        body(it * 2 + p, it, p, False)
                body(E2 - 2, E2 // 2 - 1, 0, False)
                body(E2 - 1, E2 // 2 - 1, 1, True)

            with nc.Block() as block:

                @block.sync
                def _(sp):
                    for dst, src in ((aw, "f2_aw"), (nw, "f2_nw"), (ab, "f2_ab"), (nb, "f2_nb")):
                        sp.dma_start(dst[:], t[src]).then_inc(s.c_in, 16)

                    def body(e, it, p, last):
                        sp.wait_ge(s.yt_ready, e + 1)
                        sp.dma_start(w[:, p], t["f2_packed"][bass.ds(e, 1)].rearrange("a p n -> (a p) n")
                                     ).then_inc(w_in[p], 16)
                    each(sp, body)

                @block.tensor
                def _(pe):
                    pe.wait_ge(s.c_in, 64)

                    def attend(e):
                        pe.wait_ge(s.xa_ready, e)
                        nc.tensor.matmul(g.ps[:, 0, 0:C].rearrange("p (m t) -> p m t", m=MB), aw[:],
                                         run_of(x2_t[:], e), start=True, stop=True).then_inc(s.a_ready, 1)

                    def body(e, it, p, last):
                        pe.wait_ge(w_in[p], (it + 1) * 16)
                        pe.wait_ge(s.xa_ready, e + 1)
                        pe.wait_ge(s.act_done, e * H)
                        for f in range(FC):
                            nc.tensor.matmul(g.ps[:, 1 + f, 0:C], w[:, p, f * P:(f + 1) * P], xa[:, p, :],
                                             start=True, stop=True).then_inc(s.h_ready, 1)
                        if not last:
                            attend(e + 1)
                        pe.wait_ge(s.yt_ready, e + 2)
                        for f in range(FC):
                            pe.wait_ge(s.act_done, e * H + f + 1)
                            ins = nc.tensor.matmul(g.ps[:, 5, 0:C], w[:, p, W2 + f * P:W2 + (f + 1) * P], ht[:, f, :],
                                                   start=(f == 0), stop=(f == FC - 1))
                        ins.then_inc(s.y_ready, 1)
                        pe.wait_ge(s.yt_ready, e + 3)
                        pe.wait_ge(s.z_done, e)
                        for k in range(C // P):
                            out = g.ps[:, 6, k * D:(k + 1) * D]
                            nc.tensor.matmul(out, yt[:, k * P:(k + 1) * P], nw[:], start=True, stop=False)
                            ins = nc.tensor.matmul(out, g.ones_row[:], nb[:], start=False, stop=True)
                        ins.then_inc(s.z_ready, 1)
                    attend(0)
                    each(pe, body)

                @block.scalar
                def _(act):
                    nc.scalar.preload_act_table(ACT.Gelu)

                    def body(e, it, p, last):
                        act.wait_ge(s.y_ready, e)
                        for f in range(FC):
                            act.wait_ge(s.h_ready, e * H + f + 1)
                            nc.scalar.activation(ht[:, f, :], g.ps[:, 1 + f, 0:C], ACT.Gelu,
                                                 bias=w[:, p, B1 + f:B1 + f + 1]).then_inc(s.act_done, 1)
                        act.wait_ge(s.z_ready, e + 1)
                        act.wait_ge(s.x_done, e)
                        nc.scalar.activation(z[:].rearrange("p m k d -> p (m k d)"), g.ps[:, 6, 0:C],
                                             ACT.Gelu).then_inc(s.z_done, 1)
                    each(act, body)

                @block.vector
                def _(dve):
                    dve.wait_ge(s.c_in, 64)
                    dve.sem_inc(s.yt_ready, 2)

                    def take(e, p):
                        dve.wait_ge(s.a_ready, e + 1)
                        nc.vector.scalar_tensor_tensor(
                            out=xa[:, p].rearrange("p (m t) -> p m t", m=MB),
                            in0=g.ps[:, 0, 0:C].rearrange("p (m t) -> p m t", m=MB), scalar=ab[:],
                            in1=run_of(g.xn_t[:], e), op0=ALU.add, op1=ALU.add).then_inc(s.xa_ready, 1)

                    def body(e, it, p, last):
                        if not last:
                            take(e + 1, 1 - p)
                        dve.wait_ge(s.y_ready, e + 1)
                        dve.wait_ge(s.z_ready, e)
                        nc.vector.tensor_scalar(yt[:], g.ps[:, 5, 0:C], w[:, p, B2:B2 + 1], None,
                                                ALU.add).then_inc(s.yt_ready, 1)
                        dve.wait_ge(s.z_done, e + 1)
                        xs = g.x[:].rearrange("p (m t) d -> p m (t d)", m=MB)[:, :, bass.ds(e * RUN, RUN)]
                        nc.vector.tensor_tensor(xs, xs, z[:].rearrange("p m k d -> p m (k d)"),
                                                ALU.add).then_inc(s.x_done, 1)
                    take(0, 0)
                    each(dve, body)


def attn3(nc, g, t, pool_job):
    EC = EG // P
    with ExitStack() as ctx:
        x3 = ctx.enter_context(nc.sbuf_tensor("x3", [P, NT, D], F32))
        x3_t = ctx.enter_context(nc.sbuf_tensor("x3_t", [P, N], F32))
        normalise(nc, g, "ln3", g.xn, x3, x3_t, "ln", t["a3_g"], t["a3_b"], pool_job=pool_job)
        with section(nc, "gau", "w_in", "xb_ready", "p_ready", "act_done", "qk_ready", "s_ready", "relu_done",
                     "a_ready", "o_ready", "g_ready", "f_ready", "x_step") as s:
            w = s.sb("w", [P, 2 * EG + D])
            bu = s.sb("bu", [P, EC])
            bz = s.sb("bz", [P, 1])
            bv = s.sb("bv", [1, EG])
            qk = s.sb("qk", [P, 4])
            wo = s.sb("wo", [P, EC, D])
            bo = s.sb("bo", [1, D])
            xb = s.sb("xb", [P, T])
            ut = s.sb("ut", [P, 2, EC, T])
            v = s.sb("v", [P, 2, QT, EG])
            zt = s.sb("zt", [P, T])
            q = s.sb("q", [P, 2, T])
            k = s.sb("k", [P, 2, T])
            rl = s.sb("rl", [P, QT, T])
            at = s.sb("at", [P, QT, T])
            gt = s.sb("gt", [P, EC, T])

            def each(eng, stage):
                stage(0, 1, False, True)
                with eng.Fori(0, BATCH // 2 - 1) as it:
                    for p in range(2):
                        stage(it * 2 + p, p, True, True)
                stage(BATCH - 2, 0, True, True)
                stage(BATCH - 1, 1, True, False)

            with nc.Block() as block:

                @block.sync
                def _(sp):
                    for dst, src in ((w, "a3_w"), (bu, "a3_bu"), (bz, "a3_bz"), (bv, "a3_bv"), (qk, "a3_qk"),
                                     (wo, "a3_wo"), (bo, "a3_bo")):
                        sp.dma_start(dst[:], t[src]).then_inc(s.w_in, 16)

                @block.gpsimd
                def _(pool):
                    def stage(b, p, now, ahead):
                        if ahead:
                            nb = b + 1 if now else b
                            pool.wait_ge(s.p_ready, nb)
                            nc.gpsimd.tensor_copy(xb[:], x3_t[:, bass.ds(nb * T, T)]).then_inc(s.xb_ready, 1)
                    each(pool, stage)

                @block.tensor
                def _(pe):
                    pe.wait_ge(s.w_in, 112)

                    def stage(b, p, now, ahead):
                        nb, np_ = (b + 1, 1 - p) if now else (b, 0)
                        if now:
                            pe.wait_ge(s.qk_ready, b + 1)
                            pe.wait_ge(s.relu_done, b)
                            for kt in range(QT):
                                ins = nc.tensor.matmul(g.ps[:, 3, kt * T:(kt + 1) * T], k[:, p, kt * P:(kt + 1) * P],
                                                       q[:, p, :], start=True, stop=True)
                            ins.then_inc(s.s_ready, 1)
                        if ahead:
                            pe.wait_ge(s.xb_ready, nb + 1)
                            pe.wait_ge(s.act_done, nb)
                            for c in range(EC):
                                nc.tensor.matmul(g.ps[:, 0, c * T:(c + 1) * T], w[:, c * P:(c + 1) * P], xb[:],
                                                 start=True, stop=True)
                            nc.tensor.matmul(g.ps[:, 1, 0:T], w[:, 2 * EG:2 * EG + D], xb[:], start=True, stop=True)
                            for kt in range(QT):
                                out = g.ps[:, 2, kt * EG:(kt + 1) * EG]
                                nc.tensor.matmul(out, xb[:, kt * P:(kt + 1) * P], w[:, EG:2 * EG], start=True,
                                                 stop=False)
                                ins = nc.tensor.matmul(out, g.ones_row[:], bv[:], start=False, stop=True)
                            ins.then_inc(s.p_ready, 1)
                        if now:
                            pe.wait_ge(s.a_ready, b + 1)
                            pe.wait_ge(s.g_ready, b)
                            for c in range(EC):
                                for kt in range(QT):
                                    ins = nc.tensor.matmul(g.ps[:, 4, c * T:(c + 1) * T],
                                                           v[:, p, kt, c * P:(c + 1) * P], at[:, kt, :],
                                                           start=(kt == 0), stop=(kt == QT - 1))
                            ins.then_inc(s.o_ready, 1)
                            pe.wait_ge(s.g_ready, b + 1)
                            pe.wait_ge(s.x_step, b * 2)
                            for qt in range(QT):
                                out = g.ps[:, 5, qt * D:(qt + 1) * D]
                                for c in range(EC):
                                    nc.tensor.matmul(out, gt[:, c, qt * P:(qt + 1) * P], wo[:, c, :], start=(c == 0),
                                                     stop=False)
                                ins = nc.tensor.matmul(out, g.ones_row[:], bo[:], start=False, stop=True)
                            ins.then_inc(s.f_ready, 1)
                    each(pe, stage)

                @block.scalar
                def _(act):
                    act.wait_ge(s.w_in, 112)
                    nc.scalar.preload_act_table(ACT.Silu)

                    def stage(b, p, now, ahead):
                        if ahead:
                            nb, np_ = (b + 1, 1 - p) if now else (b, 0)
                            act.wait_ge(s.p_ready, nb + 1)
                            act.wait_ge(s.qk_ready, nb)
                            if now:
                                act.wait_ge(s.g_ready, b)
                            nc.scalar.activation(zt[:], g.ps[:, 1, 0:T], ACT.Silu, bias=bz[:])
                            for c in range(EC):
                                nc.scalar.activation(ut[:, np_, c, :], g.ps[:, 0, c * T:(c + 1) * T], ACT.Silu,
                                                     bias=bu[:, c:c + 1])
                            nc.scalar.activation(v[:, np_].rearrange("p k e -> p (k e)"), g.ps[:, 2, :],
                                                 ACT.Silu).then_inc(s.act_done, 1)
                    each(act, stage)

                @block.vector
                def _(dve):
                    dve.wait_ge(s.w_in, 112)
                    vv = nc.vector

                    def stage(b, p, now, ahead):
                        nb, np_ = (b + 1, 1 - p) if now else (b, 0)
                        if now:
                            dve.wait_ge(s.s_ready, b + 1)
                            vv.tensor_scalar(rl[:].rearrange("p k t -> p (k t)"), g.ps[:, 3, :], 1.0 / T, 0.0,
                                             ALU.mult, ALU.max).then_inc(s.relu_done, 1)
                            dve.wait_ge(s.relu_done, b + 1)
                            dve.wait_ge(s.o_ready, b)
                            vv.tensor_tensor(at[:], rl[:], rl[:], ALU.mult).then_inc(s.a_ready, 1)
                        if ahead:
                            dve.wait_ge(s.act_done, nb + 1)
                            vv.tensor_scalar(q[:, np_, :], zt[:], qk[:, 0:1], qk[:, 1:2], ALU.mult, ALU.add)
                            vv.tensor_scalar(k[:, np_, :], zt[:], qk[:, 2:3], qk[:, 3:4], ALU.mult,
                                             ALU.add).then_inc(s.qk_ready, 1)
                        if now:
                            dve.wait_ge(s.o_ready, b + 1)
                            dve.wait_ge(s.f_ready, b)
                            vv.tensor_tensor(gt[:].rearrange("p c t -> p (c t)"), g.ps[:, 4, :],
                                             ut[:, p].rearrange("p c t -> p (c t)"), ALU.mult).then_inc(s.g_ready, 1)
                            dve.wait_ge(s.f_ready, b + 1)
                            xs = g.x[:, bass.ds(b * QT, QT), :]
                            vv.tensor_tensor(xs, xs, g.ps[:, 5, 0:QT * D].rearrange("p (k d) -> p k d", k=QT),
                                             ALU.add).then_inc(s.x_step, 1)
                            dve.wait_ge(s.x_step, b * 2 + 1)
                            vv.tensor_tensor(xs, xs, g.xn[:, bass.ds(b * QT, QT), :], ALU.add).then_inc(s.x_step, 1)
                    each(dve, stage)


def layer0(nc, g, t):
    with ExitStack() as l:
        u = l.enter_context(nc.sbuf_tensor("u", [P, DC, N], F32))
        gate = l.enter_context(nc.sbuf_tensor("gate", [P, DC, N], F32))
        n = (E0 - FIRST_MLP0) * CAP0
        disp = nc.dram_tensor("disp0", (n, D), F32, kind="Internal").ap()
        ybuf = nc.dram_tensor("ybuf0", (n, D), F32, kind="Internal").ap()
        with ExitStack() as c:
            xr = c.enter_context(nc.sbuf_tensor("xr", [P, NT, D], F32))
            r = Names()
            r.rows_i = c.enter_context(nc.sbuf_tensor("rows0", [P, 2, NT], I32))
            r.scat_i = c.enter_context(nc.sbuf_tensor("places0", [P, 2, NT], I32))
            r.w = c.enter_context(nc.sbuf_tensor("w0", [P, 2, NT], F32))
            r.near = c.enter_context(nc.sbuf_tensor("near0", [P, NT, FIRST_MLP0], F32))
            with nc.sbuf_tensor("xr_t", [P, N], F32) as xr_t:
                normalise(nc, g, "rms0", g.xn, xr, xr_t, "rms", w_row=t["f0_norm"])
                route(nc, g, t, "route0", xr, xr_t, "f0_router", E0, 2, CAP0, FIRST_MLP0, disp, r)
            mamba_in(nc, g, t, u, gate, lambda pool, done: scatter(nc, pool, done, xr, disp, r, 2))
            experts(nc, g, t, "mlp0", "f0_packed", E0 - FIRST_MLP0, CAP0, disp, ybuf, ACT.Gelu)
            combine(nc, g, t, "comb0", ybuf, 2, r, xr)
        delta = l.enter_context(nc.sbuf_tensor("delta", [P, DC, N], F32))
        bc3 = l.enter_context(nc.sbuf_tensor("bc3", [3 * 2 * DS, N], BF16))
        mamba_delta(nc, g, t, delta, bc3)
        mamba_scan(nc, g, t, u, gate, delta, bc3)


def store(nc, g, out):
    with section(nc, "store", "stored") as s, nc.Block() as block:

        @block.sync
        def _(sp):
            sp.dma_start(out.rearrange("(t p) d -> p t d", p=P), g.x[:]).then_inc(s.stored, 16)
            sp.wait_ge(s.stored, 16)


def program(nc, t, out, parts=None):
    with ExitStack() as ctx:
        def sb(name, shape, dt=F32):
            return ctx.enter_context(nc.sbuf_tensor(name, shape, dt))

        g = Names()
        g.ps = ctx.enter_context(nc.psum_tensor("banks", [P, 8, 512], F32))
        g.x = sb("x_tok", [P, NT, D])
        g.xn = sb("xn_tok", [P, NT, D])
        g.xn_t = sb("xn_t", [P, N])
        g.ident = sb("ident", [P, P])
        g.ident_b = sb("ident_b", [P, P], BF16)
        g.ones_b = sb("ones_b", [P, P], BF16)
        g.before = sb("before", [P, P], BF16)
        g.after_neg = sb("after_neg", [P, P], BF16)
        g.future_q = sb("future_q", [P, P], BF16)
        g.head_sel = sb("head_sel", [P, HEADS, P], BF16)
        g.ones_row = sb("ones_row", [1, P])
        g.zeros = sb("zeros", [P, 512])
        setup(nc, g, t)
        for layer, blocks in enumerate(((layer0,), (layer1,), (attn2, ffn2), (layer3,))):
            wanted = [f for f, kind in zip(blocks, "af") if parts is None or f"{layer}{kind}" in parts]
            if wanted:
                normalise(nc, g, f"norm{layer}", g.x, g.xn, g.xn_t, "ln")
            for f in wanted:
                f(nc, g, t)
        store(nc, g, out)


def layouts(i):
    import numpy as np

    def c(a):
        return np.ascontiguousarray(a)

    def cols(a):
        return c(np.asarray(a).reshape(-1, P).T)

    o = {"x": c(np.asarray(i["L0_attn_inputs"]).reshape(N, D))}
    w_x = np.asarray(i["L0_attn_W_x"])
    o["m_w_in"] = c(i["L0_attn_W_in"])
    o["m_taps"] = c(np.asarray(i["L0_attn_K_conv"])[:, 0, :].reshape(TAPS, DC, P).transpose(2, 1, 0))
    o["m_b_conv"] = cols(i["L0_attn_b_conv"])
    o["m_w_dt_in"] = c(np.pad(w_x[:, :DTR], ((0, 0), (0, P - DTR))))
    o["m_w_bc"] = c(np.concatenate([w_x[:, DTR:]] * 3, axis=1))
    o["m_w_dt"] = c(np.pad(np.asarray(i["L0_attn_W_dt"]), ((0, P - DTR), (0, 0))))
    o["m_b_dt"] = cols(i["L0_attn_b_dt"])
    o["m_a_log"] = c(np.asarray(i["L0_attn_A_log"]).reshape(DC, P, DS).transpose(1, 0, 2))
    o["m_d"] = cols(i["L0_attn_D"])
    o["m_w_out"] = c(np.asarray(i["L0_attn_W_out"]).reshape(DC, P, D).transpose(1, 0, 2))
    o["m_b_out"] = c(np.asarray(i["L0_attn_b_out"])[None, :])

    def pack(w1, b1, w2, b2):
        w1, b1, w2, b2 = (np.asarray(a) for a in (w1, b1, w2, b2))
        e, _, f = w1.shape
        return c(np.concatenate([
            w1, w2.reshape(e, f // P, P, D).transpose(0, 2, 1, 3).reshape(e, P, -1),
            b1.reshape(e, f // P, P).transpose(0, 2, 1), np.broadcast_to(b2[:, None, :], (e, P, D))], axis=2))

    o["f0_norm"] = c(np.asarray(i["L0_ffn_norm_weight"])[None, :])
    o["f0_router"] = c(np.asarray(i["L0_ffn_router_weight"]).T)
    o["f0_router_b"] = c(np.asarray(i["L0_ffn_router_bias"])[None, :])
    o["f0_const"] = c(np.asarray(i["L0_ffn_constant_vectors"])[None])
    o["f0_packed"] = pack(np.asarray(i["L0_ffn_fc1_weight"]).transpose(0, 2, 1), i["L0_ffn_fc1_bias"],
                          np.asarray(i["L0_ffn_fc2_weight"]).transpose(0, 2, 1), i["L0_ffn_fc2_bias"])
    w1, w2, w3, gate = (np.concatenate([np.asarray(i["L1_ffn_" + k]), np.asarray(i["L1_ffn_new_" + k])])
                        for k in ("w1", "w2", "w3", "gate_weight"))
    o["f1_gate"] = c(gate.T)
    o["f1_gate_b"] = c(np.concatenate([np.zeros(E1 - 1, np.float32), np.asarray(i["L1_ffn_gate_bias"])])[None, :])
    o["f1_w13"] = c(np.concatenate([w1.transpose(2, 0, 1), w3.transpose(2, 0, 1)], axis=2))
    w2 = np.pad(w2.transpose(0, 2, 1), ((0, 0), (0, len(H1_CUTS) * P - H1), (0, 0)))
    o["f1_w2"] = c(w2.reshape(E1, len(H1_CUTS), P, D).transpose(2, 0, 1, 3).reshape(P, E1, -1))
    by_d = np.arange(D).reshape(HEADS, HD).T.ravel()
    for m in "qk":
        o["a1_w" + m] = c(np.asarray(i["L1_attn_W" + m]).T[:, by_d])
        o["a1_b" + m] = c(np.asarray(i["L1_attn_b" + m])[by_d][:, None])

    def quarters(w):
        w = np.pad(np.asarray(w).reshape(HEADS // 4, 4, HD, D), ((0, 0), (0, 0), (0, P // 4 - HD), (0, 0)))
        return c(w.transpose(1, 2, 0, 3).reshape(P, HEADS // 4, D))

    o["a1_wv"], o["a1_wo"] = c(np.asarray(i["L1_attn_Wv"]).T), quarters(np.asarray(i["L1_attn_Wo"]).T)
    for m in "vo":
        o["a1_b" + m] = c(np.asarray(i["L1_attn_b" + m])[None, :])
    w_qkv, b_qkv = np.asarray(i["L2_attn_w_qkv"]), np.asarray(i["L2_attn_b_qkv"])
    o["a2_wq_t"], o["a2_wv_t"] = c(w_qkv[:, :D].T), c(w_qkv[:, 2 * D:].T)
    o["a2_wk"], o["a2_bk"] = c(w_qkv[:, D:2 * D][:, by_d]), c(b_qkv[D:2 * D][by_d][:, None])
    o["a2_bq"], o["a2_bv"] = c(b_qkv[:D][:, None]), c(b_qkv[2 * D:][:, None])
    o["a2_wo"], o["a2_bo"] = quarters(i["L2_attn_w_proj"]), c(np.asarray(i["L2_attn_b_proj"])[None, :])
    for m, order in (("q", by_d), ("v", np.arange(D))):
        a, b = np.asarray(i["L2_attn_a_" + m]), np.asarray(i["L2_attn_b_" + m])
        rank = a.shape[1]
        big_a = np.zeros((HEADS, rank, HEADS, HD), a.dtype)
        big_b = np.zeros((HEADS, rank, HEADS, HD), b.dtype)
        for h in range(HEADS):
            big_a[h, :, h, :] = a.T
            big_b[h, :, h, :] = b
        o["l" + m + "_a"] = c(big_a.reshape(2, P, D).transpose(1, 0, 2))
        o["l" + m + "_b"] = c(big_b.reshape(2, P, D)[:, :, order].transpose(1, 0, 2))
        o["l" + m + "_eye"] = c(np.eye(D, dtype=np.float32)[:, order])
    o["f2_g"], o["f2_b"] = cols(i["L2_ffn_ln_g"]), cols(i["L2_ffn_ln_b"])
    o["f2_aw"], o["f2_ab"] = c(i["L2_ffn_attn_w"]), cols(i["L2_ffn_attn_b"])
    o["f2_nw"], o["f2_nb"] = c(i["L2_ffn_next_w"]), c(np.asarray(i["L2_ffn_next_b"])[None, :])
    packed = pack(i["L2_ffn_w1"], i["L2_ffn_b1"], i["L2_ffn_w2"], i["L2_ffn_b2"])
    o["f2_packed"] = c(np.concatenate([packed[:, :, :-P], np.asarray(i["L2_ffn_b2"])[:, :, None]], axis=2))
    w_in, b_in = np.asarray(i["L3_attn_W_in"]), np.asarray(i["L3_attn_b_in"])
    o["a3_g"], o["a3_b"] = cols(i["L3_attn_ln_g"]), cols(i["L3_attn_ln_b"])
    o["a3_w"] = c(w_in)
    o["a3_bu"], o["a3_bz"] = cols(b_in[:EG]), cols(b_in[2 * EG:])
    o["a3_bv"] = c(b_in[None, EG:2 * EG])
    o["a3_qk"] = c(np.stack([np.asarray(i["L3_attn_" + n]) for n in ("gamma_q", "beta_q", "gamma_k", "beta_k")], axis=1))
    o["a3_wo"] = c(np.asarray(i["L3_attn_W_out"]).reshape(EG // P, P, D).transpose(1, 0, 2))
    o["a3_bo"] = c(np.asarray(i["L3_attn_b_out"])[None, :])
    o["f3_gate"] = c(i["L3_ffn_wg"])
    o["f3_packed"] = pack(i["L3_ffn_w1"], i["L3_ffn_b1"], i["L3_ffn_w2"], i["L3_ffn_b2"])
    return o


def kernel(**inputs):
    import numpy as np
    import concourse.bacc as bacc
    from concourse.bass_utils import run_bass_kernel_spmd

    nc = bacc.Bacc("TRN2", target_bir_lowering=False, num_devices=1)
    arrays = layouts(inputs)
    t = {name: nc.dram_tensor(name, a.shape, mybir.dt.from_np(a.dtype), kind="ExternalInput").ap()
         for name, a in arrays.items()}
    out = nc.dram_tensor("out", (N, D), F32, kind="ExternalOutput").ap()
    program(nc, t, out)
    res = run_bass_kernel_spmd(nc, [arrays], core_ids=[0])
    return np.asarray(res.results[0]["out"]).reshape(BATCH, T, D)
```
